# Optimizing a Trainium2 kernel written in Bass

```python
import numpy as np
import jax
import jax.numpy as jnp

def _softmax(x, axis=-1):
    return jax.nn.softmax(x, axis=axis)

def _gelu(x):
    return jax.nn.gelu(x, approximate=True)

def _silu(x):
    return jax.nn.silu(x)

def _sigmoid(x):
    return jax.nn.sigmoid(x)

def _layernorm(x, axis=-1, eps=1e-05):
    m = jnp.mean(x, axis=axis, keepdims=True)
    v = jnp.var(x, axis=axis, keepdims=True)
    return (x - m) / jnp.sqrt(v + eps)

def _scatter_add(tgt, idx, src, axis=0):
    return tgt.at[idx].add(src)

def _segment_sum(src, seg, n):
    return jax.ops.segment_sum(src, seg, n)
kernel_name = 'mk_gnn_preln_d4_gnn_r32_a0cbeb'

def setup_inputs(seed: int=0):
    np.random.seed(seed)
    _w = jnp.asarray

    def _rec_inputs():
        import jax
        import jax.numpy as jnp
        _gk = jax.random.key(seed)
        x = -0.000202 + 1 * jax.random.normal(jax.random.fold_in(_gk, 1), (3125, 128), jnp.float32)
        _s = jax.random.randint(jax.random.fold_in(_gk, 2), (50000,), 0, 3125, jnp.int32)
        _d = jax.random.randint(jax.random.fold_in(_gk, 3), (50000,), 0, 3125, jnp.int32)
        _loop = jnp.arange(3125, dtype=jnp.int32)
        src = jnp.concatenate([_s, _d, _loop])
        dst = jnp.concatenate([_d, _s, _loop])
        _o = jnp.argsort(dst, stable=True)
        src = src[_o]
        dst = dst[_o]
        edge_attr_32 = 0.000254156 + 0.999948 * jax.random.normal(jax.random.fold_in(_gk, 12), (103125, 32), jnp.float32)
        return (x, src, dst, edge_attr_32)
    x, src, dst, edge_attr_32 = _rec_inputs()

    def _L0_gnn_setup():
        import jax, jax.numpy as jnp
        import numpy as np
        N, E = (50000, 12500)
        HID, EDIM, H, FFN_MULT = (128, 32, 2, 2)
        C = HID

        def _layernorm(x, g, b, eps=1e-05):
            mu = jnp.mean(x, axis=-1, keepdims=True)
            var = jnp.mean(jnp.square(x - mu), axis=-1, keepdims=True)
            return (x - mu) * jax.lax.rsqrt(var + eps) * g + b
        key = jax.random.key(seed)
        ks = jax.random.split(key, 16)
        s = 0.05
        inp = {'x': jax.random.normal(ks[0], (N, HID), jnp.float32), 'edge_index': jax.random.randint(ks[1], (2, E), 0, N, jnp.int64), 'edge_attr': jax.random.normal(ks[2], (E, EDIM), jnp.float32), 'Wq': jax.random.normal(ks[3], (H * C, HID), jnp.float32) * s, 'bq': jnp.zeros((H * C,), jnp.float32), 'Wk': jax.random.normal(ks[4], (H * C, HID), jnp.float32) * s, 'bk': jnp.zeros((H * C,), jnp.float32), 'Wv': jax.random.normal(ks[5], (H * C, HID), jnp.float32) * s, 'bv': jnp.zeros((H * C,), jnp.float32), 'We': jax.random.normal(ks[6], (H * C, EDIM), jnp.float32) * s, 'Wskip': jax.random.normal(ks[7], (HID, HID), jnp.float32) * s, 'bskip': jnp.zeros((HID,), jnp.float32), 'ln1_g': jnp.ones((HID,), jnp.float32), 'ln1_b': jnp.zeros((HID,), jnp.float32), 'W1': jax.random.normal(ks[8], (HID * FFN_MULT, HID), jnp.float32) * s, 'b1': jnp.zeros((HID * FFN_MULT,), jnp.float32), 'W2': jax.random.normal(ks[9], (HID, HID * FFN_MULT), jnp.float32) * s, 'b2': jnp.zeros((HID,), jnp.float32), 'ln2_g': jnp.ones((HID,), jnp.float32), 'ln2_b': jnp.zeros((HID,), jnp.float32)}
        return inp
    _L0_gnn_all = _L0_gnn_setup()
    _L0_gnn_in = {k: v for k, v in _L0_gnn_all.items() if k in ('Wq', 'bq', 'Wk', 'bk', 'Wv', 'bv', 'We', 'Wskip', 'bskip', 'ln1_g', 'ln1_b', 'W1', 'b1', 'W2', 'b2', 'ln2_g', 'ln2_b')}
    del _L0_gnn_all

    def _L1_gnn_setup():
        import jax, jax.numpy as jnp
        import numpy as np
        N = 3125
        E = 50000
        NUM_IN = 128
        CONV = 64
        HEADS = 4
        NUM_OUT = 128
        OUT_C = NUM_OUT // HEADS
        NEG_SLOPE = 0.2

        def gat_conv(x, src, dst, W, a_src, a_dst, b):
            n = x.shape[0]
            H, C = a_src.shape
            xp = (x @ W).reshape(n, H, C)
            al_src = (xp * a_src).sum(-1)
            al_dst = (xp * a_dst).sum(-1)
            loops = jnp.arange(n)
            s = jnp.concatenate([src, loops])
            d = jnp.concatenate([dst, loops])
            e = jax.nn.leaky_relu(al_src[s] + al_dst[d], NEG_SLOPE)
            m = jax.ops.segment_max(e, d, num_segments=n)
            p = jnp.exp(e - m[d])
            denom = jax.ops.segment_sum(p, d, num_segments=n)
            alpha = p / denom[d]
            out = jax.ops.segment_sum(alpha[:, :, None] * xp[s], d, num_segments=n)
            return out.reshape(n, H * C) + b

        def _glorot(key, shape):
            fan = shape[0] + shape[-1]
            return jax.random.normal(key, shape, dtype=jnp.float32) * np.sqrt(2.0 / fan)
        key = jax.random.key(seed)
        ks = jax.random.split(key, 16)
        x = jax.random.normal(ks[0], (N, NUM_IN), dtype=jnp.float32)
        edge_index = jax.random.randint(ks[1], (2, E), 0, N, dtype=jnp.int64)
        HID = HEADS * CONV
        inp = {'x': x, 'edge_index': edge_index, 'W0': _glorot(ks[2], (NUM_IN, HID)), 'as0': _glorot(ks[3], (HEADS, CONV)), 'ad0': _glorot(ks[4], (HEADS, CONV)), 'b0': jnp.zeros((HID,), dtype=jnp.float32), 'W1': _glorot(ks[5], (HID, HID)), 'as1': _glorot(ks[6], (HEADS, CONV)), 'ad1': _glorot(ks[7], (HEADS, CONV)), 'b1': jnp.zeros((HID,), dtype=jnp.float32), 'W2': _glorot(ks[8], (HID, NUM_OUT)), 'as2': _glorot(ks[9], (HEADS, OUT_C)), 'ad2': _glorot(ks[10], (HEADS, OUT_C)), 'b2': jnp.zeros((NUM_OUT,), dtype=jnp.float32)}
        return inp
    _L1_gnn_all = _L1_gnn_setup()
    _L1_gnn_in = {k: v for k, v in _L1_gnn_all.items() if k in ('W0', 'as0', 'ad0', 'b0', 'W1', 'as1', 'ad1', 'b1', 'W2', 'as2', 'ad2', 'b2')}
    del _L1_gnn_all

    def _L2_gnn_setup():
        import jax, jax.numpy as jnp
        import numpy as np
        N = 50000
        E = 25000
        F = 128
        H = 4
        D = 32
        G = 8
        K = 3
        NEG_SLOPE = 0.2

        def _make_grid(grid_size, k):
            h = 2.0 / grid_size
            return jnp.arange(-k, grid_size + k + 1, dtype=jnp.float32) * h - 1.0

        def _bsplines(x, grid, k):
            xg = x[..., None]
            b = ((xg >= grid[:-1]) & (xg < grid[1:])).astype(x.dtype)
            for j in range(1, k + 1):
                left = (xg - grid[:-(j + 1)]) / (grid[j:-1] - grid[:-(j + 1)]) * b[..., :-1]
                right = (grid[j + 1:] - xg) / (grid[j + 1:] - grid[1:-j]) * b[..., 1:]
                b = left + right
            return b

        def _kan_linear(x, base_w, spline_w, grid, k):
            base = jax.nn.silu(x) @ base_w.T
            bs = _bsplines(x, grid, k)
            spline = jnp.einsum('nfc,ofc->no', bs, spline_w)
            return base + spline
        key = jax.random.key(seed)
        ks = jax.random.split(key, 8)
        O = H * D
        C = G + K
        x = jax.random.normal(ks[0], (N, F), dtype=jnp.float32)
        edge_index = jax.random.randint(ks[1], (2, E), 0, N, dtype=jnp.int64)
        scale = 1.0 / np.sqrt(F)
        base_w_src = jax.random.normal(ks[2], (O, F), dtype=jnp.float32) * scale
        spline_w_src = jax.random.normal(ks[3], (O, F, C), dtype=jnp.float32) * (0.1 * scale)
        base_w_dst = jax.random.normal(ks[4], (O, F), dtype=jnp.float32) * scale
        spline_w_dst = jax.random.normal(ks[5], (O, F, C), dtype=jnp.float32) * (0.1 * scale)
        double_attn = jax.random.normal(ks[6], (1, H, D), dtype=jnp.float32) * (1.0 / np.sqrt(D))
        bias = jnp.zeros((O,), dtype=jnp.float32)
        prelu_a = jnp.asarray(0.25, dtype=jnp.float32)
        return {'x': x, 'edge_index': edge_index, 'base_w_src': base_w_src, 'spline_w_src': spline_w_src, 'base_w_dst': base_w_dst, 'spline_w_dst': spline_w_dst, 'double_attn': double_attn, 'bias': bias, 'prelu_a': prelu_a}
    _L2_gnn_all = _L2_gnn_setup()
    _L2_gnn_in = {k: v for k, v in _L2_gnn_all.items() if k in ('base_w_src', 'spline_w_src', 'base_w_dst', 'spline_w_dst', 'double_attn', 'bias', 'prelu_a')}
    del _L2_gnn_all

    def _L3_gnn_setup():
        import jax, jax.numpy as jnp
        import numpy as np
        N_NODES = 50000
        N_EDGES = 50000
        IN_DIM = 128
        HID = 32
        HEADS = 4
        NEG_SLOPE = 0.2

        def _gat_forward(h, src, dst, Wq, Wk, Wv):
            n = h.shape[0]
            q = jnp.einsum('ni,hio->hno', h, Wq)
            k = jnp.einsum('ni,hio->hno', h, Wk)
            v = jnp.einsum('ni,hio->hno', h, Wv)
            e = jax.nn.leaky_relu(jnp.einsum('hed,hed->he', q[:, src], k[:, dst]), negative_slope=NEG_SLOPE)
            seg_max = jax.vmap(lambda x: jax.ops.segment_max(x, dst, num_segments=n))(e)
            seg_max = jax.lax.stop_gradient(jnp.where(jnp.isfinite(seg_max), seg_max, 0.0))
            ex = jnp.exp(e - seg_max[:, dst])
            denom = jax.vmap(lambda x: jax.ops.segment_sum(x, dst, num_segments=n))(ex)
            alpha = ex / jnp.maximum(denom, 1e-09)[:, dst]
            msg = alpha[..., None] * v[:, src]
            out = jax.vmap(lambda m: jax.ops.segment_sum(m, dst, num_segments=n))(msg)
            return out.transpose(1, 0, 2).reshape(n, HEADS * HID)
        key = jax.random.key(seed)
        ks = jax.random.split(key, 6)
        h = jax.random.normal(ks[0], (N_NODES, IN_DIM), dtype=jnp.float32)
        src = jax.random.randint(ks[1], (N_EDGES,), 0, N_NODES, dtype=jnp.int32)
        dst = jax.random.randint(ks[2], (N_EDGES,), 0, N_NODES, dtype=jnp.int32)
        s = 1.0 / np.sqrt(IN_DIM)
        Wq = jax.random.normal(ks[3], (HEADS, IN_DIM, HID), dtype=jnp.float32) * s
        Wk = jax.random.normal(ks[4], (HEADS, IN_DIM, HID), dtype=jnp.float32) * s
        Wv = jax.random.normal(ks[5], (HEADS, IN_DIM, HID), dtype=jnp.float32) * s
        return {'h': h, 'src': src, 'dst': dst, 'Wq': Wq, 'Wk': Wk, 'Wv': Wv}
    _L3_gnn_all = _L3_gnn_setup()
    _L3_gnn_in = {k: v for k, v in _L3_gnn_all.items() if k in ('Wq', 'Wk', 'Wv')}
    del _L3_gnn_all
    return {'x': x, 'src': src, 'dst': dst, 'edge_attr_32': edge_attr_32, 'L0_gnn_Wq': _L0_gnn_in['Wq'], 'L0_gnn_bq': _L0_gnn_in['bq'], 'L0_gnn_Wk': _L0_gnn_in['Wk'], 'L0_gnn_bk': _L0_gnn_in['bk'], 'L0_gnn_Wv': _L0_gnn_in['Wv'], 'L0_gnn_bv': _L0_gnn_in['bv'], 'L0_gnn_We': _L0_gnn_in['We'], 'L0_gnn_Wskip': _L0_gnn_in['Wskip'], 'L0_gnn_bskip': _L0_gnn_in['bskip'], 'L0_gnn_ln1_g': _L0_gnn_in['ln1_g'], 'L0_gnn_ln1_b': _L0_gnn_in['ln1_b'], 'L0_gnn_W1': _L0_gnn_in['W1'], 'L0_gnn_b1': _L0_gnn_in['b1'], 'L0_gnn_W2': _L0_gnn_in['W2'], 'L0_gnn_b2': _L0_gnn_in['b2'], 'L0_gnn_ln2_g': _L0_gnn_in['ln2_g'], 'L0_gnn_ln2_b': _L0_gnn_in['ln2_b'], 'L1_gnn_W0': _L1_gnn_in['W0'], 'L1_gnn_as0': _L1_gnn_in['as0'], 'L1_gnn_ad0': _L1_gnn_in['ad0'], 'L1_gnn_b0': _L1_gnn_in['b0'], 'L1_gnn_W1': _L1_gnn_in['W1'], 'L1_gnn_as1': _L1_gnn_in['as1'], 'L1_gnn_ad1': _L1_gnn_in['ad1'], 'L1_gnn_b1': _L1_gnn_in['b1'], 'L1_gnn_W2': _L1_gnn_in['W2'], 'L1_gnn_as2': _L1_gnn_in['as2'], 'L1_gnn_ad2': _L1_gnn_in['ad2'], 'L1_gnn_b2': _L1_gnn_in['b2'], 'L2_gnn_base_w_src': _L2_gnn_in['base_w_src'], 'L2_gnn_spline_w_src': _L2_gnn_in['spline_w_src'], 'L2_gnn_base_w_dst': _L2_gnn_in['base_w_dst'], 'L2_gnn_spline_w_dst': _L2_gnn_in['spline_w_dst'], 'L2_gnn_double_attn': _L2_gnn_in['double_attn'], 'L2_gnn_bias': _L2_gnn_in['bias'], 'L2_gnn_prelu_a': _L2_gnn_in['prelu_a'], 'L3_gnn_Wq': _L3_gnn_in['Wq'], 'L3_gnn_Wk': _L3_gnn_in['Wk'], 'L3_gnn_Wv': _L3_gnn_in['Wv']}

def reference(x, src, dst, edge_attr_32, L0_gnn_Wq, L0_gnn_bq, L0_gnn_Wk, L0_gnn_bk, L0_gnn_Wv, L0_gnn_bv, L0_gnn_We, L0_gnn_Wskip, L0_gnn_bskip, L0_gnn_ln1_g, L0_gnn_ln1_b, L0_gnn_W1, L0_gnn_b1, L0_gnn_W2, L0_gnn_b2, L0_gnn_ln2_g, L0_gnn_ln2_b, L1_gnn_W0, L1_gnn_as0, L1_gnn_ad0, L1_gnn_b0, L1_gnn_W1, L1_gnn_as1, L1_gnn_ad1, L1_gnn_b1, L1_gnn_W2, L1_gnn_as2, L1_gnn_ad2, L1_gnn_b2, L2_gnn_base_w_src, L2_gnn_spline_w_src, L2_gnn_base_w_dst, L2_gnn_spline_w_dst, L2_gnn_double_attn, L2_gnn_bias, L2_gnn_prelu_a, L3_gnn_Wq, L3_gnn_Wk, L3_gnn_Wv):
    import jax
    import jax.numpy as jnp

    def _L0_gnn_ref(x, edge_index, edge_attr, Wq, bq, Wk, bk, Wv, bv, We, Wskip, bskip, ln1_g, ln1_b, W1, b1, W2, b2, ln2_g, ln2_b):
        import jax, jax.numpy as jnp
        import numpy as np
        N, E = (50000, 12500)
        HID, EDIM, H, FFN_MULT = (128, 32, 2, 2)
        C = HID

        def _layernorm(x, g, b, eps=1e-05):
            mu = jnp.mean(x, axis=-1, keepdims=True)
            var = jnp.mean(jnp.square(x - mu), axis=-1, keepdims=True)
            return (x - mu) * jax.lax.rsqrt(var + eps) * g + b
        n = x.shape[0]
        src, dst = (edge_index[0], edge_index[1])
        q = (x @ Wq.T + bq).reshape(n, H, C)
        k = (x @ Wk.T + bk).reshape(n, H, C)
        v = (x @ Wv.T + bv).reshape(n, H, C)
        e = (edge_attr @ We.T).reshape(-1, H, C)
        k_j = k[src] + e
        alpha = jnp.sum(q[dst] * k_j, axis=-1) / jnp.sqrt(jnp.float32(C))
        amax = jax.ops.segment_max(alpha, dst, num_segments=n)
        amax = jnp.where(jnp.isfinite(amax), amax, 0.0)
        ex = jnp.exp(alpha - amax[dst])
        denom = jax.ops.segment_sum(ex, dst, num_segments=n)
        w = ex / (denom[dst] + 1e-16)
        msg = (v[src] + e) * w[:, :, None]
        agg = jax.ops.segment_sum(msg, dst, num_segments=n)
        out = jnp.mean(agg, axis=1)
        attn_out = out + x @ Wskip.T + bskip
        h = _layernorm(x + attn_out, ln1_g, ln1_b)
        f = jax.nn.leaky_relu(h @ W1.T + b1, negative_slope=0.01) @ W2.T + b2
        return _layernorm(h + f, ln2_g, ln2_b)

    def _L1_gnn_ref(x, edge_index, W0, as0, ad0, b0, W1, as1, ad1, b1, W2, as2, ad2, b2):
        import jax, jax.numpy as jnp
        import numpy as np
        N = 3125
        E = 50000
        NUM_IN = 128
        CONV = 64
        HEADS = 4
        NUM_OUT = 128
        OUT_C = NUM_OUT // HEADS
        NEG_SLOPE = 0.2

        def gat_conv(x, src, dst, W, a_src, a_dst, b):
            n = x.shape[0]
            H, C = a_src.shape
            xp = (x @ W).reshape(n, H, C)
            al_src = (xp * a_src).sum(-1)
            al_dst = (xp * a_dst).sum(-1)
            loops = jnp.arange(n)
            s = jnp.concatenate([src, loops])
            d = jnp.concatenate([dst, loops])
            e = jax.nn.leaky_relu(al_src[s] + al_dst[d], NEG_SLOPE)
            m = jax.ops.segment_max(e, d, num_segments=n)
            p = jnp.exp(e - m[d])
            denom = jax.ops.segment_sum(p, d, num_segments=n)
            alpha = p / denom[d]
            out = jax.ops.segment_sum(alpha[:, :, None] * xp[s], d, num_segments=n)
            return out.reshape(n, H * C) + b

        def _glorot(key, shape):
            fan = shape[0] + shape[-1]
            return jax.random.normal(key, shape, dtype=jnp.float32) * np.sqrt(2.0 / fan)
        src, dst = (edge_index[0], edge_index[1])
        h = jax.nn.relu(gat_conv(x, src, dst, W0, as0, ad0, b0))
        h = jax.nn.relu(gat_conv(h, src, dst, W1, as1, ad1, b1))
        return gat_conv(h, src, dst, W2, as2, ad2, b2)

    def _L2_gnn_ref(x, edge_index, base_w_src, spline_w_src, base_w_dst, spline_w_dst, double_attn, bias, prelu_a):
        import jax, jax.numpy as jnp
        import numpy as np
        N = 50000
        E = 25000
        F = 128
        H = 4
        D = 32
        G = 8
        K = 3
        NEG_SLOPE = 0.2

        def _make_grid(grid_size, k):
            h = 2.0 / grid_size
            return jnp.arange(-k, grid_size + k + 1, dtype=jnp.float32) * h - 1.0

        def _bsplines(x, grid, k):
            xg = x[..., None]
            b = ((xg >= grid[:-1]) & (xg < grid[1:])).astype(x.dtype)
            for j in range(1, k + 1):
                left = (xg - grid[:-(j + 1)]) / (grid[j:-1] - grid[:-(j + 1)]) * b[..., :-1]
                right = (grid[j + 1:] - xg) / (grid[j + 1:] - grid[1:-j]) * b[..., 1:]
                b = left + right
            return b

        def _kan_linear(x, base_w, spline_w, grid, k):
            base = jax.nn.silu(x) @ base_w.T
            bs = _bsplines(x, grid, k)
            spline = jnp.einsum('nfc,ofc->no', bs, spline_w)
            return base + spline
        grid = _make_grid(G, K)
        src = edge_index[0]
        dst = edge_index[1]
        num_nodes = x.shape[0]
        sp = _kan_linear(x, base_w_src, spline_w_src, grid, K).reshape(num_nodes, H, D)
        dp = _kan_linear(x, base_w_dst, spline_w_dst, grid, K).reshape(num_nodes, H, D)
        e = jax.nn.leaky_relu(sp[src] + dp[dst], NEG_SLOPE)
        attn = jnp.sum(double_attn * e, axis=-1)
        exp_attn = jnp.exp(attn - jnp.max(attn))
        denom = jax.ops.segment_sum(exp_attn, dst, num_segments=num_nodes)
        alpha = exp_attn / (denom[dst] + 1e-16)
        msg = sp[src] * alpha[..., None]
        out = jax.ops.segment_sum(msg, dst, num_segments=num_nodes)
        out = out + x.reshape(num_nodes, H, D)
        out = out.reshape(num_nodes, H * D) + bias
        return jnp.where(out >= 0, out, prelu_a * out)

    def _L3_gnn_ref(h, src, dst, Wq, Wk, Wv):
        import jax, jax.numpy as jnp
        import numpy as np
        N_NODES = 50000
        N_EDGES = 50000
        IN_DIM = 128
        HID = 32
        HEADS = 4
        NEG_SLOPE = 0.2

        def _gat_forward(h, src, dst, Wq, Wk, Wv):
            n = h.shape[0]
            q = jnp.einsum('ni,hio->hno', h, Wq)
            k = jnp.einsum('ni,hio->hno', h, Wk)
            v = jnp.einsum('ni,hio->hno', h, Wv)
            e = jax.nn.leaky_relu(jnp.einsum('hed,hed->he', q[:, src], k[:, dst]), negative_slope=NEG_SLOPE)
            seg_max = jax.vmap(lambda x: jax.ops.segment_max(x, dst, num_segments=n))(e)
            seg_max = jax.lax.stop_gradient(jnp.where(jnp.isfinite(seg_max), seg_max, 0.0))
            ex = jnp.exp(e - seg_max[:, dst])
            denom = jax.vmap(lambda x: jax.ops.segment_sum(x, dst, num_segments=n))(ex)
            alpha = ex / jnp.maximum(denom, 1e-09)[:, dst]
            msg = alpha[..., None] * v[:, src]
            out = jax.vmap(lambda m: jax.ops.segment_sum(m, dst, num_segments=n))(msg)
            return out.transpose(1, 0, 2).reshape(n, HEADS * HID)
        return _gat_forward(h, src, dst, Wq, Wk, Wv)
    edge_index = jnp.stack([src, dst])
    h = jnp.maximum(_layernorm(x, axis=-1), 0.0)
    x = x + _L0_gnn_ref(h, edge_index, edge_attr_32, L0_gnn_Wq, L0_gnn_bq, L0_gnn_Wk, L0_gnn_bk, L0_gnn_Wv, L0_gnn_bv, L0_gnn_We, L0_gnn_Wskip, L0_gnn_bskip, L0_gnn_ln1_g, L0_gnn_ln1_b, L0_gnn_W1, L0_gnn_b1, L0_gnn_W2, L0_gnn_b2, L0_gnn_ln2_g, L0_gnn_ln2_b)
    h = jnp.maximum(_layernorm(x, axis=-1), 0.0)
    x = x + _L1_gnn_ref(h, edge_index, L1_gnn_W0, L1_gnn_as0, L1_gnn_ad0, L1_gnn_b0, L1_gnn_W1, L1_gnn_as1, L1_gnn_ad1, L1_gnn_b1, L1_gnn_W2, L1_gnn_as2, L1_gnn_ad2, L1_gnn_b2)
    h = jnp.maximum(_layernorm(x, axis=-1), 0.0)
    x = x + _L2_gnn_ref(h, edge_index, L2_gnn_base_w_src, L2_gnn_spline_w_src, L2_gnn_base_w_dst, L2_gnn_spline_w_dst, L2_gnn_double_attn, L2_gnn_bias, L2_gnn_prelu_a)
    h = jnp.maximum(_layernorm(x, axis=-1), 0.0)
    x = x + _L3_gnn_ref(h, src, dst, L3_gnn_Wq, L3_gnn_Wk, L3_gnn_Wv)
    return x

_drawn_inputs = setup_inputs


def setup_inputs(seed=0):
    import zlib

    import numpy as np

    out = dict(_drawn_inputs(seed))
    spreads = {'L0_gnn_bq': (0.0, 0.8),
     'L0_gnn_bk': (0.0, 2.0),
     'L0_gnn_bv': (0.0, 0.1),
     'L0_gnn_bskip': (0.0, 0.1),
     'L0_gnn_ln1_g': (1.0, 0.2),
     'L0_gnn_ln1_b': (0.0, 0.1),
     'L0_gnn_b1': (0.0, 0.277),
     'L0_gnn_b2': (0.0, 0.1),
     'L0_gnn_ln2_g': (1.0, 0.2),
     'L0_gnn_ln2_b': (0.0, 0.1),
     'L1_gnn_b0': (0.0, 0.311),
     'L1_gnn_b1': (0.0, 0.1),
     'L1_gnn_b2': (0.0, 0.1),
     'L2_gnn_bias': (0.0, 0.1)}
    factors = {'L0_gnn_Wq': 7.113,
     'L0_gnn_Wk': 8.0,
     'L1_gnn_as0': 5.43,
     'L1_gnn_ad0': 39.816,
     'L1_gnn_as1': 22.023,
     'L1_gnn_ad1': 64.0,
     'L1_gnn_as2': 60.293,
     'L1_gnn_ad2': 64.0,
     'L2_gnn_spline_w_src': 2.834,
     'L2_gnn_base_w_dst': 33.602,
     'L2_gnn_spline_w_dst': 64.0}
    for name, (base, spread) in spreads.items():
        noise = np.random.default_rng([zlib.crc32(name.encode()), seed]).standard_normal(out[name].shape)
        drawn = base * np.exp(spread * noise) if base else spread * noise
        out[name] = jnp.asarray(drawn.astype(out[name].dtype))
    for name, factor in factors.items():
        out[name] = (out[name] * factor).astype(out[name].dtype)
    return out
```

```python
from contextlib import ExitStack

import numpy as np
import concourse.bass as bass
from concourse import mybir

F32 = mybir.dt.float32
I32 = mybir.dt.int32
ALU = mybir.AluOpType
ACT = mybir.ActivationFunctionType
X = mybir.AxisListType.X

P = 128
N = 3125
E = 103125
K = 8
CHUNKS = -(-E // K)
SLOTS = K + 1
EROWS = -(-E // P)
NB = -(-N // P)
NP_ = NB * P
RT = -(-(CHUNKS + N - 1) // P)
ROWS = RT * P
NO_NODE = 8191
G = 5
NG = NB // G
NEG = -1e30
LOW = -1e38
NEG_SLOPE = 0.2
ROW_IX = K + 2
U = 3
assert RT % 2 == 0 and NB % G == 0 and RT % U == 0


class Ctx:

    def __init__(self, nc):
        self.nc = nc
        self.keep = ExitStack()
        self.gather_sems = {n: self.keep.enter_context(nc.semaphore(n)) for n in
                            ["dsts_in", "marked", "got0", "got1"] + [f"gathered{b}" for b in range(U)]}

    def sb(self, name, shape, dt=F32, stack=None):
        return (stack or self.keep).enter_context(self.nc.sbuf_tensor(name, shape, dt))

    def dram(self, name, shape, dt=F32):
        return self.nc.dram_tensor(name, shape, dt, kind="Internal").ap()


class Phase:

    def __init__(self, c, name):
        self.c, self.nc, self.name = c, c.nc, name
        self.stack = ExitStack()
        self.sems = {}

    def sem(self, name):
        if name in self.c.gather_sems:
            self.sems[name] = self.c.gather_sems[name]
        if name not in self.sems:
            self.sems[name] = self.stack.enter_context(self.nc.semaphore(f"{self.name}_{name}"))
        return self.sems[name]

    def sb(self, name, shape, dt=F32):
        return self.stack.enter_context(self.nc.sbuf_tensor(f"{self.name}_{name}", shape, dt))

    def ps(self, name, shape, dt=F32):
        return self.stack.enter_context(self.nc.psum_tensor(f"{self.name}_{name}", shape, dt))

    def close(self):
        used = [s for n, s in self.sems.items() if n in self.c.gather_sems]
        if used:
            self.nc.gpsimd.dma_reset(range(min(x.num for x in used), max(x.num for x in used) + 1))
        for sem in self.sems.values():
            self.nc.gpsimd.sem_clear(sem)
        self.nc.all_engine_barrier()
        self.stack.close()


class Chain:

    def __init__(self, eng, sem):
        self.eng, self.sem, self.steps, self.k, self.base, self.first = eng, sem, 0, 0, 0, True

    def begin(self, i):
        if isinstance(i, int):
            self.base, self.first = 0, True
        else:
            if self.first:
                self.steps = self.k
            self.base, self.first = i * self.steps, False
        self.k = 0

    def link(self, ins):
        self.k += 1
        ins.then_inc(self.sem, 1)
        self.eng.wait_ge(self.sem, self.base + self.k)


def loop(eng, n, body):
    body(0)
    if n > 1:
        with eng.Fori(1, n) as i:
            body(i)


def reuse(eng, sem, i, per_step=1):
    if not isinstance(i, int):
        eng.wait_ge(sem, i * per_step)


def bcast(ap, shape, axis):
    return ap.unsqueeze(axis).to_broadcast(shape)


def prepare(c, T, x_in, chunk_ix, dst_rows):
    nc = c.nc
    ph = Phase(c, "prep")
    s = ph.sem
    i_col = ph.sb("i_col", [P, NB], I32)
    i_256 = ph.sb("i_256", [P, 2 * P], I32)
    i_row = ph.sb("i_row", [RT, P], I32)
    nid = ph.sb("nid", [P, NB])
    rowid = ph.sb("rowid", [RT, P])
    heads_i = ph.sb("heads_i", [P, EROWS], I32)
    heads = ph.sb("heads", [P, EROWS])
    junk = ph.sb("junk", [P, EROWS])
    before = ph.sb("before", [P, NB])
    tile_f = ph.sb("tile_f", [P, NB])
    tile_i = ph.sb("tile_i", [P, NB], I32)
    dsts = ph.sb("dsts", [P, NB, P], I32)
    less = ph.sb("less", [P, NB, P])
    inside = ph.sb("inside", [P, NB])
    start = ph.sb("start", [P, NB])
    startT = ph.sb("startT", [NB, P])
    nextT = ph.sb("nextT", [NB, P])
    fullE = ph.sb("fullE", [1, P])
    zeros = ph.sb("zeros", [P, P])
    qi = ph.sb("qi", [NB, 2, P], I32)
    q = ph.sb("q", [NB, 2, P])
    rc = ph.sb("rc", [NB, P])
    onesT = ph.sb("onesT", [RT, P])
    rp = ph.sb("rp", [NB, P])
    last_rp = ph.sb("last_rp", [NB, 1])
    upper = ph.sb("upper", [NB, NB])
    carry = ph.sb("carry", [NB, 1])
    first_row = ph.sb("first_row", [NB, P])
    offT = ph.sb("offT", [NB, P])
    rp_i = ph.sb("rp_i", [P, NB], I32)
    off = ph.sb("off", [P, NB])
    marks = ph.sb("marks", [RT, 2, P])
    run = ph.sb("run", [RT, 2, P])
    lastT = ph.sb("lastT", [2, RT])
    runT = ph.sb("runT", [2, RT + 1])
    rc_sb = ph.sb("rc_sb", [RT, 2])
    both = ph.sb("both", [RT, 2, P])
    chunk = ph.sb("chunk", [RT, P])
    new = ph.sb("new", [RT, P])
    blk_i = ph.sb("blk_i", [RT, 1], I32)
    nfirst_i = ph.sb("nfirst_i", [RT, 1], I32)
    blk = ph.sb("blk", [RT, 1])
    blk128 = ph.sb("blk128", [RT, 1])
    relT = ph.sb("relT", [RT, P])
    later = ph.sb("later", [RT, P])
    n_col = ph.sb("n_col", [P, RT])
    stage = ph.sb("stage", [P, 2, 1], I32)
    got = ph.sb("got", [P, 2, 2 * K], I32)
    differs = ph.sb("differs", [P, 2, K])
    pt = ph.ps("pt", [P, 8, 512])
    d_heads = c.dram("d_heads", [EROWS], I32)
    d_start = c.dram("d_start", [NP_ + P])
    d_mark = [c.dram(f"d_mark{j}", [ROWS, 1]) for j in range(2)]

    with nc.Block() as block:
        @block.gpsimd
        def _(g):
            g.iota(i_col[:], [[P, NB]], base=0, channel_multiplier=1).then_inc(s("iotas"), 1)
            g.iota(i_256[:], [[1, 2 * P]], base=0, channel_multiplier=0).then_inc(s("iotas"), 1)
            g.iota(i_row[:], [[1, P]], base=0, channel_multiplier=P).then_inc(s("iotas"), 1)
            g.memset(T.ident[:], 0.0).then_inc(s("blank"), 1)
            g.memset(upper[:], 1.0).then_inc(s("blank"), 1)
            g.wait_ge(s("blank"), 2)
            g.affine_select(out=T.ident[:], in_=T.ident[:], compare_op=ALU.not_equal, fill=1.0, base=0,
                            pattern=[[-1, P]], channel_multiplier=1).then_inc(s("masks"), 1)
            g.affine_select(out=upper[:], in_=upper[:], compare_op=ALU.is_gt, fill=0.0, base=0,
                            pattern=[[1, NB]], channel_multiplier=-1).then_inc(s("masks"), 1)
            g.wait_ge(s("tile_ready"), 1)
            for b in range(NB):
                g.indirect_dma_start(out=dsts[:, b, :], out_offset=None, in_=dst_rows[:, :],
                                     in_offset=bass.IndirectOffsetOnAxis(ap=tile_i[:, b:b + 1], axis=0)
                                     ).then_inc(s("dsts_in"), 16)
            g.wait_ge(s("marks_blank"), 32)
            g.wait_ge(s("marks_ready"), 2)
            for b in range(NB):
                for m, val in ((0, nid), (1, off)):
                    g.indirect_dma_start(out=d_mark[m][:, :], in_=val[:, b:b + 1], in_offset=None,
                                         out_offset=bass.IndirectOffsetOnAxis(ap=rp_i[:, b:b + 1], axis=0)
                                         ).then_inc(s("marked"), 16)

            def chunks(i):
                for b in range(2):
                    reuse(g, s(f"diff{b}"), i)
                    reuse(g, s(f"kept{b}"), i)
                    g.wait_ge(s(f"stage_ready{b}"), i + 1)
                    g.nop(nofuse=True)
                    g.indirect_dma_start(out=got[:, b, :], out_offset=None, in_=chunk_ix[:, :],
                                         in_offset=bass.IndirectOffsetOnAxis(ap=stage[:, b, :], axis=0)
                                         ).then_inc(s(f"got{b}"), 16)
            loop(g, RT // 2, chunks)

        @block.sync
        def _(sp):
            sp.dma_start(d_heads.unsqueeze(1), dst_rows[:, 0:1], allow_slow_non_contiguous=True).then_inc(s("heads_out"), 16)
            sp.wait_ge(s("heads_out"), 16)
            sp.dma_start(heads_i[:], d_heads.partition_broadcast(P)).then_inc(s("heads_in"), 16)
            sp.wait_ge(s("x_pad"), 1)
            sp.dma_start(T.xs[:, 0:NB - 1, :],
                         x_in[0:(NB - 1) * P, :].rearrange("(b p) f -> p b f", p=P)).then_inc(s("x_in"), 16)
            sp.dma_start(T.xs[0:N - (NB - 1) * P, NB - 1, :], x_in[(NB - 1) * P:N, :]).then_inc(s("x_in"), 16)
            sp.wait_ge(s("zeros"), 1)
            for m in range(2):
                sp.dma_start(d_mark[m].rearrange("(t p) o -> t (p o)", p=P), zeros[0:RT, :]
                             ).then_inc(s("marks_blank"), 16)
            sp.wait_ge(s("startT"), 1)
            sp.dma_start(d_start[0:NP_].rearrange("(b p) -> b p", p=P), startT[:]).then_inc(s("start_out"), 16)
            sp.dma_start(d_start[NP_:NP_ + P].unsqueeze(0), fullE[:]).then_inc(s("start_out"), 16)
            sp.wait_ge(s("start_out"), 32)
            sp.dma_start(nextT[:], d_start[1:NP_ + 1].rearrange("(b p) -> b p", p=P)).then_inc(s("next_in"), 16)
            sp.wait_ge(s("marked"), 2 * NB * 16)
            for m in range(2):
                sp.dma_start(marks[:, m, :], d_mark[m].rearrange("(t p) o -> t (p o)", p=P)
                             ).then_inc(s("marks_in"), 16)
            sp.wait_ge(s("x_in"), 32)

        @block.tensor
        def _(pe):
            pe.wait_ge(s("masks"), 2)
            pe.wait_ge(s("start"), 1)
            pe.transpose(pt[0:NB, 0, 0:P], start[:], T.ident[:]).then_inc(s("startT_ps"), 1)
            pe.wait_ge(s("rows_summed"), 1)
            pe.matmul(pt[0:NB, 1, 0:1], upper[:], last_rp[:], start=True, stop=True).then_inc(s("carry_ps"), 1)
            pe.wait_ge(s("first_row"), 2)
            pe.transpose(pt[:, 2, 0:NB], first_row[:], T.ident[0:NB, 0:NB]).then_inc(s("first_ps"), 1)
            pe.transpose(pt[:, 3, 0:NB], offT[:], T.ident[0:NB, 0:NB]).then_inc(s("first_ps"), 1)
            pe.wait_ge(s("run"), 2)
            pe.transpose(pt[0:2, 4, 0:RT], rc_sb[:], T.ident[0:RT, 0:RT]).then_inc(s("lastT_ps"), 1)
            pe.wait_ge(s("runT"), 1)
            pe.transpose(pt[0:RT, 5, 0:2], runT[:, 0:RT], T.ident[0:2, 0:2]).then_inc(s("carry2_ps"), 1)
            pe.wait_ge(s("row_cols"), 1)
            pe.transpose(pt[:, 0, 0:RT], both[:, 0, :], T.ident[0:RT, 0:RT]).then_inc(s("cols_ps"), 1)
            pe.transpose(pt[:, 1, 0:RT], chunk[:], T.ident[0:RT, 0:RT]).then_inc(s("cols_ps"), 1)
            pe.transpose(pt[:, 2, 0:RT], relT[:], T.ident[0:RT, 0:RT]).then_inc(s("cols_ps"), 1)
            pe.transpose(pt[0:1, 3, 0:RT], blk[:], T.ident[0:RT, 0:RT]).then_inc(s("cols_ps"), 1)
            pe.wait_ge(s("pens"), 1)
            pe.transpose(pt[:, 4, P:P + RT], later[:], T.ident[0:RT, 0:RT]).then_inc(s("pen_ps"), 1)
            pe.matmul(pt[0:RT, 5, 0:1], T.shift[:], T.pen[:, 0:1], start=True, stop=True).then_inc(s("pen_ps"), 1)
            pe.wait_ge(s("pens2"), 1)
            pe.matmul(pt[0:4, 6, 0:RT], T.pen_pre[:, P - 1:P].to_broadcast([RT, 4]), T.ident[0:RT, 0:RT],
                      start=True, stop=True).then_inc(s("pen2_ps"), 1)
            pe.matmul(pt[0:4, 7, 0:RT], T.pen_suf[:, 0:1].to_broadcast([RT, 4]), T.ident[0:RT, 0:RT],
                      start=True, stop=True).then_inc(s("pen2_ps"), 1)

        @block.vector
        def _(v):
            ch = Chain(v, s("dve"))
            ch.begin(0)
            v.memset(T.xs[:, NB - 1, :], 0.0).then_inc(s("x_pad"), 1)
            v.memset(zeros[:], 0.0).then_inc(s("zeros"), 1)
            v.memset(T.ones[:], 1.0)
            v.memset(fullE[:], float(E))
            v.memset(runT[:, 0:1], 0.0)
            ch.link(v.memset(onesT[:], 1.0))
            v.wait_ge(s("iotas"), 3)
            v.tensor_copy(nid[:], i_col[:])
            v.tensor_copy(T.iota256[:], i_256[:])
            v.tensor_copy(rowid[:], i_row[:])
            v.wait_ge(s("masks"), 2)
            v.memset(T.shift[:], 0.0)
            v.wait_ge(s("heads_in"), 16)
            ch.link(v.tensor_copy(heads[:], heads_i[:]))
            v.tensor_copy(T.shift[:, 0:RT - 1], T.ident[0:RT, 1:RT])
            for b in range(NB):
                ch.link(v.tensor_scalar(junk[:], heads[:], nid[:, b:b + 1], 0.0, ALU.is_lt, ALU.add,
                                        accum_out=before[:, b:b + 1]))
            ch.link(v.tensor_scalar(tile_f[:], before[:], -1.0, 0.0, ALU.add, ALU.max))
            v.tensor_copy(tile_i[:], tile_f[:]).then_inc(s("tile_ready"), 1)
            v.wait_ge(s("dsts_in"), NB * 16)
            ch.link(v.tensor_tensor(less[:], dsts[:], bcast(nid[:], [P, NB, P], 2), ALU.is_lt))
            ch.link(v.tensor_reduce(inside[:], less[:], X, ALU.add))
            v.scalar_tensor_tensor(start[:], tile_f[:], float(P), inside[:], ALU.mult, ALU.add
                                   ).then_inc(s("start"), 1)
            v.wait_ge(s("startT_ps"), 1)
            v.tensor_copy(startT[:], pt[0:NB, 0, 0:P]).then_inc(s("startT"), 1)
            v.wait_ge(s("next_in"), 16)
            v.wait_ge(s("startT"), 1)
            v.tensor_copy(qi[:, 0, :], startT[:])
            ch.link(v.tensor_scalar(q[:, 1, :], nextT[:], -1.0, None, ALU.add))
            ch.link(v.tensor_copy(qi[:, 1, :], q[:, 1, :]))
            shift = K.bit_length() - 1
            ch.link(v.tensor_single_scalar(qi[:], qi[:], shift, ALU.arith_shift_right))
            ch.link(v.tensor_copy(q[:], qi[:]))
            ch.link(v.tensor_tensor(rc[:], q[:, 1, :], q[:, 0, :], ALU.subtract))
            ch.link(v.tensor_scalar(rc[:], rc[:], 1.0, None, ALU.add))
            ch.link(v.tensor_tensor_scan(rp[:], onesT[0:NB, :], rc[:], 0.0, ALU.mult, ALU.add))
            v.tensor_copy(last_rp[:], rp[:, P - 1:P]).then_inc(s("rows_summed"), 1)
            ch.link(v.tensor_tensor(first_row[:], rp[:], rc[:], ALU.subtract))
            v.wait_ge(s("carry_ps"), 1)
            ch.link(v.tensor_copy(carry[:], pt[0:NB, 1, 0:1]))
            v.tensor_scalar(first_row[:], first_row[:], carry[:], None, ALU.add).then_inc(s("first_row"), 1)
            v.wait_ge(s("first_row"), 1)
            v.tensor_tensor(offT[:], first_row[:], q[:, 0, :], ALU.subtract).then_inc(s("first_row"), 1)
            v.wait_ge(s("first_ps"), 2)
            v.tensor_copy(rp_i[:], pt[:, 2, 0:NB]).then_inc(s("marks_ready"), 1)
            v.tensor_copy(off[:], pt[:, 3, 0:NB]).then_inc(s("marks_ready"), 1)
            v.wait_ge(s("marks_in"), 32)
            for m in range(2):
                ch.link(v.tensor_tensor_scan(run[:, m, :], marks[:, m, :], marks[:, m, :], 0.0, ALU.max, ALU.max))
            v.tensor_copy(rc_sb[:], run[:, :, P - 1]).then_inc(s("run"), 2)
            v.wait_ge(s("lastT_ps"), 1)
            ch.link(v.tensor_copy(lastT[:], pt[0:2, 4, 0:RT]))
            v.tensor_tensor_scan(runT[:, 1:RT + 1], lastT[:], lastT[:], 0.0, ALU.max, ALU.max
                                 ).then_inc(s("runT"), 1)
            v.wait_ge(s("carry2_ps"), 1)
            v.wait_ge(s("run"), 2)
            ch.link(v.tensor_copy(rc_sb[:], pt[0:RT, 5, 0:2]))
            for m in range(2):
                ch.link(v.tensor_scalar(both[:, m, :], run[:, m, :], rc_sb[:, m:m + 1], None, ALU.max))
            ch.link(v.tensor_tensor(chunk[:], rowid[:], both[:, 1, :], ALU.subtract))
            v.tensor_scalar(chunk[:], chunk[:], float(CHUNKS - 1), 0.0, ALU.min, ALU.max)
            v.tensor_tensor(new[:, 1:P], both[:, 0, 1:P], both[:, 0, 0:P - 1], ALU.not_equal)
            v.tensor_scalar(new[:, 0:1], both[:, 0, 0:1], rc_sb[:, 0:1], None, ALU.not_equal)
            ch.link(v.tensor_copy(nfirst_i[:], both[:, 0, 0:1]))
            ch.link(v.tensor_single_scalar(blk_i[:], nfirst_i[:], 7, ALU.arith_shift_right))
            ch.link(v.tensor_copy(blk[:], blk_i[:]))
            ch.link(v.tensor_scalar(blk128[:], blk[:], float(P), None, ALU.mult))
            v.tensor_scalar(relT[:], both[:, 0, :], blk128[:], None, ALU.subtract).then_inc(s("row_cols"), 1)
            ch.link(v.memset(new[0:1, 0:1], 1.0))
            ch.link(v.tensor_scalar(T.pen[:], new[:], LOW, None, ALU.mult))
            v.tensor_scalar(later[:], new[:], 0.0, NEG, ALU.is_equal, ALU.mult).then_inc(s("pens"), 1)
            v.wait_ge(s("cols_ps"), 4)
            ch.link(v.tensor_copy(n_col[:], pt[:, 0, 0:RT]))
            v.tensor_copy(T.ixs[:, :, K], n_col[:])
            v.tensor_copy(T.ixs[:, :, K + 1], pt[:, 1, 0:RT]).then_inc(s("chunk_ix"), 1)
            v.tensor_copy(T.rel[:], pt[:, 2, 0:RT])
            v.tensor_copy(T.blk[:], pt[0:1, 3, 0:RT])
            v.wait_ge(s("pen_ps"), 2)
            v.tensor_copy(T.pen_b[:, P - 1:P], pt[0:RT, 5, 0:1])
            v.tensor_copy(T.mask[:].rearrange("p (t k) -> p t k", k=SLOTS)[:, :, K], pt[:, 4, P:P + RT])
            v.wait_ge(s("pens"), 1)
            ch.link(v.tensor_copy(T.pen_b[:, 0:P - 1], T.pen[:, 1:P]))
            v.tensor_tensor_scan(T.pen_pre[:], T.pen[:], T.pen[:], 0.0, ALU.min, ALU.min)
            back = T.pen_b[:, ::-1]
            v.tensor_tensor_scan(T.pen_suf[:, ::-1], back, back, 0.0, ALU.min, ALU.min).then_inc(s("pens2"), 1)
            v.wait_ge(s("pen2_ps"), 2)
            v.tensor_copy(T.pen_tile[:], pt[0:4, 6, 0:RT])
            ch.link(v.tensor_copy(T.pen_tile_b[:], pt[0:4, 7, 0:RT]))

            prep_k = ch.k

            def masks(i):
                for b in range(2):
                    t = 2 * i + b
                    v.wait_ge(s(f"got{b}"), 16 * i + 16)
                    if not isinstance(i, int):
                        v.wait_ge(s(f"mask{b}"), i)
                    v.tensor_scalar(differs[:, b, :], got[:, b, K:2 * K], n_col[:, bass.ds(t, 1)], None,
                                    ALU.not_equal).then_inc(s(f"diff{b}"), 1)
                    v.wait_ge(s(f"diff{b}"), i + 1)
                    v.tensor_scalar(T.mask[:, bass.ds(t * SLOTS, K)], differs[:, b, :], NEG, None, ALU.mult
                                    ).then_inc(s(f"mask{b}"), 1)
            loop(v, RT // 2, masks)

        @block.scalar
        def _(a):
            a.wait_ge(s("chunk_ix"), 1)

            def copies(i):
                for b in range(2):
                    t = 2 * i + b
                    reuse(a, s(f"got{b}"), i, 16)
                    a.copy(stage[:, b, :], T.ixs[:, bass.ds(t, 1), K + 1]).then_inc(s(f"stage_ready{b}"), 1)
                for b in range(2):
                    t = 2 * i + b
                    a.wait_ge(s(f"got{b}"), 16 * i + 16)
                    a.copy(T.ixs[:, bass.ds(t, 1), 0:K], got[:, b, 0:K].unsqueeze(1)).then_inc(s(f"kept{b}"), 1)
            loop(a, RT // 2, copies)
    ph.close()




def edge_pass(c, T, name, H, C, src_w, node_w, table, node_table, part, kind, chunk_attr=None, vec=None):
    nc = c.nc
    ph = Phase(c, name)
    s = ph.sem
    F = H * (C + 1)
    FEAT = 128
    gathers = K + 1 + (kind == "conv")
    KS = SLOTS if kind == "gat" else K
    ix = ph.sb("ix", [P, U, ROW_IX], I32)
    src = ph.sb("src", [P, U, KS, src_w])
    node = ph.sb("node", [P, U, node_w]) if kind != "gat" else None
    attr = ph.sb("attr", [P, U, K * 32]) if kind == "conv" else None
    prod_w = {"conv": H * C, "gat": 1, "gatv2": H * C, "dot": H * C}[kind]
    prod = ph.sb("prod", [P, KS, prod_w])
    act = ph.sb("act", [P, K, prod_w]) if kind == "gatv2" else None
    raw = ph.sb("raw", [P, KS, H])
    lg = ph.sb("lg", [P, KS, H])
    top = ph.sb("top", [P, U, H])
    low = ph.sb("low", [P, U, KS, H])
    msg = ph.sb("msg", [P, U, KS, H, C + 1])
    sums = ph.sb("sums", [P, U, F])
    ps = ph.ps("ps", [P, U, 512])
    steps = RT // U

    with nc.Block() as block:
        @block.sync
        def _(sp):
            def body(i):
                for b in range(U):
                    reuse(sp, s(f"gathered{b}"), i, 16 * gathers)
                    sp.dma_start(ix[:, b, :], T.ixs[:, bass.ds(i * U + b, 1), :].rearrange("p o k -> p (o k)")
                                 ).then_inc(s(f"ix_in{b}"), 16)
            loop(sp, steps, body)

        @block.gpsimd
        def _(g):
            def gather(out, table_, col, b):
                g.indirect_dma_start(out=out, out_offset=None, in_=table_,
                                     in_offset=bass.IndirectOffsetOnAxis(ap=ix[:, b, col:col + 1], axis=0)
                                     ).then_inc(s(f"gathered{b}"), 16)

            def body(i):
                for b in range(U):
                    reuse(g, s(f"messages{b}"), i)
                    g.wait_ge(s(f"ix_in{b}"), 16 * i + 16)
                    g.nop(nofuse=True)
                    if kind == "gat":
                        gather(src[:, b, K, :], table[:, :], K, b)
                    else:
                        gather(node[:, b, :], node_table[:, :], K, b)
                    if kind == "conv":
                        gather(attr[:, b, :], chunk_attr[:, :], K + 1, b)
                    for k in range(K):
                        gather(src[:, b, k, :], table[:, :], k, b)
            loop(g, steps, body)

        @block.vector
        def _(v):
            ch = Chain(v, s("dve"))

            def feature_logits(b):
                if kind == "conv":
                    pv = prod[:].rearrange("p k (h c) -> p k h c", h=H)
                    nv = node[:, b, :].rearrange("p (h c) -> p h c", h=H)
                    v.tensor_tensor(pv[:, :, :, 0:FEAT], bcast(src[:, b, :, :], [P, K, H, FEAT], 2),
                                    bcast(nv[:, :, 0:FEAT], [P, K, H, FEAT], 1), ALU.mult)
                    av = attr[:, b, :].rearrange("p (k c) -> p k c", k=K)
                    ch.link(v.tensor_tensor(pv[:, :, :, FEAT:C], bcast(av, [P, K, H, C - FEAT], 2),
                                            bcast(nv[:, :, FEAT:C], [P, K, H, C - FEAT], 1), ALU.mult))
                    ch.link(v.tensor_reduce(lg[:], pv, X, ALU.add))
                    ch.link(v.tensor_tensor(raw[:], lg[:], bcast(nv[:, :, C], [P, K, H], 1), ALU.add))
                    return
                if kind == "gat":
                    ch.link(v.tensor_tensor(lg[:], src[:, b, :, H * C:H * C + H],
                                            bcast(src[:, b, K, H * C + H:], [P, KS, H], 1), ALU.add))
                elif kind == "dot":
                    ch.link(v.tensor_tensor(prod[:], src[:, b, :, 0:H * C],
                                            bcast(node[:, b, :], [P, K, H * C], 1), ALU.mult))
                    ch.link(v.tensor_reduce(lg[:], prod[:].rearrange("p k (h c) -> p k h c", h=H), X, ALU.add))
                elif kind == "gatv2":
                    ch.link(v.tensor_tensor(prod[:], src[:, b, :, :], bcast(node[:, b, :], [P, K, H * C], 1), ALU.add))
                    ch.link(v.scalar_tensor_tensor(act[:], prod[:], NEG_SLOPE, prod[:], ALU.mult, ALU.max))
                    ch.link(v.tensor_tensor(prod[:], act[:], bcast(vec[:], [P, K, H * C], 1), ALU.mult))
                    ch.link(v.tensor_reduce(raw[:], prod[:].rearrange("p k (h c) -> p k h c", h=H), X, ALU.add))
                    return
                ch.link(v.scalar_tensor_tensor(raw[:], lg[:], NEG_SLOPE, lg[:], ALU.mult, ALU.max))

            def body(i):
                ch.begin(i)
                for b in range(U):
                    t = i * U + b
                    v.wait_ge(s(f"gathered{b}"), (16 * i + 16) * gathers)
                    feature_logits(b)
                    ch.link(v.tensor_tensor(lg[:], raw[:], bcast(T.mask[:, bass.ds(t * SLOTS, KS)], [P, KS, H], 2), ALU.add))
                    reuse(v, s(f"tops_kept{b}"), i)
                    ch.link(v.tensor_reduce(top[:, b, :], lg[:].rearrange("p k h -> p h k"), X, ALU.max))
                    v.tensor_tensor(low[:, b, :, :], lg[:], bcast(top[:, b, :], [P, KS, H], 1), ALU.subtract
                                    ).then_inc(s(f"logits{b}"), 1)
                    v.wait_ge(s(f"weights{b}"), i + 1)
                    w = msg[:, b, :, :, C:C + 1]
                    if kind == "conv":
                        v.tensor_tensor(msg[:, b, :, :, 0:FEAT], bcast(src[:, b, :, :], [P, K, H, FEAT], 2),
                                        w.to_broadcast([P, K, H, FEAT]), ALU.mult)
                        av = attr[:, b, :].rearrange("p (k c) -> p k c", k=K)
                        last = v.tensor_tensor(msg[:, b, :, :, FEAT:C], bcast(av, [P, K, H, C - FEAT], 2),
                                               w.to_broadcast([P, K, H, C - FEAT]), ALU.mult)
                    else:
                        at = H * C if kind == "dot" else 0
                        val = src[:, b, :, at:at + H * C].rearrange("p k (h c) -> p k h c", h=H)
                        last = v.tensor_tensor(msg[:, b, :, :, 0:C], val, w.to_broadcast([P, KS, H, C]), ALU.mult)
                    last.then_inc(s(f"messages{b}"), 1)
            loop(v, steps, body)

        @block.tensor
        def _(pe):
            def body(i):
                for b in range(U):
                    pe.wait_ge(s(f"messages{b}"), i + 1)
                    reuse(pe, s(f"evacuated{b}"), i)
                    for k in range(KS):
                        last = pe.matmul(ps[:, b, 0:F], T.ident[:], msg[:, b, k, :, :].rearrange("p h c -> p (h c)"),
                                         start=(k == 0), stop=(k == KS - 1))
                    last.then_inc(s(f"summed{b}"), 1)
            loop(pe, steps, body)

        @block.scalar
        def _(a):
            def body(i):
                for b in range(U):
                    t = i * U + b
                    a.wait_ge(s(f"logits{b}"), i + 1)
                    reuse(a, s(f"summed{b}"), i)
                    a.activation(msg[:, b, :, :, C], low[:, b, :, :], ACT.Exp).then_inc(s(f"weights{b}"), 1)
                    a.copy(T.m[:, bass.ds(t * H, H)], top[:, b, :]).then_inc(s(f"tops_kept{b}"), 1)
                    a.wait_ge(s(f"summed{b}"), i + 1)
                    reuse(a, s(f"stored{b}"), i, 16)
                    a.copy(sums[:, b, :], ps[:, b, 0:F]).then_inc(s(f"evacuated{b}"), 1)
                    a.wait_ge(s(f"evacuated{b}"), i + 1)
                    a.dma_start(part[bass.ds(t * P, P), :], sums[:, b, :]).then_inc(s(f"stored{b}"), 16)
            loop(a, steps, body)
            for b in range(U):
                a.wait_ge(s(f"stored{b}"), 16 * steps)
    ph.close()


def node_maxima(c, T, name, H):
    nc = c.nc
    ph = Phase(c, name)
    s = ph.sem
    mh = ph.sb("mh", [P, H, RT])
    fwd = ph.sb("fwd", [RT, H, P])
    full = ph.sb("full", [RT, H, P])
    bwd = ph.sb("bwd", [RT, H, P])
    whole = ph.sb("whole", [RT, H, P])
    edge = ph.sb("edge", [RT, 2, H])
    edgeT = ph.sb("edgeT", [H, 2, RT])
    runs = ph.sb("runs", [H, 2, RT + 1])
    into = ph.sb("into", [RT, 2, H])
    gap = ph.sb("gap", [P, RT, H])
    pt = ph.ps("pt", [P, 8, 512])

    with nc.Block() as block:
        @block.tensor
        def _(pe):
            pe.wait_ge(s("by_head"), 1)
            for h in range(H):
                last = pe.transpose(pt[0:RT, 0, h * P:(h + 1) * P], mh[:, h, :], T.ident[:])
            last.then_inc(s("rows_T"), 1)
            for d in range(2):
                pe.wait_ge(s("edge"), d + 1)
                pe.transpose(pt[0:H, 1 + d, 0:RT], edge[:, d, :], T.ident[0:RT, 0:RT]).then_inc(s("edge_T"), 1)
                pe.wait_ge(s("runs"), d + 1)
                at = d
                pe.transpose(pt[0:RT, 3 + d, 0:H], runs[:, d, at:at + RT], T.ident[0:H, 0:H]).then_inc(s("into_T"), 1)
            pe.wait_ge(s("whole"), 1)
            for h in range(H):
                last = pe.transpose(pt[:, 5, h * RT:(h + 1) * RT], whole[:, h, :], T.ident[0:RT, 0:RT])
            last.then_inc(s("maxima"), 1)

        @block.vector
        def _(v):
            ch = Chain(v, s("dve"))
            ch.begin(0)
            v.memset(runs[:], LOW)
            v.tensor_copy(mh[:], T.m[:, 0:RT * H].rearrange("p (t h) -> p h t", h=H)).then_inc(s("by_head"), 1)
            v.wait_ge(s("rows_T"), 1)
            for h in range(H):
                last = v.tensor_tensor_scan(fwd[:, h, :], T.pen[:], pt[0:RT, 0, h * P:(h + 1) * P], LOW,
                                            ALU.add, ALU.max)
            ch.link(last)
            v.tensor_copy(edge[:, 0, :], fwd[:, :, P - 1]).then_inc(s("edge"), 1)
            v.wait_ge(s("edge_T"), 1)
            ch.link(v.tensor_copy(edgeT[:, 0, :], pt[0:H, 1, 0:RT]))
            v.tensor_tensor_scan(runs[:, 0, 1:RT + 1], T.pen_tile[0:H, :], edgeT[:, 0, :], LOW, ALU.add, ALU.max
                                 ).then_inc(s("runs"), 1)
            v.wait_ge(s("into_T"), 1)
            ch.link(v.tensor_copy(into[:, 0, :], pt[0:RT, 3, 0:H]))
            for h in range(H):
                last = v.scalar_tensor_tensor(full[:, h, :], T.pen_pre[:], into[:, 0, h:h + 1], fwd[:, h, :],
                                              ALU.add, ALU.max)
            ch.link(last)
            for h in range(H):
                last = v.tensor_tensor_scan(bwd[:, h, ::-1], T.pen_b[:, ::-1], full[:, h, ::-1], LOW,
                                            ALU.add, ALU.max)
            ch.link(last)
            v.tensor_copy(edge[:, 1, :], bwd[:, :, 0]).then_inc(s("edge"), 1)
            v.wait_ge(s("edge_T"), 2)
            ch.link(v.tensor_copy(edgeT[:, 1, :], pt[0:H, 2, 0:RT]))
            v.tensor_tensor_scan(runs[:, 1, 0:RT][:, ::-1], T.pen_tile_b[0:H, ::-1], edgeT[:, 1, ::-1], LOW,
                                 ALU.add, ALU.max).then_inc(s("runs"), 1)
            v.wait_ge(s("into_T"), 2)
            ch.link(v.tensor_copy(into[:, 1, :], pt[0:RT, 4, 0:H]))
            for h in range(H):
                last = v.scalar_tensor_tensor(whole[:, h, :], T.pen_suf[:], into[:, 1, h:h + 1], bwd[:, h, :],
                                              ALU.add, ALU.max)
            last.then_inc(s("whole"), 1)
            v.wait_ge(s("maxima"), 1)
            v.tensor_tensor(gap[:], T.m[:, 0:RT * H].rearrange("p (t h) -> p t h", h=H),
                            pt[:, 5, 0:H * RT].rearrange("p (h t) -> p t h", h=H), ALU.subtract).then_inc(s("gap"), 1)

        @block.scalar
        def _(a):
            a.wait_ge(s("gap"), 1)
            a.activation(T.factor[:, 0:RT * H], gap[:].rearrange("p t h -> p (t h)"), ACT.Exp).then_inc(s("factor"), 1)
            a.wait_ge(s("factor"), 1)
    ph.close()


def global_maximum(c, T, name, H):
    nc = c.nc
    ph = Phase(c, name)
    s = ph.sem
    top = ph.sb("top", [P, 1])
    neg = ph.sb("neg", [1, 1])
    shift = ph.sb("shift", [P, 1])
    pt = ph.ps("pt", [P, 2, 512])

    with nc.Block() as block:
        @block.vector
        def _(v):
            v.tensor_reduce(top[:], T.m[:, 0:RT * H], X, ALU.max).then_inc(s("top"), 1)
            v.wait_ge(s("top_T"), 1)
            v.tensor_reduce(neg[:], pt[0:1, 0, 0:P], X, ALU.max, negate=True).then_inc(s("neg"), 1)
            v.wait_ge(s("spread"), 1)
            v.tensor_copy(shift[:], pt[:, 1, 0:1]).then_inc(s("shift"), 1)

        @block.tensor
        def _(pe):
            pe.wait_ge(s("top"), 1)
            pe.transpose(pt[0:1, 0, 0:P], top[:], T.ident[:]).then_inc(s("top_T"), 1)
            pe.wait_ge(s("neg"), 1)
            pe.matmul(pt[:, 1, 0:1], T.ones[:], neg[:], start=True, stop=True).then_inc(s("spread"), 1)

        @block.scalar
        def _(a):
            a.wait_ge(s("shift"), 1)
            a.activation(T.factor[:, 0:RT * H], T.m[:, 0:RT * H], ACT.Exp, bias=shift[:]).then_inc(s("factor"), 1)
            a.wait_ge(s("factor"), 1)
    ph.close()


def merge_rows(c, T, name, H, C, part):
    nc = c.nc
    ph = Phase(c, name)
    s = ph.sem
    F = H * (C + 1)
    rows = ph.sb("rows", [P, U, F])
    scaled = ph.sb("scaled", [P, U, F])
    onehot = ph.sb("onehot", [P, U, 2 * P])
    ps = ph.ps("ps", [P, 2 * U, 512])
    acc = T.acc[:, 0:(NB + 1) * F].rearrange("p (b f) -> p b f", f=F)
    steps = RT // U

    with nc.Block() as block:
        @block.sync
        def _(sp):
            def body(i):
                for b in range(U):
                    reuse(sp, s(f"scaled{b}"), i)
                    sp.dma_start(rows[:, b, :], part[bass.ds((i * U + b) * P, P), :]).then_inc(s(f"rows_in{b}"), 16)
            loop(sp, steps, body)

        @block.vector
        def _(v):
            v.memset(acc, 0.0).then_inc(s("added"), 1)

            def body(i):
                for b in range(U):
                    t = i * U + b
                    reuse(v, s(f"spread{b}"), i)
                    v.tensor_scalar(onehot[:, b, :], T.iota256[:], T.rel[:, bass.ds(t, 1)], None, ALU.is_equal)
                    v.wait_ge(s(f"rows_in{b}"), 16 * i + 16)
                    v.tensor_tensor(scaled[:, b, :].rearrange("p (h c) -> p h c", h=H),
                                    rows[:, b, :].rearrange("p (h c) -> p h c", h=H),
                                    bcast(T.factor[:, bass.ds(t * H, H)], [P, H, C + 1], 2), ALU.mult
                                    ).then_inc(s(f"scaled{b}"), 1)
                for b in range(U):
                    t = i * U + b
                    block_of = v.value_load(T.blk[0:1, bass.ds(t, 1)], min_val=0, max_val=NB - 1)
                    v.wait_ge(s(f"spread{b}"), i + 1)
                    v.nop(nofuse=True)
                    half = ps[:, 2 * b:2 * b + 2, 0:F]
                    v.wait_ge(s("added"), i * U + b + 1)
                    v.tensor_tensor(acc[:, bass.ds(block_of, 2), :], acc[:, bass.ds(block_of, 2), :], half, ALU.add
                                    ).then_inc(s("added"), 1)
            loop(v, steps, body)
            v.wait_ge(s("added"), RT + 1)

        @block.tensor
        def _(pe):
            def body(i):
                for b in range(U):
                    pe.wait_ge(s(f"scaled{b}"), i + 1)
                    if not isinstance(i, int):
                        pe.wait_ge(s("added"), i * U + b - 1)
                    for j in range(2):
                        last = pe.matmul(ps[:, 2 * b + j, 0:F], onehot[:, b, j * P:(j + 1) * P],
                                         scaled[:, b, :], start=True, stop=True)
                    last.then_inc(s(f"spread{b}"), 1)
            loop(pe, steps, body)
    ph.close()


LN_EPS = 1e-5


class Dense:

    def __init__(self, c, T, name, H=0, C=0):
        self.c, self.T, self.nc = c, T, c.nc
        self.ph = Phase(c, name)
        self.s, self.sb = self.ph.sem, self.ph.sb
        self.pt = self.ph.ps("pt", [P, 8, 512])
        self.small = self.sb("small", [P, 3, G])
        self.cen = self.sb("cen", [P, G, P])
        self.sq = self.sb("sq", [P, G, P])
        if H:
            F = H * (C + 1)
            self.acc = T.acc[:, 0:NB * F].rearrange("p (b h c) -> p b h c", h=H, c=C + 1)

    def group(self, ap, i):
        return ap[:, bass.ds(i * G, G)]

    def hT_slot(self, j):
        return self.pt[:, 5 + j // 4, (j % 4) * P:(j % 4) * P + P]

    def norm_vector(self, v, ch, i, src, out, tag, relu=False, gain=None, shift=None):
        s, small, cen, sq = self.s, self.small, self.cen, self.sq
        ch.link(v.tensor_reduce(small[:, 0, :], src, X, ALU.add))
        ch.link(v.tensor_scalar(small[:, 0, :], small[:, 0, :], -1.0 / P, None, ALU.mult))
        ch.link(v.tensor_tensor(cen[:], src, bcast(small[:, 0, :], [P, G, P], 2), ALU.add))
        ch.link(v.tensor_tensor(sq[:], cen[:], cen[:], ALU.mult))
        ch.link(v.tensor_reduce(small[:, 1, :], sq[:], X, ALU.add))
        v.tensor_scalar(small[:, 1, :], small[:, 1, :], 1.0 / P, LN_EPS, ALU.mult, ALU.add).then_inc(s(f"{tag}_var"), 1)
        v.wait_ge(s(f"{tag}_std"), i + 1)
        ch.link(v.reciprocal(small[:, 2, :], small[:, 2, :]))
        ch.link(v.tensor_tensor(sq[:], cen[:], bcast(small[:, 2, :], [P, G, P], 2), ALU.mult))
        if gain is not None:
            ch.link(v.tensor_tensor(cen[:], sq[:], bcast(gain[:], [P, G, P], 1), ALU.mult))
            return v.tensor_tensor(out, cen[:], bcast(shift[:], [P, G, P], 1), ALU.add)
        return v.tensor_scalar(out, sq[:], 0.0, None, ALU.max)

    def norm_scalar(self, a, i, tag):
        a.wait_ge(self.s(f"{tag}_var"), i + 1)
        a.activation(self.small[:, 2, :], self.small[:, 1, :], ACT.Sqrt).then_inc(self.s(f"{tag}_std"), 1)


def rows_of(table, i, n=G):
    return table[bass.ds(i * (G * P), n * P), :].rearrange("(b p) w -> p b w", p=P)


def node_in(c, T, W, table, node_table):
    d = Dense(c, T, "in")
    s, pt = d.s, d.pt
    h = d.sb("h", [P, G, P])
    hT = d.sb("hT", [P, G, P])
    wq = d.sb("wq", [P, 2 * P])
    bq = d.sb("bq", [P, 2])
    kx = d.sb("kx", [P, 2, 161])
    qT = d.sb("qT", [P, G, 2, P])
    td = d.sb("td", [P, G, 322])
    with c.nc.Block() as block:
        @block.sync
        def _(sp):
            for t, w in ((wq, "L0_WqT"), (bq, "L0_bq"), (kx, "L0_kx")):
                sp.dma_start(t[:], W[w]).then_inc(s("weights_in"), 16)

            def body(i):
                sp.wait_ge(s("h"), i + 1)
                sp.dma_start(rows_of(table, i), h[:]).then_inc(s("h_out"), 16)
                sp.wait_ge(s("td"), i + 1)
                sp.dma_start(rows_of(node_table, i), td[:]).then_inc(s("td_out"), 16)
            loop(sp, NG, body)
            sp.wait_ge(s("h_out"), 16 * NG)
            sp.wait_ge(s("td_out"), 16 * NG)

        @block.vector
        def _(v):
            ch = Chain(v, s("dve"))
            v.wait_ge(s("weights_in"), 48)

            def body(i):
                ch.begin(i)
                reuse(v, s("h_out"), i, 16)
                reuse(v, s("hs"), i)
                reuse(v, s("hT_ps"), i)
                d.norm_vector(v, ch, i, d.group(T.xs, i), h[:], "ln", relu=True).then_inc(s("h"), 1)
                v.wait_ge(s("qT_ps"), i + 1)
                for m in range(2):
                    last = v.tensor_scalar(qT[:, :, m, :], pt[:, 0:G, (1 + m) * P:(2 + m) * P], bq[:, m:m + 1],
                                           float(P) ** -0.5, ALU.add, ALU.mult)
                last.then_inc(s("qT"), 1)
            loop(v, NG, body)

        @block.tensor
        def _(pe):
            def body(i):
                pe.wait_ge(s("h"), i + 1)
                reuse(pe, s("td"), i)
                for j in range(G):
                    last = pe.transpose(pt[:, j, 0:P], h[:, j, :], T.ident[:])
                last.then_inc(s("hT_ps"), 1)
                pe.wait_ge(s("hT"), i + 1)
                for j in range(G):
                    for m in range(2):
                        last = pe.matmul(pt[:, j, (1 + m) * P:(2 + m) * P], wq[:, m * P:(m + 1) * P], hT[:, j, :],
                                         start=True, stop=True)
                last.then_inc(s("qT_ps"), 1)
                pe.wait_ge(s("qT"), i + 1)
                for j in range(G):
                    for m in range(2):
                        last = pe.matmul(pt[:, j, m * 161:(m + 1) * 161], qT[:, j, m, :], kx[:, m, :],
                                         start=True, stop=True)
                last.then_inc(s("td_ps"), 1)
            loop(pe, NG, body)

        @block.scalar
        def _(a):
            def body(i):
                d.norm_scalar(a, i, "ln")
                a.wait_ge(s("h"), i + 1)
                a.copy(d.group(T.hs, i), h[:]).then_inc(s("hs"), 1)
                a.wait_ge(s("hT_ps"), i + 1)
                a.copy(hT[:], pt[:, 0:G, 0:P]).then_inc(s("hT"), 1)
                a.wait_ge(s("td_ps"), i + 1)
                reuse(a, s("td_out"), i, 16)
                a.copy(td[:], pt[:, 0:G, 0:322]).then_inc(s("td"), 1)
            loop(a, NG, body)
    d.ph.close()


def project_vector(d, v, ch, i, H, C, rows, a_src, a_dst, prod):
    s = d.s
    v.wait_ge(s("xp"), i + 1)
    pv = prod[:, :, 0:H * C]
    by_head = pv.rearrange("p g (h c) -> p g h c", h=H)
    ch.link(v.tensor_tensor(pv, rows[:, :, 0:H * C], bcast(a_src[:, 0:H * C], [P, G, H * C], 1), ALU.mult))
    ch.link(v.tensor_reduce(rows[:, :, H * C:H * C + H], by_head, X, ALU.add))
    ch.link(v.tensor_tensor(pv, rows[:, :, 0:H * C], bcast(a_dst[:, 0:H * C], [P, G, H * C], 1), ALU.mult))
    v.tensor_reduce(rows[:, :, H * C + H:], by_head, X, ALU.add).then_inc(s("rows"), 1)


def node_after_conv(c, T, W, table):
    H, C, HC = 2, 160, 256
    d = Dense(c, T, "conv_out", H, C)
    s, pt = d.s, d.pt
    names = {"wv": ("L0_WvT", [P, 2 * P]), "web": ("L0_web", [33, 2, P]), "wskip": ("L0_WskipT", [P, P]),
             "bskip": ("L0_bskip", [1, P]), "w1": ("L0_W1T", [P, 2 * P]), "b1": ("L0_b1", [P, 2]),
             "w2": ("L0_W2T", [P, 2, P]), "b2": ("L0_b2", [1, P]), "w0": ("L1_W0", [P, HC])}
    w = {k: d.sb(k, shape) for k, (_, shape) in names.items()}
    vecs = {k: d.sb(k, [P, W[n].shape[-1]]) for k, n in
            (("g1", "L0_ln1_g"), ("s1", "L0_ln1_b"), ("g2", "L0_ln2_g"), ("s2", "L0_ln2_b"),
             ("a_src", "L1_as0"), ("a_dst", "L1_ad0"))}
    vec_of = {"g1": "L0_ln1_g", "s1": "L0_ln1_b", "g2": "L0_ln2_g", "s2": "L0_ln2_b",
              "a_src": "L1_as0", "a_dst": "L1_ad0"}
    rden = d.sb("rden", [P, G, H])
    den = d.sb("den", [P, G, H])
    agg = d.sb("agg", [P, G, H, C + 1])
    aggT = d.sb("aggT", [P, G, H, P])
    attT = d.sb("attT", [33, G, H, P])
    h0 = d.sb("h0", [P, G, P])
    hT = d.sb("hT", [P, G, P])
    pre = d.sb("pre", [P, G, P])
    pre2 = d.sb("pre2", [P, G, P])
    h1 = d.sb("h1", [P, G, P])
    h1T = d.sb("h1T", [P, G, P])
    up = d.sb("up", [P, 2, G, P])
    f1 = d.sb("f1", [P, 2, G, P])
    x1 = d.sb("x1", [P, G, P])
    h = d.sb("h", [P, G, P])
    rows = d.sb("rows", [P, G, HC + 8])
    prod = d.sb("prod", [P, G, HC])
    n_loads = len(w) + len(vecs)

    with c.nc.Block() as block:
        @block.sync
        def _(sp):
            for k, (n, _) in names.items():
                sp.dma_start(w[k][:], W[n]).then_inc(s("weights_in"), 16)
            for k, t in vecs.items():
                sp.dma_start(t[:], W[vec_of[k]].partition_broadcast(P)).then_inc(s("weights_in"), 16)

            def body(i):
                sp.wait_ge(s("rows"), i + 1)
                sp.dma_start(rows_of(table, i), rows[:]).then_inc(s("rows_out"), 16)
            loop(sp, NG, body)
            sp.wait_ge(s("rows_out"), 16 * NG)

        @block.vector
        def _(v):
            ch = Chain(v, s("dve"))
            v.wait_ge(s("weights_in"), 16 * n_loads)

            def body(i):
                ch.begin(i)
                acc = d.group(d.acc, i)
                ch.link(v.tensor_scalar(den[:], acc[:, :, :, C], 1e-16, None, ALU.add))
                ch.link(v.reciprocal(rden[:], den[:]))
                reuse(v, s("aggT_ps"), i)
                v.tensor_tensor(agg[:], acc, bcast(rden[:], [P, G, H, C + 1], 3), ALU.mult).then_inc(s("agg"), 1)
                v.wait_ge(s("mixed"), i + 1)
                ch.link(v.scalar_tensor_tensor(pre[:], pt[:, 0:G, 0:P], 0.5, h0[:], ALU.mult, ALU.add))
                ch.link(v.tensor_tensor(pre2[:], pre[:], pt[:, 0:G, P:2 * P], ALU.add))
                d.norm_vector(v, ch, i, pre2[:], h1[:], "ln1", gain=vecs["g1"], shift=vecs["s1"]
                              ).then_inc(s("h1"), 1)
                v.wait_ge(s("up"), i + 1)
                v.scalar_tensor_tensor(f1[:].rearrange("p m g n -> p (m g n)"), up[:].rearrange("p m g n -> p (m g n)"),
                                       0.01, up[:].rearrange("p m g n -> p (m g n)"), ALU.mult, ALU.max
                                       ).then_inc(s("f1"), 1)
                v.wait_ge(s("f2_ps"), i + 1)
                ch.link(v.tensor_tensor(pre[:], h1[:], pt[:, 0:G, 0:P], ALU.add))
                ch.link(d.norm_vector(v, ch, i, pre[:], pre2[:], "ln2", gain=vecs["g2"], shift=vecs["s2"]))
                ch.link(v.tensor_tensor(x1[:], d.group(T.xs, i), pre2[:], ALU.add))
                v.tensor_scalar(d.group(T.xs, i), x1[:], 1.0, None, ALU.mult)
                d.norm_vector(v, ch, i, x1[:], h[:], "ln3").then_inc(s("h"), 1)
                project_vector(d, v, ch, i, 4, 64, rows, vecs["a_src"], vecs["a_dst"], prod)
            loop(v, NG, body)

        @block.tensor
        def _(pe):
            pe.wait_ge(s("weights_in"), 16 * n_loads)

            def body(i):
                reuse(pe, s("xp"), i)
                pe.wait_ge(s("agg"), i + 1)
                for j in range(G):
                    for m in range(H):
                        pe.transpose(pt[:, j, m * 256:m * 256 + P], agg[:, j, m, 0:P], T.ident[:])
                        pe.transpose(pt[0:33, j, m * 256 + P:m * 256 + 2 * P], agg[:, j, m, P:161], T.ident[:])
                pe.wait_ge(s("h0"), i + 1)
                for j in range(G):
                    last = pe.transpose(d.hT_slot(j), h0[:, j, :], T.ident[:])
                last.then_inc(s("aggT_ps"), 1)
                pe.wait_ge(s("aggT"), i + 1)
                for j in range(G):
                    for m in range(H):
                        pe.matmul(pt[:, j, 0:P], aggT[:, j, m, :], w["wv"][:, m * P:(m + 1) * P],
                                  start=(m == 0), stop=False)
                        pe.matmul(pt[:, j, 0:P], attT[:, j, m, :], w["web"][:, m, :], start=False, stop=(m == H - 1))
                    pe.matmul(pt[:, j, P:2 * P], hT[:, j, :], w["wskip"][:], start=True, stop=False)
                    last = pe.matmul(pt[:, j, P:2 * P], T.ones[:], w["bskip"][:], start=False, stop=True)
                last.then_inc(s("mixed"), 1)
                pe.wait_ge(s("h1"), i + 1)
                for j in range(G):
                    last = pe.transpose(d.hT_slot(j), h1[:, j, :], T.ident[:])
                last.then_inc(s("h1T_ps"), 1)
                pe.wait_ge(s("h1T"), i + 1)
                for j in range(G):
                    for m in range(2):
                        last = pe.matmul(pt[:, j, m * P:(m + 1) * P], w["w1"][:, m * P:(m + 1) * P], h1T[:, j, :],
                                         start=True, stop=True)
                last.then_inc(s("up_ps"), 1)
                pe.wait_ge(s("f1"), i + 1)
                for j in range(G):
                    for m in range(2):
                        pe.matmul(pt[:, j, 0:P], f1[:, m, j, :], w["w2"][:, m, :], start=(m == 0), stop=False)
                    last = pe.matmul(pt[:, j, 0:P], T.ones[:], w["b2"][:], start=False, stop=True)
                last.then_inc(s("f2_ps"), 1)
                pe.wait_ge(s("h"), i + 1)
                for j in range(G):
                    last = pe.transpose(d.hT_slot(j), h[:, j, :], T.ident[:])
                last.then_inc(s("hT2_ps"), 1)
                pe.wait_ge(s("hT2"), i + 1)
                for j in range(G):
                    last = pe.matmul(pt[:, j, 0:HC], hT[:, j, :], w["w0"][:], start=True, stop=True)
                last.then_inc(s("xp_ps"), 1)
            loop(pe, NG, body)

        @block.scalar
        def _(a):
            a.wait_ge(s("weights_in"), 16 * n_loads)

            def slots(out, tag, i):
                a.copy(out[:, 0:4, :], pt[:, 5, :].rearrange("p (g n) -> p g n", g=4))
                a.copy(out[:, 4, :], pt[:, 6, 0:P]).then_inc(s(tag), 1)

            def body(i):
                reuse(a, s("mixed"), i)
                reuse(a, s("h1"), i)
                a.copy(h0[:], d.group(T.hs, i)).then_inc(s("h0"), 1)
                a.wait_ge(s("aggT_ps"), i + 1)
                pv = pt[:, 0:G, :].rearrange("p g (m n) -> p g m n", m=2)
                a.copy(aggT[:], pv[:, :, :, 0:P])
                a.copy(attT[:], pv[0:33, :, :, P:2 * P])
                reuse(a, s("xp_ps"), i)
                slots(hT, "aggT", i)
                d.norm_scalar(a, i, "ln1")
                a.wait_ge(s("h1T_ps"), i + 1)
                slots(h1T, "h1T", i)
                a.wait_ge(s("up_ps"), i + 1)
                for m in range(2):
                    last = a.activation(up[:, m, :, :], pt[:, 0:G, m * P:(m + 1) * P], ACT.Identity,
                                        bias=w["b1"][:, m:m + 1])
                last.then_inc(s("up"), 1)
                d.norm_scalar(a, i, "ln2")
                d.norm_scalar(a, i, "ln3")
                a.wait_ge(s("hT2_ps"), i + 1)
                slots(hT, "hT2", i)
                a.wait_ge(s("xp_ps"), i + 1)
                reuse(a, s("rows_out"), i, 16)
                a.copy(rows[:, :, 0:HC], pt[:, 0:G, 0:HC]).then_inc(s("xp"), 1)
            loop(a, NG, body)
    d.ph.close()


def node_between_gats(c, T, W, name, bias_n, w_n, as_n, ad_n, HC, table):
    H, C = 4, 64
    d = Dense(c, T, name, H, C)
    s, pt = d.s, d.pt
    w = d.sb("w", [P, 2, HC])
    vecs = {k: d.sb(k, [P, W[n].shape[-1]]) for k, n in (("b", bias_n), ("a_src", as_n), ("a_dst", ad_n))}
    vec_of = {"b": bias_n, "a_src": as_n, "a_dst": ad_n}
    rden = d.sb("rden", [P, G, H])
    o = d.sb("o", [P, G, H * C])
    o2 = d.sb("o2", [P, G, H * C])
    h = d.sb("h", [P, G, H * C])
    hT = d.sb("hT", [P, G, 2, P])
    rows = d.sb("rows", [P, G, HC + 8])
    prod = d.sb("prod", [P, G, HC])
    with c.nc.Block() as block:
        @block.sync
        def _(sp):
            sp.dma_start(w[:], W[w_n]).then_inc(s("weights_in"), 16)
            for k, t in vecs.items():
                sp.dma_start(t[:], W[vec_of[k]].partition_broadcast(P)).then_inc(s("weights_in"), 16)

            def body(i):
                sp.wait_ge(s("rows"), i + 1)
                sp.dma_start(rows_of(table, i), rows[:]).then_inc(s("rows_out"), 16)
            loop(sp, NG, body)
            sp.wait_ge(s("rows_out"), 16 * NG)

        @block.vector
        def _(v):
            ch = Chain(v, s("dve"))
            v.wait_ge(s("weights_in"), 64)

            def body(i):
                ch.begin(i)
                acc = d.group(d.acc, i)
                v.nop(nofuse=True)
                ch.link(v.tensor_copy(rden[:], acc[:, :, :, C]))
                ch.link(v.reciprocal(rden[:], rden[:]))
                ch.link(v.tensor_tensor(o[:].rearrange("p g (h c) -> p g h c", h=H), acc[:, :, :, 0:C],
                                        bcast(rden[:], [P, G, H, C], 3), ALU.mult))
                ch.link(v.tensor_tensor(o2[:], o[:], bcast(vecs["b"][:], [P, G, H * C], 1), ALU.add))
                reuse(v, s("hT_ps"), i)
                v.tensor_scalar(h[:], o2[:], 0.0, None, ALU.max).then_inc(s("h"), 1)
                project_vector(d, v, ch, i, 4, HC // 4, rows, vecs["a_src"], vecs["a_dst"], prod)
            loop(v, NG, body)

        @block.tensor
        def _(pe):
            pe.wait_ge(s("weights_in"), 64)

            def body(i):
                reuse(pe, s("xp"), i)
                pe.wait_ge(s("h"), i + 1)
                for j in range(G):
                    for m in range(2):
                        last = pe.transpose(pt[:, j, m * P:(m + 1) * P], h[:, j, m * P:(m + 1) * P], T.ident[:])
                last.then_inc(s("hT_ps"), 1)
                pe.wait_ge(s("hT"), i + 1)
                for j in range(G):
                    for m in range(2):
                        last = pe.matmul(pt[:, j, 256:256 + HC], hT[:, j, m, :], w[:, m, :], start=(m == 0), stop=(m == 1))
                last.then_inc(s("xp_ps"), 1)
            loop(pe, NG, body)

        @block.scalar
        def _(a):
            def body(i):
                a.wait_ge(s("hT_ps"), i + 1)
                a.copy(hT[:], pt[:, 0:G, 0:256].rearrange("p g (m n) -> p g m n", m=2)).then_inc(s("hT"), 1)
                a.wait_ge(s("xp_ps"), i + 1)
                reuse(a, s("rows_out"), i, 16)
                a.copy(rows[:, :, 0:HC], pt[:, 0:G, 256:256 + HC]).then_inc(s("xp"), 1)
            loop(a, NG, body)
    d.ph.close()


KNOT0, KNOTS, STEP = 4, 11, 0.25
BASES = 7


def node_kan(c, T, W, table, node_table):
    H, C = 4, 32
    d = Dense(c, T, "kan", H, C)
    s, pt = d.s, d.pt
    w = d.sb("w", [P, 1 + BASES, 2 * P])
    b2 = d.sb("b2", [P, P])
    knots = d.sb("knots", [P, KNOTS])
    rden = d.sb("rden", [P, G, H])
    o = d.sb("o", [P, G, P])
    o2 = d.sb("o2", [P, G, P])
    x2 = d.sb("x2", [P, G, P])
    h = d.sb("h", [P, G, P])
    hT = d.sb("hT", [P, G, P])
    ex = d.sb("ex", [P, G, P])
    sig = d.sb("sig", [P, G, P])
    dist = d.sb("dist", [P, KNOTS, P])
    ge = d.sb("ge", [P, KNOTS, P])
    bs = d.sb("bs", [P, KNOTS, P])
    left = d.sb("left", [P, KNOTS, P])
    right = d.sb("right", [P, KNOTS, P])
    cubic = d.sb("cubic", [P, BASES, P])
    feat = d.sb("feat", [P, G, 1 + BASES, P])
    both = d.sb("both", [P, G, 2 * P])
    with c.nc.Block() as block:
        @block.sync
        def _(sp):
            sp.dma_start(w[:], W["L2_w"]).then_inc(s("weights_in"), 16)
            sp.dma_start(b2[:], W["L1_b2"].partition_broadcast(P)).then_inc(s("weights_in"), 16)

            def body(i):
                sp.wait_ge(s("both"), i + 1)
                sp.dma_start(rows_of(table, i), both[:, :, 0:P]).then_inc(s("both_out"), 16)
                sp.dma_start(rows_of(node_table, i), both[:, :, P:2 * P]).then_inc(s("both_out"), 16)
            loop(sp, NG, body)
            sp.wait_ge(s("both_out"), 32 * NG)

        @block.vector
        def _(v):
            ch = Chain(v, s("dve"))
            ch.begin(0)
            for j in range(KNOTS):
                last = v.memset(knots[:, j:j + 1], -1.75 + STEP * (KNOT0 + j))
            last.then_inc(s("knots"), 1)
            v.wait_ge(s("knots"), 1)
            v.wait_ge(s("weights_in"), 32)

            def body(i):
                ch.begin(i)
                acc = d.group(d.acc, i)
                v.nop(nofuse=True)
                ch.link(v.tensor_copy(rden[:], acc[:, :, :, C]))
                ch.link(v.reciprocal(rden[:], rden[:]))
                ch.link(v.tensor_tensor(o[:].rearrange("p g (h c) -> p g h c", h=H), acc[:, :, :, 0:C],
                                        bcast(rden[:], [P, G, H, C], 3), ALU.mult))
                ch.link(v.tensor_tensor(o2[:], o[:], bcast(b2[:], [P, G, P], 1), ALU.add))
                ch.link(v.tensor_tensor(x2[:], d.group(T.xs, i), o2[:], ALU.add))
                v.tensor_scalar(d.group(T.xs, i), x2[:], 1.0, None, ALU.mult)
                reuse(v, s("hT_ps"), i)
                reuse(v, s("hs"), i)
                d.norm_vector(v, ch, i, x2[:], h[:], "ln").then_inc(s("h"), 1)
                v.wait_ge(s("ex"), i + 1)
                ch.link(v.tensor_scalar(sig[:], ex[:], 1.0, None, ALU.add))
                ch.link(v.reciprocal(sig[:], sig[:]))
                reuse(v, s("both_ps"), i)
                ch.link(v.tensor_tensor(feat[:, :, 0, :], sig[:], hT[:], ALU.mult))
                for j in range(G):
                    xb = bcast(hT[:, j, :], [P, KNOTS, P], 1)
                    kb = bcast(knots[:], [P, KNOTS, P], 2)
                    v.tensor_tensor(dist[:], xb, kb, ALU.subtract)
                    ch.link(v.tensor_tensor(ge[:], xb, kb, ALU.is_ge))
                    m = KNOTS - 1
                    ch.link(v.tensor_tensor(bs[:, 0:m, :], ge[:, 0:m, :], ge[:, 1:KNOTS, :], ALU.subtract))
                    for r in (1, 2, 3):
                        m -= 1
                        v.tensor_tensor(left[:, 0:m, :], dist[:, 0:m, :], bs[:, 0:m, :], ALU.mult)
                        ch.link(v.tensor_tensor(right[:, 0:m, :], dist[:, r + 1:r + 1 + m, :], bs[:, 1:m + 1, :], ALU.mult))
                        if r < 3:
                            ch.link(v.tensor_tensor(bs[:, 0:m, :], left[:, 0:m, :], right[:, 0:m, :], ALU.subtract))
                    if j or not isinstance(i, int):
                        v.wait_ge(s("scaled"), i * G + j)
                    v.tensor_tensor(cubic[:], left[:, 0:m, :], right[:, 0:m, :], ALU.subtract).then_inc(s("cubic"), 1)
            loop(v, NG, body)

        @block.tensor
        def _(pe):
            pe.wait_ge(s("weights_in"), 32)

            def body(i):
                pe.wait_ge(s("h"), i + 1)
                reuse(pe, s("hT"), i)
                for j in range(G):
                    last = pe.transpose(d.hT_slot(j), h[:, j, :], T.ident[:])
                last.then_inc(s("hT_ps"), 1)
                reuse(pe, s("both"), i)
                for j in range(G):
                    pe.wait_ge(s("scaled"), i * G + j + 1)
                    for f in range(1 + BASES):
                        last = pe.matmul(pt[:, j, 0:2 * P], feat[:, j, f, :], w[:, f, :], start=(f == 0), stop=(f == BASES))
                last.then_inc(s("both_ps"), 1)
            loop(pe, NG, body)

        @block.scalar
        def _(a):
            def body(i):
                d.norm_scalar(a, i, "ln")
                a.wait_ge(s("h"), i + 1)
                a.copy(d.group(T.hs, i), h[:]).then_inc(s("hs"), 1)
                a.wait_ge(s("hT_ps"), i + 1)
                reuse(a, s("cubic"), i, G)
                a.copy(hT[:, 0:4, :], pt[:, 5, :].rearrange("p (g n) -> p g n", g=4))
                a.copy(hT[:, 4, :], pt[:, 6, 0:P]).then_inc(s("hT"), 1)
                a.wait_ge(s("hT"), i + 1)
                a.activation(ex[:], hT[:], ACT.Exp, scale=-1.0).then_inc(s("ex"), 1)
                for j in range(G):
                    a.wait_ge(s("cubic"), i * G + j + 1)
                    a.mul(feat[:, j, 1:1 + BASES, :], cubic[:], 1.0 / (6.0 * STEP ** 3)).then_inc(s("scaled"), 1)
                a.wait_ge(s("both_ps"), i + 1)
                reuse(a, s("both_out"), i, 32)
                a.copy(both[:], pt[:, 0:G, 0:2 * P]).then_inc(s("both"), 1)
            loop(a, NG, body)
    d.ph.close()


def node_after_kan(c, T, W, table, node_table):
    H, C = 4, 32
    d = Dense(c, T, "kan_out", H, C)
    s, pt = d.s, d.pt
    w = d.sb("w", [P, 3 * P])
    bias = d.sb("bias", [P, P])
    slope = d.sb("slope", [P, 1])
    den = d.sb("den", [P, G, H])
    rden = d.sb("rden", [P, G, H])
    o = d.sb("o", [P, G, P])
    o2 = d.sb("o2", [P, G, P])
    o3 = d.sb("o3", [P, G, P])
    x3 = d.sb("x3", [P, G, P])
    h = d.sb("h", [P, G, P])
    hT = d.sb("hT", [P, G, P])
    qvk = d.sb("qvk", [P, G, 3 * P])
    with c.nc.Block() as block:
        @block.sync
        def _(sp):
            sp.dma_start(w[:], W["L3_w"]).then_inc(s("weights_in"), 16)
            sp.dma_start(bias[:], W["L2_bias"].partition_broadcast(P)).then_inc(s("weights_in"), 16)
            sp.dma_start(slope[:], W["L2_prelu_a"].partition_broadcast(P)).then_inc(s("weights_in"), 16)

            def body(i):
                sp.wait_ge(s("qvk"), i + 1)
                sp.dma_start(rows_of(table, i), qvk[:, :, 0:2 * P]).then_inc(s("qvk_out"), 16)
                sp.dma_start(rows_of(node_table, i), qvk[:, :, 2 * P:3 * P]).then_inc(s("qvk_out"), 16)
            loop(sp, NG, body)
            sp.wait_ge(s("qvk_out"), 32 * NG)

        @block.vector
        def _(v):
            ch = Chain(v, s("dve"))
            v.wait_ge(s("weights_in"), 48)

            def body(i):
                ch.begin(i)
                acc = d.group(d.acc, i)
                ch.link(v.tensor_scalar(den[:], acc[:, :, :, C], 1e-16, None, ALU.add))
                ch.link(v.reciprocal(rden[:], den[:]))
                ch.link(v.tensor_tensor(o[:].rearrange("p g (h c) -> p g h c", h=H), acc[:, :, :, 0:C],
                                        bcast(rden[:], [P, G, H, C], 3), ALU.mult))
                ch.link(v.tensor_tensor(o2[:], o[:], d.group(T.hs, i), ALU.add))
                ch.link(v.tensor_tensor(o3[:], o2[:], bcast(bias[:], [P, G, P], 1), ALU.add))
                v.tensor_scalar(o[:], o3[:], 0.0, slope[:], ALU.min, ALU.mult)
                ch.link(v.tensor_scalar(o2[:], o3[:], 0.0, None, ALU.max))
                ch.link(v.tensor_tensor(o3[:], o[:], o2[:], ALU.add))
                ch.link(v.tensor_tensor(x3[:], d.group(T.xs, i), o3[:], ALU.add))
                v.tensor_scalar(d.group(T.xs, i), x3[:], 1.0, None, ALU.mult)
                reuse(v, s("hT_ps"), i)
                d.norm_vector(v, ch, i, x3[:], h[:], "ln").then_inc(s("h"), 1)
            loop(v, NG, body)

        @block.tensor
        def _(pe):
            pe.wait_ge(s("weights_in"), 48)

            def body(i):
                pe.wait_ge(s("h"), i + 1)
                reuse(pe, s("qvk"), i)
                for j in range(G):
                    last = pe.transpose(pt[:, j, 3 * P:4 * P], h[:, j, :], T.ident[:])
                last.then_inc(s("hT_ps"), 1)
                pe.wait_ge(s("hT"), i + 1)
                for j in range(G):
                    last = pe.matmul(pt[:, j, 0:3 * P], hT[:, j, :], w[:], start=True, stop=True)
                last.then_inc(s("qvk_ps"), 1)
            loop(pe, NG, body)

        @block.scalar
        def _(a):
            def body(i):
                d.norm_scalar(a, i, "ln")
                a.wait_ge(s("hT_ps"), i + 1)
                a.copy(hT[:], pt[:, 0:G, 3 * P:4 * P]).then_inc(s("hT"), 1)
                a.wait_ge(s("qvk_ps"), i + 1)
                reuse(a, s("qvk_out"), i, 32)
                a.copy(qvk[:], pt[:, 0:G, 0:3 * P]).then_inc(s("qvk"), 1)
            loop(a, NG, body)
    d.ph.close()


def node_out(c, T, out):
    H, C = 4, 32
    F = H * (C + 1)
    ph = Phase(c, "out")
    s = ph.sem
    den = ph.sb("den", [P, NB, H])
    rden = ph.sb("rden", [P, NB, H])
    o = ph.sb("o", [P, NB, P])
    res = ph.sb("res", [P, NB, P])
    acc = T.acc[:, 0:NB * F].rearrange("p (b h c) -> p b h c", h=H, c=C + 1)
    with c.nc.Block() as block:
        @block.vector
        def _(v):
            ch = Chain(v, s("dve"))
            ch.begin(0)
            ch.link(v.tensor_scalar(den[:], acc[:, :, :, C], 1e-9, None, ALU.max))
            ch.link(v.reciprocal(rden[:], den[:]))
            ch.link(v.tensor_tensor(o[:].rearrange("p b (h c) -> p b h c", h=H), acc[:, :, :, 0:C],
                                    bcast(rden[:], [P, NB, H, C], 3), ALU.mult))
            v.tensor_tensor(res[:], T.xs[:], o[:], ALU.add).then_inc(s("res"), 1)

        @block.sync
        def _(sp):
            sp.wait_ge(s("res"), 1)
            sp.dma_start(out[0:(NB - 1) * P, :].rearrange("(b p) f -> p b f", p=P), res[:, 0:NB - 1, :]
                         ).then_inc(s("stored"), 16)
            sp.dma_start(out[(NB - 1) * P:N, :], res[0:N - (NB - 1) * P, NB - 1, :]).then_inc(s("stored"), 16)
            sp.wait_ge(s("stored"), 32)
    ph.close()


def load_vec(c, T, name, dst, src):
    ph = Phase(c, name)
    s = ph.sem
    with c.nc.Block() as block:
        @block.sync
        def _(sp):
            sp.dma_start(dst[:], src.partition_broadcast(P)).then_inc(s("in"), 16)
            sp.wait_ge(s("in"), 16)
    ph.close()


class Tables:
    pass


def build(nc, A, out):
    c = Ctx(nc)
    T = Tables()
    T.ident = c.sb("ident", [P, P])
    T.ones = c.sb("ones", [1, P])
    T.iota256 = c.sb("iota256", [P, 2 * P])
    T.shift = c.sb("shift", [RT, RT])
    T.xs = c.sb("xs", [P, NB, P])
    T.hs = c.sb("hs", [P, NB, P])
    T.ixs = c.sb("ixs", [P, RT, ROW_IX], I32)
    T.mask = c.sb("mask", [P, RT * SLOTS])
    T.rel = c.sb("rel", [P, RT])
    T.blk = c.sb("blk", [1, RT], I32)
    T.pen = c.sb("pen", [RT, P])
    T.pen_b = c.sb("pen_b", [RT, P])
    T.pen_pre = c.sb("pen_pre", [RT, P])
    T.pen_suf = c.sb("pen_suf", [RT, P])
    T.pen_tile = c.sb("pen_tile", [4, RT])
    T.pen_tile_b = c.sb("pen_tile_b", [4, RT])
    T.m = c.sb("m", [P, RT * 4])
    T.factor = c.sb("factor", [P, RT * 4])
    att = c.sb("att", [P, P])
    small_stack = c.keep
    prepare(c, T, A["x"], A["chunk_ix"], A["dst_rows"])
    T.acc = c.sb("acc", [P, (NB + 1) * 322])

    tab = {w: c.dram(f"tab{w}", [NP_, w]) for w in (128, 136, 256, 264)}
    node = {w: c.dram(f"node{w}", [NP_, w]) for w in (128, 322)}
    part = {f: c.dram(f"part{f}", [ROWS, f]) for f in (132, 260, 322)}

    def message_pass(name, H, C, src_w, node_w, kind, **kw):
        F = H * (C + 1)
        edge_pass(c, T, name, H, C, src_w, node_w, tab[src_w], node.get(node_w), part[F], kind, **kw)
        if kind == "gatv2":
            global_maximum(c, T, name + "_max", H)
        else:
            node_maxima(c, T, name + "_max", H)
        merge_rows(c, T, name + "_merge", H, C, part[F])

    node_in(c, T, A, tab[128], node[322])
    message_pass("conv", 2, 160, 128, 322, "conv", chunk_attr=A["chunk_attr"])
    node_after_conv(c, T, A, tab[264])
    message_pass("gat0", 4, 64, 264, 0, "gat")
    node_between_gats(c, T, A, "mid0", "L1_b0", "L1_W1", "L1_as1", "L1_ad1", 256, tab[264])
    message_pass("gat1", 4, 64, 264, 0, "gat")
    node_between_gats(c, T, A, "mid1", "L1_b1", "L1_W2", "L1_as2", "L1_ad2", 128, tab[136])
    message_pass("gat2", 4, 32, 136, 0, "gat")
    node_kan(c, T, A, tab[128], node[128])
    load_vec(c, T, "att_in", att, A["L2_double_attn"])
    message_pass("gatv2", 4, 32, 128, 128, "gatv2", vec=att)
    node_after_kan(c, T, A, tab[256], node[128])
    message_pass("dot", 4, 32, 256, 128, "dot")
    node_out(c, T, out)
    c.keep.close()


def arrange(inputs):
    a = {k: np.ascontiguousarray(v) for k, v in inputs.items()}
    src, dst = a["src"], a["dst"]
    src_c = np.zeros((CHUNKS * K,), src.dtype)
    src_c[:E] = src
    dst_c = np.full((CHUNKS * K,), NO_NODE, dst.dtype)
    dst_c[:E] = dst
    dst_r = np.full((EROWS * P,), NO_NODE, dst.dtype)
    dst_r[:E] = dst
    ea = np.zeros((CHUNKS * K, 32), a["edge_attr_32"].dtype)
    ea[:E] = a["edge_attr_32"]
    heads2 = lambda w: w.reshape(2, P, -1).transpose(1, 0, 2)
    out = {"x": a["x"],
           "chunk_ix": np.concatenate([src_c.reshape(CHUNKS, K), dst_c.reshape(CHUNKS, K)], axis=1),
           "dst_rows": dst_r.reshape(EROWS, P),
           "chunk_attr": ea.reshape(CHUNKS, K * 32),
           "L0_WqT": a["L0_gnn_Wq"].T, "L0_bq": a["L0_gnn_bq"].reshape(2, P).T,
           "L0_kx": np.concatenate([heads2(a["L0_gnn_Wk"]), heads2(a["L0_gnn_We"]),
                                    heads2(a["L0_gnn_bk"].reshape(-1, 1))], axis=2),
           "L0_WvT": a["L0_gnn_Wv"].T,
           "L0_web": np.concatenate([a["L0_gnn_We"].T.reshape(32, 2, P), a["L0_gnn_bv"].reshape(1, 2, P)], axis=0),
           "L0_WskipT": a["L0_gnn_Wskip"].T, "L0_bskip": a["L0_gnn_bskip"].reshape(1, P),
           "L0_W1T": a["L0_gnn_W1"].T, "L0_b1": a["L0_gnn_b1"].reshape(2, P).T,
           "L0_W2T": a["L0_gnn_W2"].T.reshape(2, P, P).transpose(1, 0, 2), "L0_b2": a["L0_gnn_b2"].reshape(1, P),
           "L0_ln1_g": a["L0_gnn_ln1_g"], "L0_ln1_b": a["L0_gnn_ln1_b"],
           "L0_ln2_g": a["L0_gnn_ln2_g"], "L0_ln2_b": a["L0_gnn_ln2_b"],
           "L1_W0": a["L1_gnn_W0"], "L1_as0": a["L1_gnn_as0"].reshape(-1), "L1_ad0": a["L1_gnn_ad0"].reshape(-1),
           "L1_b0": a["L1_gnn_b0"],
           "L1_W1": a["L1_gnn_W1"].reshape(2, P, 256).transpose(1, 0, 2),
           "L1_as1": a["L1_gnn_as1"].reshape(-1), "L1_ad1": a["L1_gnn_ad1"].reshape(-1), "L1_b1": a["L1_gnn_b1"],
           "L1_W2": a["L1_gnn_W2"].reshape(2, P, P).transpose(1, 0, 2),
           "L1_as2": a["L1_gnn_as2"].reshape(-1), "L1_ad2": a["L1_gnn_ad2"].reshape(-1), "L1_b2": a["L1_gnn_b2"],
           "L2_double_attn": a["L2_gnn_double_attn"].reshape(-1), "L2_bias": a["L2_gnn_bias"],
           "L2_prelu_a": a["L2_gnn_prelu_a"].reshape(1),
           "L3_w": np.concatenate([a[f"L3_gnn_{n}"].transpose(1, 0, 2).reshape(P, P) for n in ("Wq", "Wv", "Wk")], axis=1)}
    kan = []
    for side in ("src", "dst"):
        sw = a[f"L2_gnn_spline_w_{side}"].transpose(1, 2, 0)[:, KNOT0:KNOT0 + BASES, :]
        kan.append(np.concatenate([a[f"L2_gnn_base_w_{side}"].T[:, None, :], sw], axis=1))
    out["L2_w"] = np.concatenate(kan, axis=2)
    return {k: np.ascontiguousarray(v) for k, v in out.items()}


def kernel(**inputs):
    import concourse.bacc as bacc
    from concourse.bass_utils import run_bass_kernel_spmd as run

    nc = bacc.Bacc("TRN2", target_bir_lowering=False, num_devices=1)
    arrays = {f"in_{k}": v for k, v in arrange(inputs).items()}
    A = {k[3:]: nc.dram_tensor(k, v.shape, mybir.dt.from_np(v.dtype), kind="ExternalInput").ap()
         for k, v in arrays.items()}
    out = nc.dram_tensor("out_x", (N, P), F32, kind="ExternalOutput").ap()
    build(nc, A, out)
    return run(nc, [arrays], core_ids=[0]).results[0]["out_x"]
```

```python
from contextlib import ExitStack

import numpy as np
import concourse.bass as bass
from concourse import mybir

F32 = mybir.dt.float32
I32 = mybir.dt.int32
ALU = mybir.AluOpType
ACT = mybir.ActivationFunctionType
X = mybir.AxisListType.X

P = 128
N = 3125
E = 103125
K = 8
CHUNKS = -(-E // K)
SLOTS = K + 1
EROWS = -(-E // P)
NB = -(-N // P)
NP_ = NB * P
RT = -(-(CHUNKS + N - 1) // P)
ROWS = RT * P
NO_NODE = 8191
G = 5
NG = NB // G
NEG = -1e30
LOW = -1e38
NEG_SLOPE = 0.2
ROW_IX = K + 2
UC = 6
U = 3
CT = 21
NCH = RT // CT
S = CT // U
assert RT % CT == 0 and CT % U == 0 and U == 3
assert RT % UC == 0 and NB % G == 0 and RT % U == 0


class Ctx:

    def __init__(self, nc):
        self.nc = nc
        self.keep = ExitStack()
        self.gather_sems = {n: self.keep.enter_context(nc.semaphore(n)) for n in
                            ["dsts_in", "marked"] + [f"got{b}" for b in range(UC)] + [f"gathered{b}" for b in range(U)]}

    def sb(self, name, shape, dt=F32, stack=None):
        return (stack or self.keep).enter_context(self.nc.sbuf_tensor(name, shape, dt))

    def dram(self, name, shape, dt=F32):
        return self.nc.dram_tensor(name, shape, dt, kind="Internal").ap()


class Phase:

    def __init__(self, c, name):
        self.c, self.nc, self.name = c, c.nc, name
        self.stack = ExitStack()
        self.sems = {}

    def sem(self, name):
        if name in self.c.gather_sems:
            self.sems[name] = self.c.gather_sems[name]
        if name not in self.sems:
            self.sems[name] = self.stack.enter_context(self.nc.semaphore(f"{self.name}_{name}"))
        return self.sems[name]

    def sb(self, name, shape, dt=F32):
        return self.stack.enter_context(self.nc.sbuf_tensor(f"{self.name}_{name}", shape, dt))

    def ps(self, name, shape, dt=F32):
        return self.stack.enter_context(self.nc.psum_tensor(f"{self.name}_{name}", shape, dt))

    def close(self):
        used = [s for n, s in self.sems.items() if n in self.c.gather_sems]
        if used:
            self.nc.gpsimd.dma_reset(range(min(x.num for x in used), max(x.num for x in used) + 1))
        for sem in self.sems.values():
            self.nc.gpsimd.sem_clear(sem)
        self.nc.all_engine_barrier()
        self.stack.close()


class Chain:

    def __init__(self, eng, sem, steps=None):
        self.eng, self.sem, self.steps, self.k, self.base, self.first = eng, sem, steps, 0, 0, steps is None
        self.fixed = steps is not None

    def begin(self, i):
        if self.fixed:
            assert self.k in (0, self.steps), self.k
            self.base = i * self.steps
        elif isinstance(i, int):
            self.base, self.first = 0, True
        else:
            if self.first:
                self.steps = self.k
            self.base, self.first = i * self.steps, False
        self.k = 0

    def link(self, ins):
        self.k += 1
        ins.then_inc(self.sem, 1)
        self.eng.wait_ge(self.sem, self.base + self.k)


def loop(eng, n, body):
    body(0)
    if n > 1:
        with eng.Fori(1, n) as i:
            body(i)


def reuse(eng, sem, i, per_step=1):
    if not isinstance(i, int):
        eng.wait_ge(sem, i * per_step)


def bcast(ap, shape, axis):
    return ap.unsqueeze(axis).to_broadcast(shape)


def prepare(c, T, x_in, chunk_ix, dst_rows):
    nc = c.nc
    ph = Phase(c, "prep")
    s = ph.sem
    i_col = ph.sb("i_col", [P, NB], I32)
    i_256 = ph.sb("i_256", [P, 2 * P], I32)
    i_row = ph.sb("i_row", [RT, P], I32)
    nid = ph.sb("nid", [P, NB])
    rowid = ph.sb("rowid", [RT, P])
    heads_i = ph.sb("heads_i", [P, EROWS], I32)
    heads = ph.sb("heads", [P, EROWS])
    junk = ph.sb("junk", [P, EROWS])
    before = ph.sb("before", [P, NB])
    tile_f = ph.sb("tile_f", [P, NB])
    tile_i = ph.sb("tile_i", [P, NB], I32)
    dsts = ph.sb("dsts", [P, NB, P], I32)
    less = ph.sb("less", [P, NB, P])
    inside = ph.sb("inside", [P, NB])
    start = ph.sb("start", [P, NB])
    startT = ph.sb("startT", [NB, P])
    nextT = ph.sb("nextT", [NB, P])
    fullE = ph.sb("fullE", [1, P])
    zeros = ph.sb("zeros", [P, 2 * P])
    qi = ph.sb("qi", [NB, 2, P], I32)
    q = ph.sb("q", [NB, 2, P])
    rc = ph.sb("rc", [NB, P])
    onesT = ph.sb("onesT", [RT, P])
    rp = ph.sb("rp", [NB, P])
    last_rp = ph.sb("last_rp", [NB, 1])
    upper = ph.sb("upper", [NB, NB])
    carry = ph.sb("carry", [NB, 1])
    first_row = ph.sb("first_row", [NB, P])
    offT = ph.sb("offT", [NB, P])
    rp_i = ph.sb("rp_i", [P, NB], I32)
    mark = ph.sb("mark", [P, NB, 2])
    marks = ph.sb("marks", [RT, P, 2])
    run = ph.sb("run", [RT, 2, P])
    lastT = ph.sb("lastT", [2, RT])
    runT = ph.sb("runT", [2, RT + 1])
    rc_sb = ph.sb("rc_sb", [RT, 2])
    both = ph.sb("both", [RT, 2, P])
    chunk = ph.sb("chunk", [RT, P])
    new = ph.sb("new", [RT, P])
    blk_i = ph.sb("blk_i", [RT, 1], I32)
    nfirst_i = ph.sb("nfirst_i", [RT, 1], I32)
    blk = ph.sb("blk", [RT, 1])
    blk128 = ph.sb("blk128", [RT, 1])
    relT = ph.sb("relT", [RT, P])
    later = ph.sb("later", [RT, P])
    n_col = ph.sb("n_col", [P, RT])
    shift = ph.sb("shift", [RT, RT])
    pen, pen_b, pen_pre, pen_suf = [ph.sb(n, [RT, P]) for n in ("pen", "pen_b", "pen_pre", "pen_suf")]
    pen_r = ph.sb("pen_r", [RT, P])
    d_pen = c.dram("d_pen", [4, RT, P])
    stage = ph.sb("stage", [P, UC, 1], I32)
    got = ph.sb("got", [P, UC, 2 * K], I32)
    differs = ph.sb("differs", [P, UC, K])
    pt = ph.ps("pt", [P, 8, 512])
    d_heads = c.dram("d_heads", [EROWS], I32)
    d_start = c.dram("d_start", [NP_ + P])
    d_mark = c.dram("d_mark", [ROWS, 2])

    with nc.Block() as block:
        @block.gpsimd
        def _(g):
            g.iota(i_col[:], [[P, NB]], base=0, channel_multiplier=1).then_inc(s("iotas"), 1)
            g.iota(i_256[:], [[1, 2 * P]], base=0, channel_multiplier=0).then_inc(s("iotas"), 1)
            g.iota(i_row[:], [[1, P]], base=0, channel_multiplier=P).then_inc(s("iotas"), 1)
            g.memset(T.ident[:], 0.0).then_inc(s("blank"), 1)
            g.memset(upper[:], 1.0).then_inc(s("blank"), 1)
            g.wait_ge(s("blank"), 2)
            g.affine_select(out=T.ident[:], in_=T.ident[:], compare_op=ALU.not_equal, fill=1.0, base=0,
                            pattern=[[-1, P]], channel_multiplier=1).then_inc(s("masks"), 1)
            g.affine_select(out=upper[:], in_=upper[:], compare_op=ALU.is_gt, fill=0.0, base=0,
                            pattern=[[1, NB]], channel_multiplier=-1).then_inc(s("masks"), 1)
            g.wait_ge(s("tile_ready"), 1)
            for b in range(NB):
                g.indirect_dma_start(out=dsts[:, b, :], out_offset=None, in_=dst_rows[:, :],
                                     in_offset=bass.IndirectOffsetOnAxis(ap=tile_i[:, b:b + 1], axis=0)
                                     ).then_inc(s("dsts_in"), 16)
            g.wait_ge(s("marks_blank"), 16)
            g.wait_ge(s("marks_ready"), 2)
            for b in range(NB):
                g.indirect_dma_start(out=d_mark[:, :], in_=mark[:, b, :], in_offset=None,
                                     out_offset=bass.IndirectOffsetOnAxis(ap=rp_i[:, b:b + 1], axis=0)
                                     ).then_inc(s("marked"), 16)

            def chunks(i):
                for b in range(UC):
                    reuse(g, s(f"diff{b}"), i)
                    reuse(g, s(f"kept{b}"), i)
                    g.wait_ge(s(f"stage_ready{b}"), i + 1)
                    g.nop(nofuse=True)
                    g.indirect_dma_start(out=got[:, b, :], out_offset=None, in_=chunk_ix[:, :],
                                         in_offset=bass.IndirectOffsetOnAxis(ap=stage[:, b, :], axis=0)
                                         ).then_inc(s(f"got{b}"), 16)
            loop(g, RT // UC, chunks)

        @block.sync
        def _(sp):
            sp.dma_start(d_heads.unsqueeze(1), dst_rows[:, 0:1], allow_slow_non_contiguous=True).then_inc(s("heads_out"), 16)
            sp.wait_ge(s("heads_out"), 16)
            sp.dma_start(heads_i[:], d_heads.partition_broadcast(P)).then_inc(s("heads_in"), 16)
            sp.wait_ge(s("x_pad"), 1)
            sp.dma_start(T.xs[:, 0:NB - 1, :],
                         x_in[0:(NB - 1) * P, :].rearrange("(b p) f -> p b f", p=P)).then_inc(s("x_in"), 16)
            sp.dma_start(T.xs[0:N - (NB - 1) * P, NB - 1, :], x_in[(NB - 1) * P:N, :]).then_inc(s("x_in"), 16)
            sp.wait_ge(s("zeros"), 1)
            sp.dma_start(d_mark.rearrange("(t p) o -> t (p o)", p=P), zeros[0:RT, :]).then_inc(s("marks_blank"), 16)
            sp.wait_ge(s("startT"), 1)
            sp.dma_start(d_start[0:NP_].rearrange("(b p) -> b p", p=P), startT[:]).then_inc(s("start_out"), 16)
            sp.dma_start(d_start[NP_:NP_ + P].unsqueeze(0), fullE[:]).then_inc(s("start_out"), 16)
            sp.wait_ge(s("start_out"), 32)
            sp.dma_start(nextT[:], d_start[1:NP_ + 1].rearrange("(b p) -> b p", p=P)).then_inc(s("next_in"), 16)
            sp.wait_ge(s("marked"), NB * 16)
            sp.dma_start(marks[:], d_mark.rearrange("(t p) o -> t p o", p=P)).then_inc(s("marks_in"), 16)
            sp.wait_ge(s("x_in"), 32)
            sp.wait_ge(s("pens2"), 1)
            for m, own in enumerate((pen, pen_r, pen_pre, pen_suf)):
                sp.dma_start(d_pen[m], own[:]).then_inc(s("pen_out"), 16)
            sp.wait_ge(s("pen_out"), 64)
            for m, kept in enumerate((T.pen, T.pen_b, T.pen_pre, T.pen_suf)):
                sp.dma_start(kept[:].rearrange("t (c p) -> t c p", p=P), d_pen[m].rearrange("(c t) p -> t c p", t=CT)
                             ).then_inc(s("pen_in"), 16)
            sp.wait_ge(s("pen_in"), 64)

        @block.tensor
        def _(pe):
            pe.wait_ge(s("masks"), 2)
            pe.wait_ge(s("start"), 1)
            pe.transpose(pt[0:NB, 0, 0:P], start[:], T.ident[:]).then_inc(s("startT_ps"), 1)
            pe.wait_ge(s("rows_summed"), 1)
            pe.matmul(pt[0:NB, 1, 0:1], upper[:], last_rp[:], start=True, stop=True).then_inc(s("carry_ps"), 1)
            pe.wait_ge(s("first_row"), 2)
            pe.transpose(pt[:, 2, 0:NB], first_row[:], T.ident[0:NB, 0:NB]).then_inc(s("first_ps"), 1)
            pe.transpose(pt[:, 3, 0:NB], offT[:], T.ident[0:NB, 0:NB]).then_inc(s("first_ps"), 1)
            pe.wait_ge(s("run"), 2)
            pe.transpose(pt[0:2, 4, 0:RT], rc_sb[:], T.ident[0:RT, 0:RT]).then_inc(s("lastT_ps"), 1)
            pe.wait_ge(s("runT"), 1)
            pe.transpose(pt[0:RT, 5, 0:2], runT[:, 0:RT], T.ident[0:2, 0:2]).then_inc(s("carry2_ps"), 1)
            pe.wait_ge(s("row_cols"), 1)
            pe.transpose(pt[:, 0, 0:RT], both[:, 0, :], T.ident[0:RT, 0:RT]).then_inc(s("cols_ps"), 1)
            pe.transpose(pt[:, 1, 0:RT], chunk[:], T.ident[0:RT, 0:RT]).then_inc(s("cols_ps"), 1)
            pe.transpose(pt[:, 2, 0:RT], relT[:], T.ident[0:RT, 0:RT]).then_inc(s("cols_ps"), 1)
            pe.transpose(pt[0:1, 3, 0:RT], blk[:], T.ident[0:RT, 0:RT]).then_inc(s("cols_ps"), 1)
            pe.wait_ge(s("pens"), 1)
            pe.transpose(pt[:, 4, P:P + RT], later[:], T.ident[0:RT, 0:RT]).then_inc(s("pen_ps"), 1)
            pe.matmul(pt[0:RT, 5, 0:1], shift[:], pen[:, 0:1], start=True, stop=True).then_inc(s("pen_ps"), 1)
            pe.wait_ge(s("pens2"), 1)
            pe.matmul(pt[0:4, 6, 0:RT], pen_pre[:, P - 1:P].to_broadcast([RT, 4]), T.ident[0:RT, 0:RT],
                      start=True, stop=True).then_inc(s("pen2_ps"), 1)
            pe.matmul(pt[0:4, 7, 0:RT], pen_suf[:, 0:1].to_broadcast([RT, 4]), T.ident[0:RT, 0:RT],
                      start=True, stop=True).then_inc(s("pen2_ps"), 1)

        @block.vector
        def _(v):
            ch = Chain(v, s("dve"))
            ch.begin(0)
            v.memset(T.xs[:, NB - 1, :], 0.0).then_inc(s("x_pad"), 1)
            v.memset(zeros[:], 0.0).then_inc(s("zeros"), 1)
            v.memset(T.ones[:], 1.0)
            v.memset(fullE[:], float(E))
            v.memset(runT[:, 0:1], 0.0)
            ch.link(v.memset(onesT[:], 1.0))
            v.wait_ge(s("iotas"), 3)
            v.tensor_copy(nid[:], i_col[:])
            v.tensor_copy(T.iota256[:], i_256[:])
            v.tensor_copy(T.pid[:], i_col[:, 0:1])
            v.tensor_copy(rowid[:], i_row[:])
            v.wait_ge(s("masks"), 2)
            v.memset(shift[:], 0.0)
            v.wait_ge(s("heads_in"), 16)
            ch.link(v.tensor_copy(heads[:], heads_i[:]))
            v.tensor_copy(shift[:, 0:RT - 1], T.ident[0:RT, 1:RT])
            for b in range(NB):
                ch.link(v.tensor_scalar(junk[:], heads[:], nid[:, b:b + 1], 0.0, ALU.is_lt, ALU.add,
                                        accum_out=before[:, b:b + 1]))
            ch.link(v.tensor_scalar(tile_f[:], before[:], -1.0, 0.0, ALU.add, ALU.max))
            v.tensor_copy(tile_i[:], tile_f[:]).then_inc(s("tile_ready"), 1)
            v.wait_ge(s("dsts_in"), NB * 16)
            ch.link(v.tensor_tensor(less[:], dsts[:], bcast(nid[:], [P, NB, P], 2), ALU.is_lt))
            ch.link(v.tensor_reduce(inside[:], less[:], X, ALU.add))
            v.scalar_tensor_tensor(start[:], tile_f[:], float(P), inside[:], ALU.mult, ALU.add
                                   ).then_inc(s("start"), 1)
            v.wait_ge(s("startT_ps"), 1)
            v.tensor_copy(startT[:], pt[0:NB, 0, 0:P]).then_inc(s("startT"), 1)
            v.wait_ge(s("next_in"), 16)
            v.wait_ge(s("startT"), 1)
            v.tensor_copy(qi[:, 0, :], startT[:])
            ch.link(v.tensor_scalar(q[:, 1, :], nextT[:], -1.0, None, ALU.add))
            ch.link(v.tensor_copy(qi[:, 1, :], q[:, 1, :]))
            ch.link(v.tensor_single_scalar(qi[:], qi[:], K.bit_length() - 1, ALU.arith_shift_right))
            ch.link(v.tensor_copy(q[:], qi[:]))
            ch.link(v.tensor_tensor(rc[:], q[:, 1, :], q[:, 0, :], ALU.subtract))
            ch.link(v.tensor_scalar(rc[:], rc[:], 1.0, None, ALU.add))
            ch.link(v.tensor_tensor_scan(rp[:], onesT[0:NB, :], rc[:], 0.0, ALU.mult, ALU.add))
            v.tensor_copy(last_rp[:], rp[:, P - 1:P]).then_inc(s("rows_summed"), 1)
            ch.link(v.tensor_tensor(first_row[:], rp[:], rc[:], ALU.subtract))
            v.wait_ge(s("carry_ps"), 1)
            ch.link(v.tensor_copy(carry[:], pt[0:NB, 1, 0:1]))
            v.tensor_scalar(first_row[:], first_row[:], carry[:], None, ALU.add).then_inc(s("first_row"), 1)
            v.wait_ge(s("first_row"), 1)
            v.tensor_tensor(offT[:], first_row[:], q[:, 0, :], ALU.subtract).then_inc(s("first_row"), 1)
            v.wait_ge(s("first_ps"), 2)
            v.tensor_copy(rp_i[:], pt[:, 2, 0:NB]).then_inc(s("marks_ready"), 1)
            v.tensor_copy(mark[:, :, 0], nid[:])
            v.tensor_copy(mark[:, :, 1], pt[:, 3, 0:NB]).then_inc(s("marks_ready"), 1)
            v.wait_ge(s("marks_in"), 16)
            for m in range(2):
                ch.link(v.tensor_tensor_scan(run[:, m, :], marks[:, :, m], marks[:, :, m], 0.0, ALU.max, ALU.max))
            v.tensor_copy(rc_sb[:], run[:, :, P - 1]).then_inc(s("run"), 2)
            v.wait_ge(s("lastT_ps"), 1)
            ch.link(v.tensor_copy(lastT[:], pt[0:2, 4, 0:RT]))
            v.tensor_tensor_scan(runT[:, 1:RT + 1], lastT[:], lastT[:], 0.0, ALU.max, ALU.max
                                 ).then_inc(s("runT"), 1)
            v.wait_ge(s("carry2_ps"), 1)
            v.wait_ge(s("run"), 2)
            ch.link(v.tensor_copy(rc_sb[:], pt[0:RT, 5, 0:2]))
            for m in range(2):
                ch.link(v.tensor_scalar(both[:, m, :], run[:, m, :], rc_sb[:, m:m + 1], None, ALU.max))
            ch.link(v.tensor_tensor(chunk[:], rowid[:], both[:, 1, :], ALU.subtract))
            v.tensor_scalar(chunk[:], chunk[:], float(CHUNKS - 1), 0.0, ALU.min, ALU.max)
            v.tensor_tensor(new[:, 1:P], both[:, 0, 1:P], both[:, 0, 0:P - 1], ALU.not_equal)
            v.tensor_scalar(new[:, 0:1], both[:, 0, 0:1], rc_sb[:, 0:1], None, ALU.not_equal)
            ch.link(v.tensor_copy(nfirst_i[:], both[:, 0, 0:1]))
            ch.link(v.tensor_single_scalar(blk_i[:], nfirst_i[:], 7, ALU.arith_shift_right))
            ch.link(v.tensor_copy(blk[:], blk_i[:]))
            ch.link(v.tensor_scalar(blk128[:], blk[:], float(P), None, ALU.mult))
            v.tensor_scalar(relT[:], both[:, 0, :], blk128[:], None, ALU.subtract).then_inc(s("row_cols"), 1)
            ch.link(v.memset(new[0:1, 0:1], 1.0))
            ch.link(v.tensor_scalar(pen[:], new[:], LOW, None, ALU.mult))
            v.tensor_scalar(later[:], new[:], 0.0, NEG, ALU.is_equal, ALU.mult).then_inc(s("pens"), 1)
            v.wait_ge(s("cols_ps"), 4)
            ch.link(v.tensor_copy(n_col[:], pt[:, 0, 0:RT]))
            v.tensor_copy(T.ixs[:, :, K], n_col[:])
            v.tensor_copy(T.ixs[:, :, K + 1], pt[:, 1, 0:RT]).then_inc(s("chunk_ix"), 1)
            v.tensor_copy(T.rel[:], pt[:, 2, 0:RT])
            v.tensor_copy(T.blk[:], pt[0:1, 3, 0:RT])
            v.wait_ge(s("pen_ps"), 2)
            v.tensor_copy(pen_b[:, P - 1:P], pt[0:RT, 5, 0:1])
            v.tensor_copy(T.mask[:].rearrange("p (t k) -> p t k", k=SLOTS)[:, :, K], pt[:, 4, P:P + RT])
            v.wait_ge(s("pens"), 1)
            ch.link(v.tensor_copy(pen_b[:, 0:P - 1], pen[:, 1:P]))
            v.tensor_tensor_scan(pen_pre[:], pen[:], pen[:], 0.0, ALU.min, ALU.min)
            back = pen_b[:, ::-1]
            v.tensor_copy(pen_r[:], back)
            v.tensor_tensor_scan(pen_suf[:, ::-1], back, back, 0.0, ALU.min, ALU.min).then_inc(s("pens2"), 1)
            v.wait_ge(s("pen2_ps"), 2)
            v.tensor_copy(T.pen_tile[:], pt[0:4, 6, 0:RT])
            ch.link(v.tensor_copy(T.pen_tile_b[:].rearrange("h (c t) -> h c t", t=CT)[:, :, ::-1],
                                  pt[0:4, 7, 0:RT].rearrange("h (c t) -> h c t", t=CT)))

            prep_k = ch.k

            def masks(i):
                for b in range(UC):
                    t = i * UC + b
                    v.wait_ge(s(f"got{b}"), 16 * i + 16)
                    if not isinstance(i, int):
                        v.wait_ge(s(f"mask{b}"), i)
                    v.tensor_scalar(differs[:, b, :], got[:, b, K:2 * K], n_col[:, bass.ds(t, 1)], None,
                                    ALU.not_equal).then_inc(s(f"diff{b}"), 1)
                    v.wait_ge(s(f"diff{b}"), i + 1)
                    v.tensor_scalar(T.mask[:, bass.ds(t * SLOTS, K)], differs[:, b, :], NEG, None, ALU.mult
                                    ).then_inc(s(f"mask{b}"), 1)
            loop(v, RT // UC, masks)

        @block.scalar
        def _(a):
            a.wait_ge(s("chunk_ix"), 1)

            def copies(i):
                for b in range(UC):
                    t = i * UC + b
                    reuse(a, s(f"got{b}"), i, 16)
                    a.copy(stage[:, b, :], T.ixs[:, bass.ds(t, 1), K + 1]).then_inc(s(f"stage_ready{b}"), 1)
                for b in range(UC):
                    t = i * UC + b
                    a.wait_ge(s(f"got{b}"), 16 * i + 16)
                    a.copy(T.ixs[:, bass.ds(t, 1), 0:K], got[:, b, 0:K].unsqueeze(1)).then_inc(s(f"kept{b}"), 1)
            loop(a, RT // UC, copies)
    ph.close()


def message_pass(c, T, name, H, C, src_w, node_w, table, node_table, kind, chunk_attr=None, vec=None):
    nc = c.nc
    ph = Phase(c, name)
    s = ph.sem
    F = H * (C + 1)
    FEAT = 128
    gathers = K + 1 + (kind == "conv")
    KS = SLOTS if kind == "gat" else K
    ix = ph.sb("ix", [P, U, ROW_IX], I32)
    src = ph.sb("src", [P, U, KS, src_w])
    node = ph.sb("node", [P, U, node_w]) if kind != "gat" else None
    attr = ph.sb("attr", [P, U, K * 32]) if kind == "conv" else None
    prod_w = {"conv": H * C, "gat": 1, "gatv2": H * C, "dot": H * C}[kind]
    prod = ph.sb("prod", [P, KS, prod_w])
    act = ph.sb("act", [P, K, prod_w]) if kind == "gatv2" else None
    raw = ph.sb("raw", [P, KS, H])
    lg = ph.sb("lg", [P, KS, H])
    top = ph.sb("top", [P, U, H])
    low = ph.sb("low", [P, U, KS, H])
    msg = ph.sb("msg", [P, U, KS, H, C + 1])
    ring = ph.sb("ring", [P, CT, F])
    scaled = ph.sb("scaled", [P, U, F])
    onehot = ph.sb("onehot", [P, U, 2 * P])
    gap = ph.sb("gap", [P, CT, H])
    mh = ph.sb("mh", [P, H, CT])
    fwd, full, bwd, whole = [ph.sb(n, [CT, H, P]) for n in ("fwd", "full", "bwd", "whole")]
    edge = ph.sb("edge", [CT, 2, H])
    edgeT = ph.sb("edgeT", [H, 2, CT])
    runs = ph.sb("runs", [H, 2, CT + 1])
    into = ph.sb("into", [CT, 2, H])
    delta = ph.sb("delta", [1, H + 1])
    chosen = ph.sb("chosen", [P, 1])
    shrink_log = ph.sb("shrink_log", [P, H])
    shrink = ph.sb("shrink", [P, H])
    top1 = ph.sb("top1", [P, 1])
    largest = ph.sb("largest", [1, 2])
    sums_ps = ph.ps("sums_ps", [P, U, 512])
    merge_ps = ph.ps("merge_ps", [P, 4, 512])
    mx_ps = ph.ps("mx_ps", [P, 512])
    acc = T.acc[:, 0:(NB + 1) * F].rearrange("p (b f) -> p b f", f=F)
    whole_max = kind == "gatv2"

    def all_chunks(eng, edges, maxima, merge_only):
        edges(0, 0, None)
        with eng.Fori(1, S) as j:
            edges(j, j, None)
        with eng.Fori(1, NCH) as ch:
            maxima(ch - 1)
            edges(ch * S, 0, (ch - 1) * S)
            with eng.Fori(1, S) as j:
                edges(ch * S + j, j, (ch - 1) * S + j)
        maxima(NCH - 1)
        with eng.Fori(0, S) as j:
            merge_only((NCH - 1) * S + j, j)

    def gather_steps(eng, body):
        body(0)
        with eng.Fori(1, RT // U) as i:
            body(i)

    with nc.Block() as block:
        @block.sync
        def _(sp):
            def body(i):
                for b in range(U):
                    reuse(sp, s(f"gathered{b}"), i, 16 * gathers)
                    sp.dma_start(ix[:, b, :], T.ixs[:, bass.ds(i * U + b, 1), :].rearrange("p o k -> p (o k)")
                                 ).then_inc(s(f"ix_in{b}"), 16)
            gather_steps(sp, body)

        @block.gpsimd
        def _(g):
            def gather(out, table_, col, b):
                g.indirect_dma_start(out=out, out_offset=None, in_=table_,
                                     in_offset=bass.IndirectOffsetOnAxis(ap=ix[:, b, col:col + 1], axis=0)
                                     ).then_inc(s(f"gathered{b}"), 16)

            def body(i):
                for b in range(U):
                    reuse(g, s(f"messages{b}"), i)
                    g.wait_ge(s(f"ix_in{b}"), 16 * i + 16)
                    g.nop(nofuse=True)
                    if kind == "gat":
                        gather(src[:, b, K, :], table[:, :], K, b)
                    else:
                        gather(node[:, b, :], node_table[:, :], K, b)
                    if kind == "conv":
                        gather(attr[:, b, :], chunk_attr[:, :], K + 1, b)
                    for k in range(K):
                        gather(src[:, b, k, :], table[:, :], k, b)
            gather_steps(g, body)

        @block.vector
        def _(v):
            ch = Chain(v, s("dve"))
            mc = Chain(v, s("dve_maxima"), 5 if whole_max else 11)

            def feature_logits(b):
                if kind == "conv":
                    pv = prod[:].rearrange("p k (h c) -> p k h c", h=H)
                    nv = node[:, b, :].rearrange("p (h c) -> p h c", h=H)
                    v.tensor_tensor(pv[:, :, :, 0:FEAT], bcast(src[:, b, :, :], [P, K, H, FEAT], 2),
                                    bcast(nv[:, :, 0:FEAT], [P, K, H, FEAT], 1), ALU.mult)
                    av = attr[:, b, :].rearrange("p (k c) -> p k c", k=K)
                    ch.link(v.tensor_tensor(pv[:, :, :, FEAT:C], bcast(av, [P, K, H, C - FEAT], 2),
                                            bcast(nv[:, :, FEAT:C], [P, K, H, C - FEAT], 1), ALU.mult))
                    ch.link(v.tensor_reduce(lg[:], pv, X, ALU.add))
                    ch.link(v.tensor_tensor(raw[:], lg[:], bcast(nv[:, :, C], [P, K, H], 1), ALU.add))
                    return
                if kind == "gat":
                    ch.link(v.tensor_tensor(lg[:], src[:, b, :, H * C:H * C + H],
                                            bcast(src[:, b, K, H * C + H:], [P, KS, H], 1), ALU.add))
                elif kind == "dot":
                    ch.link(v.tensor_tensor(prod[:], src[:, b, :, 0:H * C],
                                            bcast(node[:, b, :], [P, K, H * C], 1), ALU.mult))
                    ch.link(v.tensor_reduce(lg[:], prod[:].rearrange("p k (h c) -> p k h c", h=H), X, ALU.add))
                elif kind == "gatv2":
                    ch.link(v.tensor_tensor(prod[:], src[:, b, :, :], bcast(node[:, b, :], [P, K, H * C], 1), ALU.add))
                    ch.link(v.scalar_tensor_tensor(act[:], prod[:], NEG_SLOPE, prod[:], ALU.mult, ALU.max))
                    ch.link(v.tensor_tensor(prod[:], act[:], bcast(vec[:], [P, K, H * C], 1), ALU.mult))
                    ch.link(v.tensor_reduce(raw[:], prod[:].rearrange("p k (h c) -> p k h c", h=H), X, ALU.add))
                    return
                ch.link(v.scalar_tensor_tensor(raw[:], lg[:], NEG_SLOPE, lg[:], ALU.mult, ALU.max))

            def one_hot(im, b):
                v.wait_ge(s(f"spread{b}"), im + 1)
                v.tensor_scalar(onehot[:, b, :], T.iota256[:], T.rel[:, bass.ds(im * U + b, 1)], None,
                                ALU.is_equal).then_inc(s(f"onehot{b}"), 1)

            def add(im, b):
                t = im * U + b
                block_of = v.value_load(T.blk[0:1, bass.ds(t, 1)], min_val=0, max_val=NB - 1)
                v.wait_ge(s(f"spread{b}"), im + 2)
                v.nop(nofuse=True)
                v.wait_ge(s("added"), t + U + 1)
                pair = merge_ps[:, 2 * (b % 2):2 * (b % 2) + 2, 0:F]
                v.tensor_tensor(acc[:, bass.ds(block_of, 2), :], acc[:, bass.ds(block_of, 2), :], pair, ALU.add
                                ).then_inc(s("added"), 1)

            def edges(i, j, im):
                ch.begin(i)
                for b in range(U):
                    t = i * U + b
                    v.wait_ge(s(f"gathered{b}"), (16 * i + 16) * gathers)
                    feature_logits(b)
                    ch.link(v.tensor_tensor(lg[:], raw[:], bcast(T.mask[:, bass.ds(t * SLOTS, KS)], [P, KS, H], 2), ALU.add))
                    reuse(v, s(f"tops_kept{b}"), i)
                    ch.link(v.tensor_reduce(top[:, b, :], lg[:].rearrange("p k h -> p h k"), X, ALU.max))
                    v.tensor_tensor(low[:, b, :, :], lg[:], bcast(top[:, b, :], [P, KS, H], 1), ALU.subtract
                                    ).then_inc(s(f"logits{b}"), 1)
                    if im is not None:
                        one_hot(im, b)
                    v.wait_ge(s(f"weights{b}"), i + 1)
                    w = msg[:, b, :, :, C:C + 1]
                    if kind == "conv":
                        v.tensor_tensor(msg[:, b, :, :, 0:FEAT], bcast(src[:, b, :, :], [P, K, H, FEAT], 2),
                                        w.to_broadcast([P, K, H, FEAT]), ALU.mult)
                        av = attr[:, b, :].rearrange("p (k c) -> p k c", k=K)
                        last = v.tensor_tensor(msg[:, b, :, :, FEAT:C], bcast(av, [P, K, H, C - FEAT], 2),
                                               w.to_broadcast([P, K, H, C - FEAT]), ALU.mult)
                    else:
                        at = H * C if kind == "dot" else 0
                        val = src[:, b, :, at:at + H * C].rearrange("p k (h c) -> p k h c", h=H)
                        last = v.tensor_tensor(msg[:, b, :, :, 0:C], val, w.to_broadcast([P, KS, H, C]), ALU.mult)
                    last.then_inc(s(f"messages{b}"), 1)
                    if im is not None and b:
                        add(im, b - 1)
                if im is not None:
                    add(im, U - 1)

            def merge_only(im, j):
                for b in range(U):
                    one_hot(im, b)
                for b in range(U):
                    add(im, b)

            def node_maxima(cm):
                pen = lambda tab: tab[:, bass.ds(cm * P, P)]
                for b in range(U):
                    v.wait_ge(s(f"tops_kept{b}"), cm * S + S)
                v.nop(nofuse=True)
                mc.begin(cm)
                v.tensor_copy(mh[:], T.m[:, bass.ds(cm * (CT * H), CT * H)].rearrange("p (t h) -> p h t", h=H)
                              ).then_inc(s("by_head"), 1)
                v.wait_ge(s("rows_T"), cm + 1)
                for h in range(H):
                    last = v.tensor_tensor_scan(fwd[:, h, :], pen(T.pen), mx_ps[0:CT, h * P:(h + 1) * P], LOW,
                                                ALU.add, ALU.max)
                mc.link(last)
                v.tensor_copy(edge[:, 0, :], fwd[:, :, P - 1]).then_inc(s("edge"), 1)
                v.wait_ge(s("edge_T"), cm * 2 + 1)
                mc.link(v.tensor_copy(edgeT[:, 0, :], mx_ps[0:H, 0:CT]))
                v.tensor_tensor_scan(runs[:, 0, 1:CT + 1], T.pen_tile[0:H, bass.ds(cm * CT, CT)], edgeT[:, 0, :],
                                     runs[:, 0, 0:1], ALU.add, ALU.max).then_inc(s("runs"), 1)
                v.wait_ge(s("into_T"), cm * 2 + 1)
                mc.link(v.tensor_copy(into[:, 0, :], mx_ps[0:CT, 64:64 + H]))
                mc.link(v.tensor_copy(runs[:, 0, 0:1], runs[:, 0, CT:CT + 1]))
                for h in range(H):
                    last = v.scalar_tensor_tensor(full[:, h, :], pen(T.pen_pre), into[:, 0, h:h + 1], fwd[:, h, :],
                                                  ALU.add, ALU.max)
                mc.link(last)
                for h in range(H):
                    last = v.tensor_tensor_scan(bwd[:, h, ::-1], pen(T.pen_b), full[:, h, ::-1], LOW,
                                                ALU.add, ALU.max)
                mc.link(last)
                v.tensor_copy(edge[:, 1, :], bwd[:, :, 0]).then_inc(s("edge"), 1)
                v.wait_ge(s("edge_T"), cm * 2 + 2)
                mc.link(v.tensor_copy(edgeT[:, 1, :], mx_ps[0:H, 32:32 + CT]))
                v.tensor_tensor_scan(runs[:, 1, 0:CT][:, ::-1], T.pen_tile_b[0:H, bass.ds(cm * CT, CT)],
                                     edgeT[:, 1, ::-1], LOW, ALU.add, ALU.max).then_inc(s("runs"), 1)
                v.wait_ge(s("into_T"), cm * 2 + 2)
                mc.link(v.tensor_copy(into[:, 1, :], mx_ps[0:CT, 72:72 + H]))
                for h in range(H):
                    last = v.scalar_tensor_tensor(whole[:, h, :], pen(T.pen_suf), into[:, 1, h:h + 1], bwd[:, h, :],
                                                  ALU.add, ALU.max)
                last.then_inc(s("whole"), 1)
                v.wait_ge(s("whole"), cm + 1)
                mc.link(v.tensor_tensor(edge[0:1, 0, :], into[0:1, 0, :], whole[0:1, :, 0], ALU.subtract))
                mc.link(v.tensor_scalar(delta[:, 0:H], edge[0:1, 0, :], 0.0, None, ALU.min))
                v.nop(nofuse=True)
                v.tensor_copy(delta[:, H:H + 1], T.rel[0:1, bass.ds(cm * CT, 1)]).then_inc(s("delta"), 1)
                v.wait_ge(s("maxima"), cm + 1)
                v.tensor_tensor(gap[:], T.m[:, bass.ds(cm * (CT * H), CT * H)].rearrange("p (t h) -> p t h", h=H),
                                mx_ps[:, 128:128 + H * CT].rearrange("p (h t) -> p t h", h=H), ALU.subtract
                                ).then_inc(s("gap"), 1)
                mc.link(v.tensor_scalar(chosen[:], T.pid[:], mx_ps[:, 256 + H:257 + H], None, ALU.is_equal))
                v.tensor_scalar(shrink_log[:], mx_ps[:, 256:256 + H], chosen[:], None, ALU.mult
                                ).then_inc(s("shrink_log"), 1)
                block_of = v.value_load(T.blk[0:1, bass.ds(cm * CT, 1)], min_val=0, max_val=NB - 1)
                v.wait_ge(s("shrink"), cm + 1)
                v.nop(nofuse=True)
                v.wait_ge(s("added"), cm * CT + U + 1)
                own = acc[:, bass.ds(block_of, 1), :].rearrange("p o (h c) -> p (o h) c", h=H)
                v.tensor_tensor(own, own, bcast(shrink[:], [P, H, C + 1], 2), ALU.mult).then_inc(s("shrunk"), 1)
                v.wait_ge(s("shrunk"), cm + 1)

            def global_maximum(cm):
                for b in range(U):
                    v.wait_ge(s(f"tops_kept{b}"), cm * S + S)
                v.nop(nofuse=True)
                mc.begin(cm)
                v.tensor_reduce(top1[:], T.m[:, bass.ds(cm * (CT * H), CT * H)], X, ALU.max).then_inc(s("by_head"), 1)
                v.wait_ge(s("rows_T"), cm + 1)
                mc.link(v.tensor_reduce(edge[0:1, 0, 0:1], mx_ps[0:1, 0:P], X, ALU.max))
                mc.link(v.tensor_tensor(largest[:, 1:2], largest[:, 0:1], edge[0:1, 0, 0:1], ALU.max))
                v.tensor_tensor(delta[:, 1:2], largest[:, 0:1], largest[:, 1:2], ALU.subtract)
                mc.link(v.tensor_scalar(delta[:, 0:1], largest[:, 1:2], -1.0, None, ALU.mult))
                mc.link(v.tensor_copy(largest[:, 0:1], largest[:, 1:2]))
                v.memset(delta[:, 2:], 0.0).then_inc(s("delta"), 1)
                v.wait_ge(s("delta_all"), cm + 1)
                mc.link(v.tensor_copy(shrink_log[:, 0:2], mx_ps[:, 256:258]))
                v.tensor_copy(chosen[:], shrink_log[:, 0:1]).then_inc(s("gap"), 1)
                v.wait_ge(s("shrink"), cm + 1)
                v.nop(nofuse=True)
                v.wait_ge(s("added"), cm * CT + U + 1)
                v.tensor_scalar(acc, acc, shrink[:, 1:2], None, ALU.mult).then_inc(s("shrunk"), 1)
                v.wait_ge(s("shrunk"), cm + 1)

            v.memset(acc, 0.0).then_inc(s("added"), U + 1)
            v.memset(runs[:], LOW)
            v.memset(largest[:], LOW).then_inc(s("blank"), 1)
            v.wait_ge(s("blank"), 1)
            all_chunks(v, edges, global_maximum if whole_max else node_maxima, merge_only)
            assert mc.k == mc.steps
            v.wait_ge(s("added"), RT + U + 1)

        @block.tensor
        def _(pe):
            def merge(im, b):
                t = im * U + b
                pe.wait_ge(s(f"scaled{b}"), im + 1)
                pe.wait_ge(s(f"onehot{b}"), im + 1)
                pe.wait_ge(s("added"), t + U + 2 - (1, 3, 2)[b])
                for j in range(2):
                    last = pe.matmul(merge_ps[:, 2 * (b % 2) + j, 0:F], onehot[:, b, j * P:(j + 1) * P],
                                     scaled[:, b, :], start=True, stop=True)
                last.then_inc(s(f"spread{b}"), 1)

            def edges(i, j, im):
                for b in range(U):
                    if im is not None:
                        merge(im, b)
                    pe.wait_ge(s(f"messages{b}"), i + 1)
                    reuse(pe, s(f"evacuated{b}"), i)
                    for k in range(KS):
                        last = pe.matmul(sums_ps[:, b, 0:F], T.ident[:],
                                         msg[:, b, k, :, :].rearrange("p h c -> p (h c)"),
                                         start=(k == 0), stop=(k == KS - 1))
                    last.then_inc(s(f"summed{b}"), 1)

            def merge_only(im, j):
                for b in range(U):
                    merge(im, b)

            def maxima(cm):
                pe.wait_ge(s("by_head"), cm + 1)
                if whole_max:
                    pe.transpose(mx_ps[0:1, 0:P], top1[:], T.ident[:]).then_inc(s("rows_T"), 1)
                    pe.wait_ge(s("delta"), cm + 1)
                    pe.matmul(mx_ps[:, 256:257 + H], T.ones[:], delta[:], start=True, stop=True
                              ).then_inc(s("delta_all"), 1)
                    return
                for h in range(H):
                    last = pe.transpose(mx_ps[0:CT, h * P:(h + 1) * P], mh[:, h, :], T.ident[:])
                last.then_inc(s("rows_T"), 1)
                for d in range(2):
                    pe.wait_ge(s("edge"), cm * 2 + d + 1)
                    pe.nop(nofuse=True)
                    pe.transpose(mx_ps[0:H, 32 * d:32 * d + CT], edge[:, d, :], T.ident[0:CT, 0:CT]
                                 ).then_inc(s("edge_T"), 1)
                    pe.wait_ge(s("runs"), cm * 2 + d + 1)
                    pe.nop(nofuse=True)
                    pe.transpose(mx_ps[0:CT, 64 + 8 * d:64 + 8 * d + H], runs[:, d, d:d + CT], T.ident[0:H, 0:H]
                                 ).then_inc(s("into_T"), 1)
                pe.wait_ge(s("whole"), cm + 1)
                pe.nop(nofuse=True)
                for h in range(H):
                    pe.transpose(mx_ps[:, 128 + h * CT:128 + (h + 1) * CT], whole[:, h, :], T.ident[0:CT, 0:CT])
                pe.wait_ge(s("delta"), cm + 1)
                pe.matmul(mx_ps[:, 256:257 + H], T.ones[:], delta[:], start=True, stop=True).then_inc(s("maxima"), 1)

            for b in range(U):
                pe.nop(nofuse=True).then_inc(s(f"spread{b}"), 1)
            all_chunks(pe, edges, maxima, merge_only)

        @block.scalar
        def _(a):
            def keep(i, b, slot):
                a.wait_ge(s(f"summed{b}"), i + 1)
                a.nop(nofuse=True)
                a.copy(ring[:, slot, :], sums_ps[:, b, 0:F]).then_inc(s(f"evacuated{b}"), 1)

            def scale(im, j, b):
                t = im * U + b
                a.wait_ge(s(f"spread{b}"), im + 1)
                a.wait_ge(s(f"evacuated{b}"), im + 1)
                a.nop(nofuse=True)
                for h in range(H):
                    own = slice(h * (C + 1), (h + 1) * (C + 1))
                    last = a.activation(scaled[:, b, own],
                                        ring[:, bass.ds(j * U + b, 1), own].rearrange("p o c -> p (o c)"), ACT.Copy,
                                        scale=T.factor[:, bass.ds(t * H + h, 1)])
                last.then_inc(s(f"scaled{b}"), 1)

            def edges(i, j, im):
                for b in range(U):
                    t = i * U + b
                    a.wait_ge(s(f"logits{b}"), i + 1)
                    reuse(a, s(f"summed{b}"), i)
                    a.activation(msg[:, b, :, :, C], low[:, b, :, :], ACT.Exp).then_inc(s(f"weights{b}"), 1)
                    a.copy(T.m[:, bass.ds(t * H, H)], top[:, b, :]).then_inc(s(f"tops_kept{b}"), 1)
                    if b:
                        keep(i, b - 1, bass.ds(j * U + b - 1, 1))
                    elif isinstance(j, int) and im is not None:
                        keep(i - 1, U - 1, bass.ds(CT - 1, 1))
                    elif not isinstance(j, int):
                        keep(i - 1, U - 1, bass.ds(j * U - 1, 1))
                    if im is not None:
                        scale(im, j, b)

            def merge_only(im, j):
                for b in range(U):
                    scale(im, j, b)

            def maxima(cm):
                if isinstance(cm, int):
                    keep(NCH * S - 1, U - 1, bass.ds(CT - 1, 1))
                a.wait_ge(s("gap"), cm + 1)
                a.nop(nofuse=True)
                mine = T.factor[:, bass.ds(cm * (CT * H), CT * H)]
                if whole_max:
                    a.activation(mine, T.m[:, bass.ds(cm * (CT * H), CT * H)], ACT.Exp, bias=chosen[:])
                    a.activation(shrink[:, 0:2], shrink_log[:, 0:2], ACT.Exp).then_inc(s("shrink"), 1)
                    a.wait_ge(s("shrink"), cm + 1)
                    return
                a.activation(mine, gap[:].rearrange("p t h -> p (t h)"), ACT.Exp)
                a.wait_ge(s("shrink_log"), cm + 1)
                a.activation(shrink[:], shrink_log[:], ACT.Exp).then_inc(s("shrink"), 1)
                a.wait_ge(s("shrink"), cm + 1)
            all_chunks(a, edges, maxima, merge_only)
    ph.close()


LN_EPS = 1e-5


class Dense:

    def __init__(self, c, T, name, H=0, C=0):
        self.c, self.T, self.nc = c, T, c.nc
        self.ph = Phase(c, name)
        self.s, self.sb = self.ph.sem, self.ph.sb
        self.pt = self.ph.ps("pt", [P, 8, 512])
        self.small = self.sb("small", [P, 3, G])
        self.cen = self.sb("cen", [P, G, P])
        self.sq = self.sb("sq", [P, G, P])
        if H:
            F = H * (C + 1)
            self.acc = T.acc[:, 0:NB * F].rearrange("p (b h c) -> p b h c", h=H, c=C + 1)

    def group(self, ap, i):
        return ap[:, bass.ds(i * G, G)]

    def hT_slot(self, j):
        return self.pt[:, 5 + j // 4, (j % 4) * P:(j % 4) * P + P]

    def norm_vector(self, v, ch, i, src, out, tag, relu=False, gain=None, shift=None):
        s, small, cen, sq = self.s, self.small, self.cen, self.sq
        ch.link(v.tensor_reduce(small[:, 0, :], src, X, ALU.add))
        ch.link(v.tensor_scalar(small[:, 0, :], small[:, 0, :], -1.0 / P, None, ALU.mult))
        ch.link(v.tensor_tensor(cen[:], src, bcast(small[:, 0, :], [P, G, P], 2), ALU.add))
        ch.link(v.tensor_tensor(sq[:], cen[:], cen[:], ALU.mult))
        ch.link(v.tensor_reduce(small[:, 1, :], sq[:], X, ALU.add))
        v.tensor_scalar(small[:, 1, :], small[:, 1, :], 1.0 / P, LN_EPS, ALU.mult, ALU.add).then_inc(s(f"{tag}_var"), 1)
        v.wait_ge(s(f"{tag}_std"), i + 1)
        ch.link(v.reciprocal(small[:, 2, :], small[:, 2, :]))
        ch.link(v.tensor_tensor(sq[:], cen[:], bcast(small[:, 2, :], [P, G, P], 2), ALU.mult))
        if gain is not None:
            ch.link(v.tensor_tensor(cen[:], sq[:], bcast(gain[:], [P, G, P], 1), ALU.mult))
            return v.tensor_tensor(out, cen[:], bcast(shift[:], [P, G, P], 1), ALU.add)
        return v.tensor_scalar(out, sq[:], 0.0, None, ALU.max)

    def norm_scalar(self, a, i, tag):
        a.wait_ge(self.s(f"{tag}_var"), i + 1)
        a.activation(self.small[:, 2, :], self.small[:, 1, :], ACT.Sqrt).then_inc(self.s(f"{tag}_std"), 1)


def rows_of(table, i, n=G):
    return table[bass.ds(i * (G * P), n * P), :].rearrange("(b p) w -> p b w", p=P)


def node_in(c, T, W, table, node_table):
    d = Dense(c, T, "in")
    s, pt = d.s, d.pt
    h = d.sb("h", [P, G, P])
    hT = d.sb("hT", [P, G, P])
    wq = d.sb("wq", [P, 2 * P])
    bq = d.sb("bq", [P, 2])
    kx = d.sb("kx", [P, 2, 161])
    qT = d.sb("qT", [P, G, 2, P])
    td = d.sb("td", [P, G, 322])
    with c.nc.Block() as block:
        @block.sync
        def _(sp):
            for t, w in ((wq, "L0_WqT"), (bq, "L0_bq"), (kx, "L0_kx")):
                sp.dma_start(t[:], W[w]).then_inc(s("weights_in"), 16)

            def body(i):
                sp.wait_ge(s("h"), i + 1)
                sp.dma_start(rows_of(table, i), h[:]).then_inc(s("h_out"), 16)
                sp.wait_ge(s("td"), i + 1)
                sp.dma_start(rows_of(node_table, i), td[:]).then_inc(s("td_out"), 16)
            loop(sp, NG, body)
            sp.wait_ge(s("h_out"), 16 * NG)
            sp.wait_ge(s("td_out"), 16 * NG)

        @block.vector
        def _(v):
            ch = Chain(v, s("dve"))
            v.wait_ge(s("weights_in"), 48)

            def body(i):
                ch.begin(i)
                reuse(v, s("h_out"), i, 16)
                reuse(v, s("hs"), i)
                reuse(v, s("hT_ps"), i)
                d.norm_vector(v, ch, i, d.group(T.xs, i), h[:], "ln", relu=True).then_inc(s("h"), 1)
                v.wait_ge(s("qT_ps"), i + 1)
                for m in range(2):
                    last = v.tensor_scalar(qT[:, :, m, :], pt[:, 0:G, (1 + m) * P:(2 + m) * P], bq[:, m:m + 1],
                                           float(P) ** -0.5, ALU.add, ALU.mult)
                last.then_inc(s("qT"), 1)
            loop(v, NG, body)

        @block.tensor
        def _(pe):
            def body(i):
                pe.wait_ge(s("h"), i + 1)
                reuse(pe, s("td"), i)
                for j in range(G):
                    last = pe.transpose(pt[:, j, 0:P], h[:, j, :], T.ident[:])
                last.then_inc(s("hT_ps"), 1)
                pe.wait_ge(s("hT"), i + 1)
                for j in range(G):
                    for m in range(2):
                        last = pe.matmul(pt[:, j, (1 + m) * P:(2 + m) * P], wq[:, m * P:(m + 1) * P], hT[:, j, :],
                                         start=True, stop=True)
                last.then_inc(s("qT_ps"), 1)
                pe.wait_ge(s("qT"), i + 1)
                for j in range(G):
                    for m in range(2):
                        last = pe.matmul(pt[:, j, m * 161:(m + 1) * 161], qT[:, j, m, :], kx[:, m, :],
                                         start=True, stop=True)
                last.then_inc(s("td_ps"), 1)
            loop(pe, NG, body)

        @block.scalar
        def _(a):
            def body(i):
                d.norm_scalar(a, i, "ln")
                a.wait_ge(s("h"), i + 1)
                a.copy(d.group(T.hs, i), h[:]).then_inc(s("hs"), 1)
                a.wait_ge(s("hT_ps"), i + 1)
                a.copy(hT[:], pt[:, 0:G, 0:P]).then_inc(s("hT"), 1)
                a.wait_ge(s("td_ps"), i + 1)
                reuse(a, s("td_out"), i, 16)
                a.copy(td[:], pt[:, 0:G, 0:322]).then_inc(s("td"), 1)
            loop(a, NG, body)
    d.ph.close()


def project_vector(d, v, ch, i, H, C, rows, a_src, a_dst, prod):
    s = d.s
    v.wait_ge(s("xp"), i + 1)
    pv = prod[:, :, 0:H * C]
    by_head = pv.rearrange("p g (h c) -> p g h c", h=H)
    ch.link(v.tensor_tensor(pv, rows[:, :, 0:H * C], bcast(a_src[:, 0:H * C], [P, G, H * C], 1), ALU.mult))
    ch.link(v.tensor_reduce(rows[:, :, H * C:H * C + H], by_head, X, ALU.add))
    ch.link(v.tensor_tensor(pv, rows[:, :, 0:H * C], bcast(a_dst[:, 0:H * C], [P, G, H * C], 1), ALU.mult))
    v.tensor_reduce(rows[:, :, H * C + H:], by_head, X, ALU.add).then_inc(s("rows"), 1)


def node_after_conv(c, T, W, table):
    H, C, HC = 2, 160, 256
    d = Dense(c, T, "conv_out", H, C)
    s, pt = d.s, d.pt
    names = {"wv": ("L0_WvT", [P, 2 * P]), "web": ("L0_web", [33, 2, P]), "wskip": ("L0_WskipT", [P, P]),
             "bskip": ("L0_bskip", [1, P]), "w1": ("L0_W1T", [P, 2 * P]), "b1": ("L0_b1", [P, 2]),
             "w2": ("L0_W2T", [P, 2, P]), "b2": ("L0_b2", [1, P]), "w0": ("L1_W0", [P, HC])}
    w = {k: d.sb(k, shape) for k, (_, shape) in names.items()}
    vecs = {k: d.sb(k, [P, W[n].shape[-1]]) for k, n in
            (("g1", "L0_ln1_g"), ("s1", "L0_ln1_b"), ("g2", "L0_ln2_g"), ("s2", "L0_ln2_b"),
             ("a_src", "L1_as0"), ("a_dst", "L1_ad0"))}
    vec_of = {"g1": "L0_ln1_g", "s1": "L0_ln1_b", "g2": "L0_ln2_g", "s2": "L0_ln2_b",
              "a_src": "L1_as0", "a_dst": "L1_ad0"}
    rden = d.sb("rden", [P, G, H])
    den = d.sb("den", [P, G, H])
    agg = d.sb("agg", [P, G, H, C + 1])
    aggT = d.sb("aggT", [P, G, H, P])
    attT = d.sb("attT", [33, G, H, P])
    h0 = d.sb("h0", [P, G, P])
    hT = d.sb("hT", [P, G, P])
    pre = d.sb("pre", [P, G, P])
    pre2 = d.sb("pre2", [P, G, P])
    h1 = d.sb("h1", [P, G, P])
    h1T = d.sb("h1T", [P, G, P])
    up = d.sb("up", [P, 2, G, P])
    f1 = d.sb("f1", [P, 2, G, P])
    x1 = d.sb("x1", [P, G, P])
    h = d.sb("h", [P, G, P])
    rows = d.sb("rows", [P, G, HC + 8])
    prod = d.sb("prod", [P, G, HC])
    n_loads = len(w) + len(vecs)

    with c.nc.Block() as block:
        @block.sync
        def _(sp):
            for k, (n, _) in names.items():
                sp.dma_start(w[k][:], W[n]).then_inc(s("weights_in"), 16)
            for k, t in vecs.items():
                sp.dma_start(t[:], W[vec_of[k]].partition_broadcast(P)).then_inc(s("weights_in"), 16)

            def body(i):
                sp.wait_ge(s("rows"), i + 1)
                sp.dma_start(rows_of(table, i), rows[:]).then_inc(s("rows_out"), 16)
            loop(sp, NG, body)
            sp.wait_ge(s("rows_out"), 16 * NG)

        @block.vector
        def _(v):
            ch = Chain(v, s("dve"))
            v.wait_ge(s("weights_in"), 16 * n_loads)

            def body(i):
                ch.begin(i)
                acc = d.group(d.acc, i)
                ch.link(v.tensor_scalar(den[:], acc[:, :, :, C], 1e-16, None, ALU.add))
                ch.link(v.reciprocal(rden[:], den[:]))
                reuse(v, s("aggT_ps"), i)
                v.tensor_tensor(agg[:], acc, bcast(rden[:], [P, G, H, C + 1], 3), ALU.mult).then_inc(s("agg"), 1)
                v.wait_ge(s("mixed"), i + 1)
                ch.link(v.scalar_tensor_tensor(pre[:], pt[:, 0:G, 0:P], 0.5, h0[:], ALU.mult, ALU.add))
                ch.link(v.tensor_tensor(pre2[:], pre[:], pt[:, 0:G, P:2 * P], ALU.add))
                d.norm_vector(v, ch, i, pre2[:], h1[:], "ln1", gain=vecs["g1"], shift=vecs["s1"]
                              ).then_inc(s("h1"), 1)
                v.wait_ge(s("up"), i + 1)
                v.scalar_tensor_tensor(f1[:].rearrange("p m g n -> p (m g n)"), up[:].rearrange("p m g n -> p (m g n)"),
                                       0.01, up[:].rearrange("p m g n -> p (m g n)"), ALU.mult, ALU.max
                                       ).then_inc(s("f1"), 1)
                v.wait_ge(s("f2_ps"), i + 1)
                ch.link(v.tensor_tensor(pre[:], h1[:], pt[:, 0:G, 0:P], ALU.add))
                ch.link(d.norm_vector(v, ch, i, pre[:], pre2[:], "ln2", gain=vecs["g2"], shift=vecs["s2"]))
                ch.link(v.tensor_tensor(x1[:], d.group(T.xs, i), pre2[:], ALU.add))
                v.tensor_scalar(d.group(T.xs, i), x1[:], 1.0, None, ALU.mult)
                d.norm_vector(v, ch, i, x1[:], h[:], "ln3").then_inc(s("h"), 1)
                project_vector(d, v, ch, i, 4, 64, rows, vecs["a_src"], vecs["a_dst"], prod)
            loop(v, NG, body)

        @block.tensor
        def _(pe):
            pe.wait_ge(s("weights_in"), 16 * n_loads)

            def body(i):
                reuse(pe, s("xp"), i)
                pe.wait_ge(s("agg"), i + 1)
                for j in range(G):
                    for m in range(H):
                        pe.transpose(pt[:, j, m * 256:m * 256 + P], agg[:, j, m, 0:P], T.ident[:])
                        pe.transpose(pt[0:33, j, m * 256 + P:m * 256 + 2 * P], agg[:, j, m, P:161], T.ident[:])
                pe.wait_ge(s("h0"), i + 1)
                for j in range(G):
                    last = pe.transpose(d.hT_slot(j), h0[:, j, :], T.ident[:])
                last.then_inc(s("aggT_ps"), 1)
                pe.wait_ge(s("aggT"), i + 1)
                for j in range(G):
                    for m in range(H):
                        pe.matmul(pt[:, j, 0:P], aggT[:, j, m, :], w["wv"][:, m * P:(m + 1) * P],
                                  start=(m == 0), stop=False)
                        pe.matmul(pt[:, j, 0:P], attT[:, j, m, :], w["web"][:, m, :], start=False, stop=(m == H - 1))
                    pe.matmul(pt[:, j, P:2 * P], hT[:, j, :], w["wskip"][:], start=True, stop=False)
                    last = pe.matmul(pt[:, j, P:2 * P], T.ones[:], w["bskip"][:], start=False, stop=True)
                last.then_inc(s("mixed"), 1)
                pe.wait_ge(s("h1"), i + 1)
                for j in range(G):
                    last = pe.transpose(d.hT_slot(j), h1[:, j, :], T.ident[:])
                last.then_inc(s("h1T_ps"), 1)
                pe.wait_ge(s("h1T"), i + 1)
                for j in range(G):
                    for m in range(2):
                        last = pe.matmul(pt[:, j, m * P:(m + 1) * P], w["w1"][:, m * P:(m + 1) * P], h1T[:, j, :],
                                         start=True, stop=True)
                last.then_inc(s("up_ps"), 1)
                pe.wait_ge(s("f1"), i + 1)
                for j in range(G):
                    for m in range(2):
                        pe.matmul(pt[:, j, 0:P], f1[:, m, j, :], w["w2"][:, m, :], start=(m == 0), stop=False)
                    last = pe.matmul(pt[:, j, 0:P], T.ones[:], w["b2"][:], start=False, stop=True)
                last.then_inc(s("f2_ps"), 1)
                pe.wait_ge(s("h"), i + 1)
                for j in range(G):
                    last = pe.transpose(d.hT_slot(j), h[:, j, :], T.ident[:])
                last.then_inc(s("hT2_ps"), 1)
                pe.wait_ge(s("hT2"), i + 1)
                for j in range(G):
                    last = pe.matmul(pt[:, j, 0:HC], hT[:, j, :], w["w0"][:], start=True, stop=True)
                last.then_inc(s("xp_ps"), 1)
            loop(pe, NG, body)

        @block.scalar
        def _(a):
            a.wait_ge(s("weights_in"), 16 * n_loads)

            def slots(out, tag, i):
                a.copy(out[:, 0:4, :], pt[:, 5, :].rearrange("p (g n) -> p g n", g=4))
                a.copy(out[:, 4, :], pt[:, 6, 0:P]).then_inc(s(tag), 1)

            def body(i):
                reuse(a, s("mixed"), i)
                reuse(a, s("h1"), i)
                a.copy(h0[:], d.group(T.hs, i)).then_inc(s("h0"), 1)
                a.wait_ge(s("aggT_ps"), i + 1)
                pv = pt[:, 0:G, :].rearrange("p g (m n) -> p g m n", m=2)
                a.copy(aggT[:], pv[:, :, :, 0:P])
                a.copy(attT[:], pv[0:33, :, :, P:2 * P])
                reuse(a, s("xp_ps"), i)
                slots(hT, "aggT", i)
                d.norm_scalar(a, i, "ln1")
                a.wait_ge(s("h1T_ps"), i + 1)
                slots(h1T, "h1T", i)
                a.wait_ge(s("up_ps"), i + 1)
                for m in range(2):
                    last = a.activation(up[:, m, :, :], pt[:, 0:G, m * P:(m + 1) * P], ACT.Identity,
                                        bias=w["b1"][:, m:m + 1])
                last.then_inc(s("up"), 1)
                d.norm_scalar(a, i, "ln2")
                d.norm_scalar(a, i, "ln3")
                a.wait_ge(s("hT2_ps"), i + 1)
                slots(hT, "hT2", i)
                a.wait_ge(s("xp_ps"), i + 1)
                reuse(a, s("rows_out"), i, 16)
                a.copy(rows[:, :, 0:HC], pt[:, 0:G, 0:HC]).then_inc(s("xp"), 1)
            loop(a, NG, body)
    d.ph.close()


def node_between_gats(c, T, W, name, bias_n, w_n, as_n, ad_n, HC, table):
    H, C = 4, 64
    d = Dense(c, T, name, H, C)
    s, pt = d.s, d.pt
    w = d.sb("w", [P, 2, HC])
    vecs = {k: d.sb(k, [P, W[n].shape[-1]]) for k, n in (("b", bias_n), ("a_src", as_n), ("a_dst", ad_n))}
    vec_of = {"b": bias_n, "a_src": as_n, "a_dst": ad_n}
    rden = d.sb("rden", [P, G, H])
    o = d.sb("o", [P, G, H * C])
    o2 = d.sb("o2", [P, G, H * C])
    h = d.sb("h", [P, G, H * C])
    hT = d.sb("hT", [P, G, 2, P])
    rows = d.sb("rows", [P, G, HC + 8])
    prod = d.sb("prod", [P, G, HC])
    with c.nc.Block() as block:
        @block.sync
        def _(sp):
            sp.dma_start(w[:], W[w_n]).then_inc(s("weights_in"), 16)
            for k, t in vecs.items():
                sp.dma_start(t[:], W[vec_of[k]].partition_broadcast(P)).then_inc(s("weights_in"), 16)

            def body(i):
                sp.wait_ge(s("rows"), i + 1)
                sp.dma_start(rows_of(table, i), rows[:]).then_inc(s("rows_out"), 16)
            loop(sp, NG, body)
            sp.wait_ge(s("rows_out"), 16 * NG)

        @block.vector
        def _(v):
            ch = Chain(v, s("dve"))
            v.wait_ge(s("weights_in"), 64)

            def body(i):
                ch.begin(i)
                acc = d.group(d.acc, i)
                v.nop(nofuse=True)
                ch.link(v.tensor_copy(rden[:], acc[:, :, :, C]))
                ch.link(v.reciprocal(rden[:], rden[:]))
                ch.link(v.tensor_tensor(o[:].rearrange("p g (h c) -> p g h c", h=H), acc[:, :, :, 0:C],
                                        bcast(rden[:], [P, G, H, C], 3), ALU.mult))
                ch.link(v.tensor_tensor(o2[:], o[:], bcast(vecs["b"][:], [P, G, H * C], 1), ALU.add))
                reuse(v, s("hT_ps"), i)
                v.tensor_scalar(h[:], o2[:], 0.0, None, ALU.max).then_inc(s("h"), 1)
                project_vector(d, v, ch, i, 4, HC // 4, rows, vecs["a_src"], vecs["a_dst"], prod)
            loop(v, NG, body)

        @block.tensor
        def _(pe):
            pe.wait_ge(s("weights_in"), 64)

            def body(i):
                reuse(pe, s("xp"), i)
                pe.wait_ge(s("h"), i + 1)
                for j in range(G):
                    for m in range(2):
                        last = pe.transpose(pt[:, j, m * P:(m + 1) * P], h[:, j, m * P:(m + 1) * P], T.ident[:])
                last.then_inc(s("hT_ps"), 1)
                pe.wait_ge(s("hT"), i + 1)
                for j in range(G):
                    for m in range(2):
                        last = pe.matmul(pt[:, j, 256:256 + HC], hT[:, j, m, :], w[:, m, :], start=(m == 0), stop=(m == 1))
                last.then_inc(s("xp_ps"), 1)
            loop(pe, NG, body)

        @block.scalar
        def _(a):
            def body(i):
                a.wait_ge(s("hT_ps"), i + 1)
                a.copy(hT[:], pt[:, 0:G, 0:256].rearrange("p g (m n) -> p g m n", m=2)).then_inc(s("hT"), 1)
                a.wait_ge(s("xp_ps"), i + 1)
                reuse(a, s("rows_out"), i, 16)
                a.copy(rows[:, :, 0:HC], pt[:, 0:G, 256:256 + HC]).then_inc(s("xp"), 1)
            loop(a, NG, body)
    d.ph.close()


KNOT0, BASES, STEP = 4, 7, 0.25


def node_kan(c, T, W, table, node_table):
    H, C = 4, 32
    d = Dense(c, T, "kan", H, C)
    s, pt = d.s, d.pt
    w = d.sb("w", [P, 1 + BASES, 2 * P])
    b2 = d.sb("b2", [P, P])
    centres = d.sb("centres", [P, BASES])
    two = d.sb("two", [P, 1])
    one = d.sb("one", [P, 1])
    rden = d.sb("rden", [P, G, H])
    o = d.sb("o", [P, G, P])
    o2 = d.sb("o2", [P, G, P])
    x2 = d.sb("x2", [P, G, P])
    h = d.sb("h", [P, G, P])
    hT = d.sb("hT", [P, G, P])
    ex = d.sb("ex", [P, G, P])
    sig = d.sb("sig", [P, G, P])
    dist, far, near2, near1, square2, square1, cube2, cube1 = [
        d.sb(n, [P, 2, BASES, P]) for n in ("dist", "far", "near2", "near1", "square2", "square1", "cube2", "cube1")]
    feat = d.sb("feat", [P, G, 1 + BASES, P])
    both = d.sb("both", [P, G, 2 * P])
    with c.nc.Block() as block:
        @block.sync
        def _(sp):
            sp.dma_start(w[:], W["L2_w"]).then_inc(s("weights_in"), 16)
            sp.dma_start(b2[:], W["L1_b2"].partition_broadcast(P)).then_inc(s("weights_in"), 16)

            def body(i):
                sp.wait_ge(s("both"), i + 1)
                sp.dma_start(rows_of(table, i), both[:, :, 0:P]).then_inc(s("both_out"), 16)
                sp.dma_start(rows_of(node_table, i), both[:, :, P:2 * P]).then_inc(s("both_out"), 16)
            loop(sp, NG, body)
            sp.wait_ge(s("both_out"), 32 * NG)

        @block.vector
        def _(v):
            ch = Chain(v, s("dve"))
            ch.begin(0)
            v.memset(two[:], 2.0)
            v.memset(one[:], 1.0)
            for j in range(BASES):
                last = v.memset(centres[:, j:j + 1], -1.75 + STEP * (KNOT0 + j + 2))
            last.then_inc(s("centres"), 1)
            v.wait_ge(s("centres"), 1)
            v.wait_ge(s("weights_in"), 32)

            def body(i):
                ch.begin(i)
                acc = d.group(d.acc, i)
                v.nop(nofuse=True)
                ch.link(v.tensor_copy(rden[:], acc[:, :, :, C]))
                ch.link(v.reciprocal(rden[:], rden[:]))
                ch.link(v.tensor_tensor(o[:].rearrange("p g (h c) -> p g h c", h=H), acc[:, :, :, 0:C],
                                        bcast(rden[:], [P, G, H, C], 3), ALU.mult))
                ch.link(v.tensor_tensor(o2[:], o[:], bcast(b2[:], [P, G, P], 1), ALU.add))
                ch.link(v.tensor_tensor(x2[:], d.group(T.xs, i), o2[:], ALU.add))
                v.tensor_scalar(d.group(T.xs, i), x2[:], 1.0, None, ALU.mult)
                reuse(v, s("hT_ps"), i)
                reuse(v, s("hs"), i)
                d.norm_vector(v, ch, i, x2[:], h[:], "ln").then_inc(s("h"), 1)
                v.wait_ge(s("ex"), i + 1)
                ch.link(v.tensor_scalar(sig[:], ex[:], 1.0, None, ALU.add))
                ch.link(v.reciprocal(sig[:], sig[:]))
                reuse(v, s("both_ps"), i)
                ch.link(v.tensor_tensor(feat[:, :, 0, :], sig[:], hT[:], ALU.mult))

                def distances(j):
                    v.tensor_tensor(dist[:, j % 2], bcast(hT[:, j, :], [P, BASES, P], 1),
                                    bcast(centres[:], [P, BASES, P], 2), ALU.subtract).then_inc(s("dist"), 1)

                distances(0)
                distances(1)
                for j in range(G):
                    v.wait_ge(s("squares"), i * G + j + 1)
                    v.tensor_tensor(cube2[:, j % 2], square2[:, j % 2], near2[:, j % 2], ALU.mult)
                    ch.link(v.tensor_tensor(cube1[:, j % 2], square1[:, j % 2], near1[:, j % 2], ALU.mult))
                    v.tensor_tensor(feat[:, j, 1:1 + BASES, :], cube2[:, j % 2], cube1[:, j % 2], ALU.subtract
                                    ).then_inc(s("splines"), 1)
                    if j + 2 < G:
                        distances(j + 2)
            loop(v, NG, body)

        @block.tensor
        def _(pe):
            pe.wait_ge(s("weights_in"), 32)

            def body(i):
                pe.wait_ge(s("h"), i + 1)
                reuse(pe, s("hT"), i)
                for j in range(G):
                    last = pe.transpose(d.hT_slot(j), h[:, j, :], T.ident[:])
                last.then_inc(s("hT_ps"), 1)
                reuse(pe, s("both"), i)
                for j in range(G):
                    pe.wait_ge(s("splines"), i * G + j + 1)
                    for f in range(1 + BASES):
                        last = pe.matmul(pt[:, j, 0:2 * P], feat[:, j, f, :], w[:, f, :], start=(f == 0), stop=(f == BASES))
                last.then_inc(s("both_ps"), 1)
            loop(pe, NG, body)

        @block.scalar
        def _(a):
            ch = Chain(a, s("act"))

            def body(i):
                ch.begin(i)
                d.norm_scalar(a, i, "ln")
                a.wait_ge(s("h"), i + 1)
                a.copy(d.group(T.hs, i), h[:]).then_inc(s("hs"), 1)
                a.wait_ge(s("hT_ps"), i + 1)
                reuse(a, s("dist"), i, G)
                a.copy(hT[:, 0:4, :], pt[:, 5, :].rearrange("p (g n) -> p g n", g=4))
                a.copy(hT[:, 4, :], pt[:, 6, 0:P]).then_inc(s("hT"), 1)
                a.wait_ge(s("hT"), i + 1)
                a.activation(ex[:], hT[:], ACT.Exp, scale=-1.0).then_inc(s("ex"), 1)
                for j in range(G):
                    k = j % 2
                    a.wait_ge(s("dist"), i * G + j + 1)
                    if j >= 2:
                        a.wait_ge(s("splines"), i * G + j - 1)
                    else:
                        reuse(a, s("splines"), i, G)
                    ch.link(a.activation(far[:, k], dist[:, k], ACT.Abs, scale=1.0 / STEP))
                    a.activation(near2[:, k], far[:, k], ACT.Relu, bias=two[:], scale=-1.0)
                    ch.link(a.activation(near1[:, k], far[:, k], ACT.Relu, bias=one[:], scale=-1.0))
                    a.activation(square2[:, k], near2[:, k], ACT.Square, scale=6.0 ** -0.5)
                    a.activation(square1[:, k], near1[:, k], ACT.Square, scale=(4.0 / 6.0) ** 0.5).then_inc(s("squares"), 1)
                a.wait_ge(s("both_ps"), i + 1)
                reuse(a, s("both_out"), i, 32)
                a.copy(both[:], pt[:, 0:G, 0:2 * P]).then_inc(s("both"), 1)
            loop(a, NG, body)
    d.ph.close()


def node_after_kan(c, T, W, table, node_table):
    H, C = 4, 32
    d = Dense(c, T, "kan_out", H, C)
    s, pt = d.s, d.pt
    w = d.sb("w", [P, 3 * P])
    bias = d.sb("bias", [P, P])
    slope = d.sb("slope", [P, 1])
    den = d.sb("den", [P, G, H])
    rden = d.sb("rden", [P, G, H])
    o = d.sb("o", [P, G, P])
    o2 = d.sb("o2", [P, G, P])
    o3 = d.sb("o3", [P, G, P])
    x3 = d.sb("x3", [P, G, P])
    h = d.sb("h", [P, G, P])
    hT = d.sb("hT", [P, G, P])
    qvk = d.sb("qvk", [P, G, 3 * P])
    with c.nc.Block() as block:
        @block.sync
        def _(sp):
            sp.dma_start(w[:], W["L3_w"]).then_inc(s("weights_in"), 16)
            sp.dma_start(bias[:], W["L2_bias"].partition_broadcast(P)).then_inc(s("weights_in"), 16)
            sp.dma_start(slope[:], W["L2_prelu_a"].partition_broadcast(P)).then_inc(s("weights_in"), 16)

            def body(i):
                sp.wait_ge(s("qvk"), i + 1)
                sp.dma_start(rows_of(table, i), qvk[:, :, 0:2 * P]).then_inc(s("qvk_out"), 16)
                sp.dma_start(rows_of(node_table, i), qvk[:, :, 2 * P:3 * P]).then_inc(s("qvk_out"), 16)
            loop(sp, NG, body)
            sp.wait_ge(s("qvk_out"), 32 * NG)

        @block.vector
        def _(v):
            ch = Chain(v, s("dve"))
            v.wait_ge(s("weights_in"), 48)

            def body(i):
                ch.begin(i)
                acc = d.group(d.acc, i)
                ch.link(v.tensor_scalar(den[:], acc[:, :, :, C], 1e-16, None, ALU.add))
                ch.link(v.reciprocal(rden[:], den[:]))
                ch.link(v.tensor_tensor(o[:].rearrange("p g (h c) -> p g h c", h=H), acc[:, :, :, 0:C],
                                        bcast(rden[:], [P, G, H, C], 3), ALU.mult))
                ch.link(v.tensor_tensor(o2[:], o[:], d.group(T.hs, i), ALU.add))
                ch.link(v.tensor_tensor(o3[:], o2[:], bcast(bias[:], [P, G, P], 1), ALU.add))
                v.tensor_scalar(o[:], o3[:], 0.0, slope[:], ALU.min, ALU.mult)
                ch.link(v.tensor_scalar(o2[:], o3[:], 0.0, None, ALU.max))
                ch.link(v.tensor_tensor(o3[:], o[:], o2[:], ALU.add))
                ch.link(v.tensor_tensor(x3[:], d.group(T.xs, i), o3[:], ALU.add))
                v.tensor_scalar(d.group(T.xs, i), x3[:], 1.0, None, ALU.mult)
                reuse(v, s("hT_ps"), i)
                d.norm_vector(v, ch, i, x3[:], h[:], "ln").then_inc(s("h"), 1)
            loop(v, NG, body)

        @block.tensor
        def _(pe):
            pe.wait_ge(s("weights_in"), 48)

            def body(i):
                pe.wait_ge(s("h"), i + 1)
                reuse(pe, s("qvk"), i)
                for j in range(G):
                    last = pe.transpose(pt[:, j, 3 * P:4 * P], h[:, j, :], T.ident[:])
                last.then_inc(s("hT_ps"), 1)
                pe.wait_ge(s("hT"), i + 1)
                for j in range(G):
                    last = pe.matmul(pt[:, j, 0:3 * P], hT[:, j, :], w[:], start=True, stop=True)
                last.then_inc(s("qvk_ps"), 1)
            loop(pe, NG, body)

        @block.scalar
        def _(a):
            def body(i):
                d.norm_scalar(a, i, "ln")
                a.wait_ge(s("hT_ps"), i + 1)
                a.copy(hT[:], pt[:, 0:G, 3 * P:4 * P]).then_inc(s("hT"), 1)
                a.wait_ge(s("qvk_ps"), i + 1)
                reuse(a, s("qvk_out"), i, 32)
                a.copy(qvk[:], pt[:, 0:G, 0:3 * P]).then_inc(s("qvk"), 1)
            loop(a, NG, body)
    d.ph.close()


def node_out(c, T, out):
    H, C = 4, 32
    F = H * (C + 1)
    ph = Phase(c, "out")
    s = ph.sem
    den = ph.sb("den", [P, NB, H])
    rden = ph.sb("rden", [P, NB, H])
    o = ph.sb("o", [P, NB, P])
    res = ph.sb("res", [P, NB, P])
    acc = T.acc[:, 0:NB * F].rearrange("p (b h c) -> p b h c", h=H, c=C + 1)
    with c.nc.Block() as block:
        @block.vector
        def _(v):
            ch = Chain(v, s("dve"))
            ch.begin(0)
            ch.link(v.tensor_scalar(den[:], acc[:, :, :, C], 1e-9, None, ALU.max))
            ch.link(v.reciprocal(rden[:], den[:]))
            ch.link(v.tensor_tensor(o[:].rearrange("p b (h c) -> p b h c", h=H), acc[:, :, :, 0:C],
                                    bcast(rden[:], [P, NB, H, C], 3), ALU.mult))
            v.tensor_tensor(res[:], T.xs[:], o[:], ALU.add).then_inc(s("res"), 1)

        @block.sync
        def _(sp):
            sp.wait_ge(s("res"), 1)
            sp.dma_start(out[0:(NB - 1) * P, :].rearrange("(b p) f -> p b f", p=P), res[:, 0:NB - 1, :]
                         ).then_inc(s("stored"), 16)
            sp.dma_start(out[(NB - 1) * P:N, :], res[0:N - (NB - 1) * P, NB - 1, :]).then_inc(s("stored"), 16)
            sp.wait_ge(s("stored"), 32)
    ph.close()


def load_vec(c, T, name, dst, src):
    ph = Phase(c, name)
    s = ph.sem
    with c.nc.Block() as block:
        @block.sync
        def _(sp):
            sp.dma_start(dst[:], src.partition_broadcast(P)).then_inc(s("in"), 16)
            sp.wait_ge(s("in"), 16)
    ph.close()


class Tables:
    pass


def build(nc, A, out):
    c = Ctx(nc)
    T = Tables()
    T.ident = c.sb("ident", [P, P])
    T.ones = c.sb("ones", [1, P])
    T.iota256 = c.sb("iota256", [P, 2 * P])
    T.xs = c.sb("xs", [P, NB, P])
    T.hs = c.sb("hs", [P, NB, P])
    T.ixs = c.sb("ixs", [P, RT, ROW_IX], I32)
    T.mask = c.sb("mask", [P, RT * SLOTS])
    T.rel = c.sb("rel", [P, RT])
    T.blk = c.sb("blk", [1, RT], I32)
    T.pid = c.sb("pid", [P, 1])
    T.pen = c.sb("pen", [CT, NCH * P])
    T.pen_b = c.sb("pen_b", [CT, NCH * P])
    T.pen_pre = c.sb("pen_pre", [CT, NCH * P])
    T.pen_suf = c.sb("pen_suf", [CT, NCH * P])
    T.pen_tile = c.sb("pen_tile", [4, RT])
    T.pen_tile_b = c.sb("pen_tile_b", [4, RT])
    T.m = c.sb("m", [P, RT * 4])
    T.factor = c.sb("factor", [P, RT * 4])
    att = c.sb("att", [P, P])
    prepare(c, T, A["x"], A["chunk_ix"], A["dst_rows"])
    T.acc = c.sb("acc", [P, (NB + 1) * 322])

    tab = {w: c.dram(f"tab{w}", [NP_, w]) for w in (128, 136, 256, 264)}
    node = {w: c.dram(f"node{w}", [NP_, w]) for w in (128, 322)}
    def attention(name, H, C, src_w, node_w, kind, **kw):
        message_pass(c, T, name, H, C, src_w, node_w, tab[src_w], node.get(node_w), kind, **kw)

    node_in(c, T, A, tab[128], node[322])
    attention("conv", 2, 160, 128, 322, "conv", chunk_attr=A["chunk_attr"])
    node_after_conv(c, T, A, tab[264])
    attention("gat0", 4, 64, 264, 0, "gat")
    node_between_gats(c, T, A, "mid0", "L1_b0", "L1_W1", "L1_as1", "L1_ad1", 256, tab[264])
    attention("gat1", 4, 64, 264, 0, "gat")
    node_between_gats(c, T, A, "mid1", "L1_b1", "L1_W2", "L1_as2", "L1_ad2", 128, tab[136])
    attention("gat2", 4, 32, 136, 0, "gat")
    node_kan(c, T, A, tab[128], node[128])
    load_vec(c, T, "att_in", att, A["L2_double_attn"])
    attention("gatv2", 4, 32, 128, 128, "gatv2", vec=att)
    node_after_kan(c, T, A, tab[256], node[128])
    attention("dot", 4, 32, 256, 128, "dot")
    node_out(c, T, out)
    c.keep.close()


def arrange(inputs):
    a = {k: np.ascontiguousarray(v) for k, v in inputs.items()}
    src, dst = a["src"], a["dst"]
    src_c = np.zeros((CHUNKS * K,), src.dtype)
    src_c[:E] = src
    dst_c = np.full((CHUNKS * K,), NO_NODE, dst.dtype)
    dst_c[:E] = dst
    dst_r = np.full((EROWS * P,), NO_NODE, dst.dtype)
    dst_r[:E] = dst
    ea = np.zeros((CHUNKS * K, 32), a["edge_attr_32"].dtype)
    ea[:E] = a["edge_attr_32"]
    heads2 = lambda w: w.reshape(2, P, -1).transpose(1, 0, 2)
    out = {"x": a["x"],
           "chunk_ix": np.concatenate([src_c.reshape(CHUNKS, K), dst_c.reshape(CHUNKS, K)], axis=1),
           "dst_rows": dst_r.reshape(EROWS, P),
           "chunk_attr": ea.reshape(CHUNKS, K * 32),
           "L0_WqT": a["L0_gnn_Wq"].T, "L0_bq": a["L0_gnn_bq"].reshape(2, P).T,
           "L0_kx": np.concatenate([heads2(a["L0_gnn_Wk"]), heads2(a["L0_gnn_We"]),
                                    heads2(a["L0_gnn_bk"].reshape(-1, 1))], axis=2),
           "L0_WvT": a["L0_gnn_Wv"].T,
           "L0_web": np.concatenate([a["L0_gnn_We"].T.reshape(32, 2, P), a["L0_gnn_bv"].reshape(1, 2, P)], axis=0),
           "L0_WskipT": a["L0_gnn_Wskip"].T, "L0_bskip": a["L0_gnn_bskip"].reshape(1, P),
           "L0_W1T": a["L0_gnn_W1"].T, "L0_b1": a["L0_gnn_b1"].reshape(2, P).T,
           "L0_W2T": a["L0_gnn_W2"].T.reshape(2, P, P).transpose(1, 0, 2), "L0_b2": a["L0_gnn_b2"].reshape(1, P),
           "L0_ln1_g": a["L0_gnn_ln1_g"], "L0_ln1_b": a["L0_gnn_ln1_b"],
           "L0_ln2_g": a["L0_gnn_ln2_g"], "L0_ln2_b": a["L0_gnn_ln2_b"],
           "L1_W0": a["L1_gnn_W0"], "L1_as0": a["L1_gnn_as0"].reshape(-1), "L1_ad0": a["L1_gnn_ad0"].reshape(-1),
           "L1_b0": a["L1_gnn_b0"],
           "L1_W1": a["L1_gnn_W1"].reshape(2, P, 256).transpose(1, 0, 2),
           "L1_as1": a["L1_gnn_as1"].reshape(-1), "L1_ad1": a["L1_gnn_ad1"].reshape(-1), "L1_b1": a["L1_gnn_b1"],
           "L1_W2": a["L1_gnn_W2"].reshape(2, P, P).transpose(1, 0, 2),
           "L1_as2": a["L1_gnn_as2"].reshape(-1), "L1_ad2": a["L1_gnn_ad2"].reshape(-1), "L1_b2": a["L1_gnn_b2"],
           "L2_double_attn": a["L2_gnn_double_attn"].reshape(-1), "L2_bias": a["L2_gnn_bias"],
           "L2_prelu_a": a["L2_gnn_prelu_a"].reshape(1),
           "L3_w": np.concatenate([a[f"L3_gnn_{n}"].transpose(1, 0, 2).reshape(P, P) for n in ("Wq", "Wv", "Wk")], axis=1)}
    kan = []
    for side in ("src", "dst"):
        sw = a[f"L2_gnn_spline_w_{side}"].transpose(1, 2, 0)[:, KNOT0:KNOT0 + BASES, :]
        kan.append(np.concatenate([a[f"L2_gnn_base_w_{side}"].T[:, None, :], sw], axis=1))
    out["L2_w"] = np.concatenate(kan, axis=2)
    return {k: np.ascontiguousarray(v) for k, v in out.items()}


def kernel(**inputs):
    import concourse.bacc as bacc
    from concourse.bass_utils import run_bass_kernel_spmd as run

    nc = bacc.Bacc("TRN2", target_bir_lowering=False, num_devices=1)
    arrays = {f"in_{k}": v for k, v in arrange(inputs).items()}
    A = {k[3:]: nc.dram_tensor(k, v.shape, mybir.dt.from_np(v.dtype), kind="ExternalInput").ap()
         for k, v in arrays.items()}
    out = nc.dram_tensor("out_x", (N, P), F32, kind="ExternalOutput").ap()
    build(nc, A, out)
    return run(nc, [arrays], core_ids=[0]).results[0]["out_x"]
```

```python
from contextlib import ExitStack

import numpy as np
import concourse.bass as bass
from concourse import mybir

F32 = mybir.dt.float32
I32 = mybir.dt.int32
ALU = mybir.AluOpType
ACT = mybir.ActivationFunctionType
X = mybir.AxisListType.X

P = 128
N = 3125
E = 103125
K = 8
CHUNKS = -(-E // K)
SLOTS = K + 1
EROWS = -(-E // P)
NB = -(-N // P)
NP_ = NB * P
RT = -(-(CHUNKS + N - 1) // P)
ROWS = RT * P
NO_NODE = 8191
G = 5
NG = NB // G
NEG = -1e30
LOW = -1e38
NEG_SLOPE = 0.2
ROW_IX = K + 2
UC = 6
U = 3
CT = 18
NCH = RT // CT
S = CT // U
assert RT % CT == 0 and CT % U == 0 and U == 3
assert RT % UC == 0 and NB % G == 0 and RT % U == 0


class Ctx:

    def __init__(self, nc):
        self.nc = nc
        self.keep = ExitStack()
        self.gather_sems = {n: self.keep.enter_context(nc.semaphore(n)) for n in
                            ["dsts_in", "marked"] + [f"got{b}" for b in range(UC)] + [f"gathered{b}" for b in range(U)]}

    def sb(self, name, shape, dt=F32, stack=None):
        return (stack or self.keep).enter_context(self.nc.sbuf_tensor(name, shape, dt))

    def dram(self, name, shape, dt=F32):
        return self.nc.dram_tensor(name, shape, dt, kind="Internal").ap()


class Phase:

    def __init__(self, c, name):
        self.c, self.nc, self.name = c, c.nc, name
        self.stack = ExitStack()
        self.sems = {}

    def sem(self, name):
        if name in self.c.gather_sems:
            self.sems[name] = self.c.gather_sems[name]
        if name not in self.sems:
            self.sems[name] = self.stack.enter_context(self.nc.semaphore(f"{self.name}_{name}"))
        return self.sems[name]

    def sb(self, name, shape, dt=F32):
        return self.stack.enter_context(self.nc.sbuf_tensor(f"{self.name}_{name}", shape, dt))

    def ps(self, name, shape, dt=F32):
        return self.stack.enter_context(self.nc.psum_tensor(f"{self.name}_{name}", shape, dt))

    def close(self):
        used = [s for n, s in self.sems.items() if n in self.c.gather_sems]
        if used:
            self.nc.gpsimd.dma_reset(range(min(x.num for x in used), max(x.num for x in used) + 1))
        for sem in self.sems.values():
            self.nc.gpsimd.sem_clear(sem)
        self.nc.all_engine_barrier()
        self.stack.close()


class Chain:

    def __init__(self, eng, sem, steps=None):
        self.eng, self.sem, self.steps, self.k, self.base, self.first = eng, sem, steps, 0, 0, steps is None
        self.fixed = steps is not None

    def begin(self, i):
        if self.fixed:
            assert self.k in (0, self.steps), self.k
            self.base = i * self.steps
        elif isinstance(i, int):
            self.base, self.first = 0, True
        else:
            if self.first:
                self.steps = self.k
            self.base, self.first = i * self.steps, False
        self.k = 0

    def link(self, ins):
        self.k += 1
        ins.then_inc(self.sem, 1)
        self.eng.wait_ge(self.sem, self.base + self.k)


def loop(eng, n, body):
    body(0)
    if n > 1:
        with eng.Fori(1, n) as i:
            body(i)


def reuse(eng, sem, i, per_step=1):
    if not (isinstance(i, int) and i == 0):
        eng.wait_ge(sem, i * per_step)


def bcast(ap, shape, axis):
    return ap.unsqueeze(axis).to_broadcast(shape)


def prepare(c, T, x_in, chunk_ix, dst_rows, W, table, node_table):
    nc = c.nc
    ph = Phase(c, "prep")
    s = ph.sem
    i_col = ph.sb("i_col", [P, NB], I32)
    i_256 = ph.sb("i_256", [P, 2 * P], I32)
    i_row = ph.sb("i_row", [RT, P], I32)
    nid = ph.sb("nid", [P, NB])
    rowid = ph.sb("rowid", [RT, P])
    heads_i = ph.sb("heads_i", [P, EROWS], I32)
    heads = ph.sb("heads", [P, EROWS])
    junk = ph.sb("junk", [P, EROWS])
    before = ph.sb("before", [P, NB])
    tile_f = ph.sb("tile_f", [P, NB])
    tile_i = ph.sb("tile_i", [P, NB], I32)
    dsts = ph.sb("dsts", [P, NB, P], I32)
    less = ph.sb("less", [P, NB, P])
    inside = ph.sb("inside", [P, NB])
    start = ph.sb("start", [P, NB])
    startT = ph.sb("startT", [NB, P])
    nextT = ph.sb("nextT", [NB, P])
    fullE = ph.sb("fullE", [1, P])
    zeros = ph.sb("zeros", [P, 2 * P])
    qi = ph.sb("qi", [NB, 2, P], I32)
    q = ph.sb("q", [NB, 2, P])
    row_count = ph.sb("row_count", [NB, P])
    onesT = ph.sb("onesT", [RT, P])
    rp = ph.sb("rp", [NB, P])
    last_rp = ph.sb("last_rp", [NB, 1])
    upper = ph.sb("upper", [NB, NB])
    carry = ph.sb("carry", [NB, 1])
    first_row = ph.sb("first_row", [NB, P])
    offT = ph.sb("offT", [NB, P])
    rp_i = ph.sb("rp_i", [P, NB], I32)
    mark = ph.sb("mark", [P, NB, 2])
    marks = ph.sb("marks", [RT, P, 2])
    run = ph.sb("run", [RT, 2, P])
    lastT = ph.sb("lastT", [2, RT])
    runT = ph.sb("runT", [2, RT + 1])
    tile_run = ph.sb("tile_run", [RT, 2])
    both = ph.sb("both", [RT, 2, P])
    chunk = ph.sb("chunk", [RT, P])
    new = ph.sb("new", [RT, P])
    blk_i = ph.sb("blk_i", [RT, 1], I32)
    nfirst_i = ph.sb("nfirst_i", [RT, 1], I32)
    blk = ph.sb("blk", [RT, 1])
    blk128 = ph.sb("blk128", [RT, 1])
    relT = ph.sb("relT", [RT, P])
    rel_far = ph.sb("rel_far", [RT, P])
    later = ph.sb("later", [RT, P])
    n_col = ph.sb("n_col", [P, RT])
    shift = ph.sb("shift", [RT, RT])
    pen, pen_b, pen_pre, pen_suf = [ph.sb(n, [RT, P]) for n in ("pen", "pen_b", "pen_pre", "pen_suf")]
    pen_r = ph.sb("pen_r", [RT, P])
    d_pen = c.dram("d_pen", [4, RT, P])
    stage = ph.sb("stage", [P, UC, 1], I32)
    got = ph.sb("got", [P, UC, 2 * K], I32)
    differs = ph.sb("differs", [P, UC, K])
    pt = ph.ps("pt", [P, 8, 512])
    node_in = NodeIn(c, T, ph, pt, W, table, node_table)
    d_heads = c.dram("d_heads", [EROWS], I32)
    d_start = c.dram("d_start", [NP_ + P])
    d_mark = c.dram("d_mark", [ROWS, 2])

    with nc.Block() as block:
        @block.gpsimd
        def _(g):
            g.iota(i_col[:], [[P, NB]], base=0, channel_multiplier=1).then_inc(s("iotas"), 1)
            g.iota(i_256[:], [[1, 2 * P]], base=0, channel_multiplier=0).then_inc(s("iotas"), 1)
            g.iota(i_row[:], [[1, P]], base=0, channel_multiplier=P).then_inc(s("iotas"), 1)
            g.memset(T.ident[:], 0.0).then_inc(s("blank"), 1)
            g.memset(upper[:], 1.0).then_inc(s("blank"), 1)
            g.wait_ge(s("blank"), 2)
            g.affine_select(out=T.ident[:], in_=T.ident[:], compare_op=ALU.not_equal, fill=1.0, base=0,
                            pattern=[[-1, P]], channel_multiplier=1).then_inc(s("masks"), 1)
            g.affine_select(out=upper[:], in_=upper[:], compare_op=ALU.is_gt, fill=0.0, base=0,
                            pattern=[[1, NB]], channel_multiplier=-1).then_inc(s("masks"), 1)
            g.wait_ge(s("tile_ready"), 1)
            for b in range(NB):
                g.indirect_dma_start(out=dsts[:, b, :], out_offset=None, in_=dst_rows[:, :],
                                     in_offset=bass.IndirectOffsetOnAxis(ap=tile_i[:, b:b + 1], axis=0)
                                     ).then_inc(s("dsts_in"), 16)
            g.wait_ge(s("marks_blank"), 16)
            g.wait_ge(s("marks_ready"), 2)
            for b in range(NB):
                g.indirect_dma_start(out=d_mark[:, :], in_=mark[:, b, :], in_offset=None,
                                     out_offset=bass.IndirectOffsetOnAxis(ap=rp_i[:, b:b + 1], axis=0)
                                     ).then_inc(s("marked"), 16)

            def chunks(i):
                for b in range(UC):
                    reuse(g, s(f"diff{b}"), i)
                    reuse(g, s(f"kept{b}"), i)
                    g.wait_ge(s(f"stage_ready{b}"), i + 1)
                    g.nop(nofuse=True)
                    g.indirect_dma_start(out=got[:, b, :], out_offset=None, in_=chunk_ix[:, :],
                                         in_offset=bass.IndirectOffsetOnAxis(ap=stage[:, b, :], axis=0)
                                         ).then_inc(s(f"got{b}"), 16)
            loop(g, RT // UC, chunks)

        @block.sync
        def _(sp):
            sp.dma_start(d_heads.unsqueeze(1), dst_rows[:, 0:1], allow_slow_non_contiguous=True).then_inc(s("heads_out"), 16)
            sp.wait_ge(s("heads_out"), 16)
            sp.dma_start(heads_i[:], d_heads.partition_broadcast(P)).then_inc(s("heads_in"), 16)
            node_in.weights(sp)
            sp.wait_ge(s("x_pad"), 1)
            sp.dma_start(T.xs[:, 0:NB - 1, :],
                         x_in[0:(NB - 1) * P, :].rearrange("(b p) f -> p b f", p=P)).then_inc(s("x_in"), 16)
            sp.dma_start(T.xs[0:N - (NB - 1) * P, NB - 1, :], x_in[(NB - 1) * P:N, :]).then_inc(s("x_in"), 16)
            sp.wait_ge(s("zeros"), 1)
            sp.dma_start(d_mark.rearrange("(t p) o -> t (p o)", p=P), zeros[0:RT, :]).then_inc(s("marks_blank"), 16)
            sp.wait_ge(s("startT"), 1)
            sp.dma_start(d_start[0:NP_].rearrange("(b p) -> b p", p=P), startT[:]).then_inc(s("start_out"), 16)
            sp.dma_start(d_start[NP_:NP_ + P].unsqueeze(0), fullE[:]).then_inc(s("start_out"), 16)
            sp.wait_ge(s("start_out"), 32)
            sp.dma_start(nextT[:], d_start[1:NP_ + 1].rearrange("(b p) -> b p", p=P)).then_inc(s("next_in"), 16)
            sp.wait_ge(s("marked"), NB * 16)
            sp.dma_start(marks[:], d_mark.rearrange("(t p) o -> t p o", p=P)).then_inc(s("marks_in"), 16)
            sp.wait_ge(s("x_in"), 32)
            sp.wait_ge(s("rel_far"), 1)
            sp.dma_start(T.d_rel[0:RT, 0:P], relT[:]).then_inc(s("rel_out"), 16)
            sp.dma_start(T.d_rel[0:RT, P:], rel_far[:]).then_inc(s("rel_out"), 16)
            sp.dma_start(T.d_rel[RT:, :], zeros[0:U, :]).then_inc(s("rel_out"), 16)
            sp.wait_ge(s("rel_out"), 48)
            sp.wait_ge(s("pens2"), 1)
            for m, own in enumerate((pen, pen_r, pen_pre, pen_suf)):
                sp.dma_start(d_pen[m], own[:]).then_inc(s("pen_out"), 16)
            sp.wait_ge(s("pen_out"), 64)
            for m, kept in enumerate((T.pen, T.pen_b, T.pen_pre, T.pen_suf)):
                sp.dma_start(kept[:].rearrange("t (c p) -> t c p", p=P), d_pen[m].rearrange("(c t) p -> t c p", t=CT)
                             ).then_inc(s("pen_in"), 16)
            sp.wait_ge(s("pen_in"), 64)

        @block.tensor
        def _(pe):
            pe.wait_ge(s("masks"), 2)
            pe.wait_ge(s("weights_in"), 48)
            node_in.tensor(pe, 0)
            node_in.tensor(pe, 1)
            pe.wait_ge(s("start"), 1)
            pe.transpose(pt[0:NB, 0, 0:P], start[:], T.ident[:]).then_inc(s("startT_ps"), 1)
            pe.wait_ge(s("rows_summed"), 1)
            pe.matmul(pt[0:NB, 1, 0:1], upper[:], last_rp[:], start=True, stop=True).then_inc(s("carry_ps"), 1)
            pe.wait_ge(s("first_row"), 2)
            pe.transpose(pt[:, 2, 0:NB], first_row[:], T.ident[0:NB, 0:NB]).then_inc(s("first_ps"), 1)
            pe.transpose(pt[:, 3, 0:NB], offT[:], T.ident[0:NB, 0:NB]).then_inc(s("first_ps"), 1)
            node_in.tensor(pe, 2)
            node_in.tensor(pe, 3)
            pe.wait_ge(s("run"), 2)
            pe.transpose(pt[0:2, 4, 0:RT], tile_run[:], T.ident[0:RT, 0:RT]).then_inc(s("lastT_ps"), 1)
            pe.wait_ge(s("runT"), 1)
            pe.transpose(pt[0:RT, 5, 0:2], runT[:, 0:RT], T.ident[0:2, 0:2]).then_inc(s("carry2_ps"), 1)
            pe.wait_ge(s("row_cols"), 1)
            pe.transpose(pt[:, 0, 0:RT], both[:, 0, :], T.ident[0:RT, 0:RT]).then_inc(s("cols_ps"), 1)
            pe.transpose(pt[:, 1, 0:RT], chunk[:], T.ident[0:RT, 0:RT]).then_inc(s("cols_ps"), 1)
            pe.transpose(pt[:, 2, 0:RT], relT[:], T.ident[0:RT, 0:RT]).then_inc(s("cols_ps"), 1)
            pe.transpose(pt[0:1, 3, 0:RT], blk[:], T.ident[0:RT, 0:RT]).then_inc(s("cols_ps"), 1)
            pe.wait_ge(s("pens"), 1)
            pe.transpose(pt[:, 4, P:P + RT], later[:], T.ident[0:RT, 0:RT]).then_inc(s("pen_ps"), 1)
            pe.matmul(pt[0:RT, 5, 0:1], shift[:], pen[:, 0:1], start=True, stop=True).then_inc(s("pen_ps"), 1)
            pe.wait_ge(s("pens2"), 1)
            pe.matmul(pt[0:4, 6, 0:RT], pen_pre[:, P - 1:P].to_broadcast([RT, 4]), T.ident[0:RT, 0:RT],
                      start=True, stop=True).then_inc(s("pen2_ps"), 1)
            pe.matmul(pt[0:4, 7, 0:RT], pen_suf[:, 0:1].to_broadcast([RT, 4]), T.ident[0:RT, 0:RT],
                      start=True, stop=True).then_inc(s("pen2_ps"), 1)
            node_in.tensor(pe, 4)

        @block.vector
        def _(v):
            ch = Chain(v, s("dve"))
            ch.begin(0)
            v.memset(T.xs[:, NB - 1, :], 0.0).then_inc(s("x_pad"), 1)
            v.memset(zeros[:], 0.0).then_inc(s("zeros"), 1)
            v.memset(T.ones[:], 1.0)
            v.memset(fullE[:], float(E))
            v.memset(runT[:, 0:1], 0.0)
            ch.link(v.memset(onesT[:], 1.0))
            v.wait_ge(s("iotas"), 3)
            v.tensor_copy(nid[:], i_col[:])
            v.tensor_copy(T.iota256[:], i_256[:])
            v.tensor_copy(T.pid[:], i_col[:, 0:1])
            v.tensor_copy(rowid[:], i_row[:])
            v.wait_ge(s("masks"), 2)
            v.memset(shift[:], 0.0)
            v.wait_ge(s("heads_in"), 16)
            ch.link(v.tensor_copy(heads[:], heads_i[:]))
            v.tensor_copy(shift[:, 0:RT - 1], T.ident[0:RT, 1:RT])
            for b in range(NB):
                ch.link(v.tensor_scalar(junk[:], heads[:], nid[:, b:b + 1], 0.0, ALU.is_lt, ALU.add,
                                        accum_out=before[:, b:b + 1]))
            ch.link(v.tensor_scalar(tile_f[:], before[:], -1.0, 0.0, ALU.add, ALU.max))
            v.tensor_copy(tile_i[:], tile_f[:]).then_inc(s("tile_ready"), 1)
            in_ch = Chain(v, s("dve_in"))
            v.wait_ge(s("x_in"), 32)
            v.wait_ge(s("weights_in"), 48)
            node_in.vector(v, in_ch, 0)
            node_in.vector(v, in_ch, 1)
            v.wait_ge(s("dsts_in"), NB * 16)
            ch.link(v.tensor_tensor(less[:], dsts[:], bcast(nid[:], [P, NB, P], 2), ALU.is_lt))
            ch.link(v.tensor_reduce(inside[:], less[:], X, ALU.add))
            v.scalar_tensor_tensor(start[:], tile_f[:], float(P), inside[:], ALU.mult, ALU.add
                                   ).then_inc(s("start"), 1)
            v.wait_ge(s("startT_ps"), 1)
            v.tensor_copy(startT[:], pt[0:NB, 0, 0:P]).then_inc(s("startT"), 1)
            v.wait_ge(s("next_in"), 16)
            v.wait_ge(s("startT"), 1)
            v.tensor_copy(qi[:, 0, :], startT[:])
            ch.link(v.tensor_scalar(q[:, 1, :], nextT[:], -1.0, None, ALU.add))
            ch.link(v.tensor_copy(qi[:, 1, :], q[:, 1, :]))
            ch.link(v.tensor_single_scalar(qi[:], qi[:], K.bit_length() - 1, ALU.arith_shift_right))
            ch.link(v.tensor_copy(q[:], qi[:]))
            ch.link(v.tensor_tensor(row_count[:], q[:, 1, :], q[:, 0, :], ALU.subtract))
            ch.link(v.tensor_scalar(row_count[:], row_count[:], 1.0, None, ALU.add))
            ch.link(v.tensor_tensor_scan(rp[:], onesT[0:NB, :], row_count[:], 0.0, ALU.mult, ALU.add))
            v.tensor_copy(last_rp[:], rp[:, P - 1:P]).then_inc(s("rows_summed"), 1)
            ch.link(v.tensor_tensor(first_row[:], rp[:], row_count[:], ALU.subtract))
            v.wait_ge(s("carry_ps"), 1)
            ch.link(v.tensor_copy(carry[:], pt[0:NB, 1, 0:1]))
            v.tensor_scalar(first_row[:], first_row[:], carry[:], None, ALU.add).then_inc(s("first_row"), 1)
            v.wait_ge(s("first_row"), 1)
            v.tensor_tensor(offT[:], first_row[:], q[:, 0, :], ALU.subtract).then_inc(s("first_row"), 1)
            v.wait_ge(s("first_ps"), 2)
            v.tensor_copy(rp_i[:], pt[:, 2, 0:NB]).then_inc(s("marks_ready"), 1)
            v.tensor_copy(mark[:, :, 0], nid[:])
            v.tensor_copy(mark[:, :, 1], pt[:, 3, 0:NB]).then_inc(s("marks_ready"), 1)
            node_in.vector(v, in_ch, 2)
            node_in.vector(v, in_ch, 3)
            v.wait_ge(s("marks_in"), 16)
            for m in range(2):
                ch.link(v.tensor_tensor_scan(run[:, m, :], marks[:, :, m], marks[:, :, m], 0.0, ALU.max, ALU.max))
            v.tensor_copy(tile_run[:], run[:, :, P - 1]).then_inc(s("run"), 2)
            v.wait_ge(s("lastT_ps"), 1)
            ch.link(v.tensor_copy(lastT[:], pt[0:2, 4, 0:RT]))
            v.tensor_tensor_scan(runT[:, 1:RT + 1], lastT[:], lastT[:], 0.0, ALU.max, ALU.max
                                 ).then_inc(s("runT"), 1)
            v.wait_ge(s("carry2_ps"), 1)
            v.wait_ge(s("run"), 2)
            ch.link(v.tensor_copy(tile_run[:], pt[0:RT, 5, 0:2]))
            for m in range(2):
                ch.link(v.tensor_scalar(both[:, m, :], run[:, m, :], tile_run[:, m:m + 1], None, ALU.max))
            ch.link(v.tensor_tensor(chunk[:], rowid[:], both[:, 1, :], ALU.subtract))
            v.tensor_scalar(chunk[:], chunk[:], float(CHUNKS - 1), 0.0, ALU.min, ALU.max)
            v.tensor_tensor(new[:, 1:P], both[:, 0, 1:P], both[:, 0, 0:P - 1], ALU.not_equal)
            v.tensor_scalar(new[:, 0:1], both[:, 0, 0:1], tile_run[:, 0:1], None, ALU.not_equal)
            ch.link(v.tensor_copy(nfirst_i[:], both[:, 0, 0:1]))
            ch.link(v.tensor_single_scalar(blk_i[:], nfirst_i[:], 7, ALU.arith_shift_right))
            ch.link(v.tensor_copy(blk[:], blk_i[:]))
            ch.link(v.tensor_scalar(blk128[:], blk[:], float(P), None, ALU.mult))
            v.tensor_scalar(relT[:], both[:, 0, :], blk128[:], None, ALU.subtract).then_inc(s("row_cols"), 1)
            v.wait_ge(s("row_cols"), 1)
            v.tensor_scalar(rel_far[:], relT[:], -float(P), None, ALU.add).then_inc(s("rel_far"), 1)
            ch.link(v.memset(new[0:1, 0:1], 1.0))
            ch.link(v.tensor_scalar(pen[:], new[:], LOW, None, ALU.mult))
            v.tensor_scalar(later[:], new[:], 0.0, NEG, ALU.is_equal, ALU.mult).then_inc(s("pens"), 1)
            v.wait_ge(s("cols_ps"), 4)
            ch.link(v.tensor_copy(n_col[:], pt[:, 0, 0:RT]))
            v.tensor_copy(T.ixs[:, :, K], n_col[:])
            v.tensor_copy(T.ixs[:, :, K + 1], pt[:, 1, 0:RT]).then_inc(s("chunk_ix"), 1)
            v.tensor_copy(T.rel[:], pt[:, 2, 0:RT])
            v.tensor_copy(T.blk[:, 0:RT], pt[0:1, 3, 0:RT])
            v.memset(T.blk[:, RT:], 0)
            v.wait_ge(s("pen_ps"), 2)
            v.tensor_copy(pen_b[:, P - 1:P], pt[0:RT, 5, 0:1])
            v.tensor_copy(T.mask[:].rearrange("p (t k) -> p t k", k=SLOTS)[:, :, K], pt[:, 4, P:P + RT])
            v.wait_ge(s("pens"), 1)
            ch.link(v.tensor_copy(pen_b[:, 0:P - 1], pen[:, 1:P]))
            v.tensor_tensor_scan(pen_pre[:], pen[:], pen[:], 0.0, ALU.min, ALU.min)
            back = pen_b[:, ::-1]
            v.tensor_copy(pen_r[:], back)
            v.tensor_tensor_scan(pen_suf[:, ::-1], back, back, 0.0, ALU.min, ALU.min).then_inc(s("pens2"), 1)
            v.wait_ge(s("pen2_ps"), 2)
            v.tensor_copy(T.pen_tile[:], pt[0:4, 6, 0:RT])
            ch.link(v.tensor_copy(T.pen_tile_b[:].rearrange("h (c t) -> h c t", t=CT)[:, :, ::-1],
                                  pt[0:4, 7, 0:RT].rearrange("h (c t) -> h c t", t=CT)))

            node_in.vector(v, in_ch, 4)

            prep_k = ch.k

            def masks(i):
                for b in range(UC):
                    t = i * UC + b
                    v.wait_ge(s(f"got{b}"), 16 * i + 16)
                    if not isinstance(i, int):
                        v.wait_ge(s(f"mask{b}"), i)
                    v.tensor_scalar(differs[:, b, :], got[:, b, K:2 * K], n_col[:, bass.ds(t, 1)], None,
                                    ALU.not_equal).then_inc(s(f"diff{b}"), 1)
                    v.wait_ge(s(f"diff{b}"), i + 1)
                    v.tensor_scalar(T.mask[:, bass.ds(t * SLOTS, K)], differs[:, b, :], NEG, None, ALU.mult
                                    ).then_inc(s(f"mask{b}"), 1)
            loop(v, RT // UC, masks)

        @block.scalar
        def _(a):
            for i in range(NG):
                node_in.scalar(a, i)
            a.wait_ge(s("chunk_ix"), 1)

            def copies(i):
                for b in range(UC):
                    t = i * UC + b
                    reuse(a, s(f"got{b}"), i, 16)
                    a.copy(stage[:, b, :], T.ixs[:, bass.ds(t, 1), K + 1]).then_inc(s(f"stage_ready{b}"), 1)
                for b in range(UC):
                    t = i * UC + b
                    a.wait_ge(s(f"got{b}"), 16 * i + 16)
                    a.copy(T.ixs[:, bass.ds(t, 1), 0:K], got[:, b, 0:K].unsqueeze(1)).then_inc(s(f"kept{b}"), 1)
            loop(a, RT // UC, copies)
            a.wait_ge(s("h_out"), 16 * NG)
            a.wait_ge(s("td_out"), 16 * NG)
    ph.close()


def message_pass(c, T, name, H, C, src_w, node_w, table, node_table, kind, chunk_attr=None, vec=None):
    nc = c.nc
    ph = Phase(c, name)
    s = ph.sem
    F = H * (C + 1)
    FEAT = 128
    expand = kind != "conv"
    wide = 2 * F > 512
    halve = kind == "gat" and wide
    gathers = K + (not expand) + (kind == "conv")
    KS = SLOTS if kind == "gat" else K
    ix = ph.sb("ix", [P, U, ROW_IX], I32)
    src = ph.sb("src", [P, U, KS, src_w])
    node = ph.sb("node", [P, U, node_w]) if kind != "gat" else None
    attr = ph.sb("attr", [P, U, K * 32]) if kind == "conv" else None
    prod_w = {"conv": H * C, "gat": 1, "gatv2": H * C, "dot": H * C}[kind]
    prod = ph.sb("prod", [P, KS, prod_w])
    act = ph.sb("act", [P, K, prod_w]) if kind == "gatv2" else None
    raw = ph.sb("raw", [P, KS, H])
    lg = ph.sb("lg", [P, KS, H])
    top = ph.sb("top", [P, U, H])
    low = ph.sb("low", [P, U, KS, H])
    msg = ph.sb("msg", [P, U, KS, H, C + 1])
    ring = ph.sb("ring", [P, CT, F])
    scaled = ph.sb("scaled", [P, U, F])
    onehot = ph.sb("onehot", [P, U, 2 * P])
    gap = ph.sb("gap", [P, CT, H])
    mh = ph.sb("mh", [P, H, CT])
    fwd, bwd = ph.sb("fwd", [CT, H, P]), ph.sb("bwd", [CT, H, P])
    full, whole = fwd, bwd
    edge = ph.sb("edge", [CT, 2, H])
    edgeT = ph.sb("edgeT", [H, 2, CT])
    runs = ph.sb("runs", [H, 2, CT + 1])
    into = ph.sb("into", [CT, 2, H])
    delta = ph.sb("delta", [1, H + 1])
    chosen = ph.sb("chosen", [P, 1])
    shrink_log = ph.sb("shrink_log", [P, H])
    shrink = ph.sb("shrink", [P, H])
    top1 = ph.sb("top1", [P, 1])
    largest = ph.sb("largest", [1, 2])
    sums_ps = ph.ps("sums_ps", [P, U, 512])
    if expand:
        own_w = src_w if kind == "gat" else node_w
        own_table = table if kind == "gat" else node_table
        nodes_sb = ph.sb("nodes_sb", [P, NB + 1, own_w])
        spare = T.acc[:, (NB + 1) * F:(NB + 1) * F + 4 * U * P].rearrange("p (m u n) -> p m u n", m=2, u=U)
        rel_rows, pick = spare[:, 0], spare[:, 1]
        merge_ps = ph.ps("merge_ps", [P, 4, 512])
        nodes_ps = merge_ps[:, 2:4, :]
    else:
        merge_ps = ph.ps("merge_ps", [P, 4, 512])

    def merge_pair(b, tail):
        if not wide:
            return merge_ps[:, b % 2, 0:2 * F].rearrange("p (o f) -> p o f", f=F)
        if expand and not tail:
            return merge_ps[:, 0:2, 0:F]
        return merge_ps[:, 2 * (b % 2):2 * (b % 2) + 2, 0:F]

    mx_ps = ph.ps("mx_ps", [P, 512])
    acc = T.acc[:, 0:(NB + 1) * F].rearrange("p (b f) -> p b f", f=F)
    whole_max = kind == "gatv2"

    def all_chunks(eng, edges, maxima, merge_only):
        edges(0, 0, None)
        with eng.Fori(1, S) as j:
            edges(j, j, None)
        with eng.Fori(1, NCH) as ch:
            maxima(ch - 1)
            edges(ch * S, 0, (ch - 1) * S)
            with eng.Fori(1, S) as j:
                edges(ch * S + j, j, (ch - 1) * S + j)
        maxima(NCH - 1)
        with eng.Fori(0, S) as j:
            merge_only((NCH - 1) * S + j, j)

    def gather_steps(eng, body):
        body(0)
        with eng.Fori(1, RT // U) as i:
            body(i)

    with nc.Block() as block:
        @block.sync
        def _(sp):
            def body(i):
                for b in range(U):
                    reuse(sp, s(f"gathered{b}"), i, 16 * gathers)
                    sp.dma_start(ix[:, b, :], T.ixs[:, bass.ds(i * U + b, 1), :].rearrange("p o k -> p (o k)")
                                 ).then_inc(s(f"ix_in{b}"), 16)
                    if expand:
                        rel_in(i + 1, b)

            def rel_in(n, b):
                reuse(sp, s(f"pick{b}"), n)
                sp.dma_start(rel_rows[:, b, :], T.d_rel[bass.ds(n * U + b, 1), :].rearrange("o n -> (o n)")
                             .partition_broadcast(P)).then_inc(s(f"rel_in{b}"), 16)

            if expand:
                for b in range(U):
                    rel_in(0, b)
                sp.dma_start(nodes_sb[:, 0:NB, :], own_table.rearrange("(b p) w -> p b w", p=P)
                             ).then_inc(s("nodes_in"), 16)
            gather_steps(sp, body)
            if expand:
                for b in range(U):
                    sp.wait_ge(s(f"rel_in{b}"), 16 * (RT // U + 1))

        @block.gpsimd
        def _(g):
            def gather(out, table_, col, b):
                g.indirect_dma_start(out=out, out_offset=None, in_=table_,
                                     in_offset=bass.IndirectOffsetOnAxis(ap=ix[:, b, col:col + 1], axis=0)
                                     ).then_inc(s(f"gathered{b}"), 16)

            def body(i):
                for b in range(U):
                    reuse(g, s(f"messages{b}"), i)
                    g.wait_ge(s(f"ix_in{b}"), 16 * i + 16)
                    g.nop(nofuse=True)
                    if expand:
                        pass
                    elif kind == "gat":
                        gather(src[:, b, K, :], table[:, :], K, b)
                    else:
                        gather(node[:, b, :], node_table[:, :], K, b)
                    if kind == "conv":
                        gather(attr[:, b, :], chunk_attr[:, :], K + 1, b)
                    for k in range(K):
                        gather(src[:, b, k, :], table[:, :], k, b)
            gather_steps(g, body)

        @block.vector
        def _(v):
            ch = Chain(v, s("dve"))
            mc = Chain(v, s("dve_maxima"), 5 if whole_max else 11)

            def feature_logits(b):
                if kind == "conv":
                    pv = prod[:].rearrange("p k (h c) -> p k h c", h=H)
                    nv = node[:, b, :].rearrange("p (h c) -> p h c", h=H)
                    v.tensor_tensor(pv[:, :, :, 0:FEAT], bcast(src[:, b, :, :], [P, K, H, FEAT], 2),
                                    bcast(nv[:, :, 0:FEAT], [P, K, H, FEAT], 1), ALU.mult)
                    av = attr[:, b, :].rearrange("p (k c) -> p k c", k=K)
                    ch.link(v.tensor_tensor(pv[:, :, :, FEAT:C], bcast(av, [P, K, H, C - FEAT], 2),
                                            bcast(nv[:, :, FEAT:C], [P, K, H, C - FEAT], 1), ALU.mult))
                    ch.link(v.tensor_reduce(lg[:], pv, X, ALU.add))
                    ch.link(v.tensor_tensor(raw[:], lg[:], bcast(nv[:, :, C], [P, K, H], 1), ALU.add))
                    return
                if kind == "gat":
                    ch.link(v.tensor_tensor(lg[:], src[:, b, :, H * C:H * C + H],
                                            bcast(src[:, b, K, H * C + H:], [P, KS, H], 1), ALU.add))
                elif kind == "dot":
                    ch.link(v.tensor_tensor(prod[:], src[:, b, :, 0:H * C],
                                            bcast(node[:, b, :], [P, K, H * C], 1), ALU.mult))
                    ch.link(v.tensor_reduce(lg[:], prod[:].rearrange("p k (h c) -> p k h c", h=H), X, ALU.add))
                elif kind == "gatv2":
                    ch.link(v.tensor_tensor(prod[:], src[:, b, :, :], bcast(node[:, b, :], [P, K, H * C], 1), ALU.add))
                    ch.link(v.scalar_tensor_tensor(act[:], prod[:], NEG_SLOPE, prod[:], ALU.mult, ALU.max))
                    ch.link(v.tensor_tensor(prod[:], act[:], bcast(vec[:], [P, K, H * C], 1), ALU.mult))
                    ch.link(v.tensor_reduce(raw[:], prod[:].rearrange("p k (h c) -> p k h c", h=H), X, ALU.add))
                    return
                ch.link(v.scalar_tensor_tensor(raw[:], lg[:], NEG_SLOPE, lg[:], ALU.mult, ALU.max))

            def one_hot(im, b):
                v.wait_ge(s(f"spread{b}"), im + 1)
                v.tensor_scalar(onehot[:, b, :], T.iota256[:], T.rel[:, bass.ds(im * U + b, 1)], None,
                                ALU.is_equal).then_inc(s(f"onehot{b}"), 1)

            def add(im, b, tail=False):
                t = im * U + b
                block_of = v.value_load(T.blk[0:1, bass.ds(t, 1)], min_val=0, max_val=NB - 1)
                v.wait_ge(s(f"spread{b}"), im + 2)
                v.nop(nofuse=True)
                v.wait_ge(s("added"), t + U + 1)
                v.tensor_tensor(acc[:, bass.ds(block_of, 2), :], acc[:, bass.ds(block_of, 2), :], merge_pair(b, tail), ALU.add
                                ).then_inc(s("added"), 1)

            def picks(n, b):
                v.wait_ge(s(f"rel_in{b}"), 16 * n + 16)
                reuse(v, s(f"nodes_ps{b}"), n)
                v.nop(nofuse=True)
                v.tensor_scalar(pick[:, b, :], rel_rows[:, b, :], T.pid[:], None, ALU.is_equal
                                ).then_inc(s(f"pick{b}"), 1)

            def edges(i, j, im):
                ch.begin(i)
                for b in range(U):
                    t = i * U + b
                    v.wait_ge(s(f"gathered{b}"), (16 * i + 16) * gathers)
                    if expand:
                        v.wait_ge(s(f"nodes_kept{b}"), i + 1)
                    feature_logits(b)
                    ch.link(v.tensor_tensor(lg[:], raw[:], bcast(T.mask[:, bass.ds(t * SLOTS, KS)], [P, KS, H], 2), ALU.add))
                    reuse(v, s(f"tops_kept{b}"), i)
                    ch.link(v.tensor_reduce(top[:, b, :], lg[:].rearrange("p k h -> p h k"), X, ALU.max))
                    v.tensor_tensor(low[:, b, :, :], lg[:], bcast(top[:, b, :], [P, KS, H], 1), ALU.subtract
                                    ).then_inc(s(f"logits{b}"), 1)
                    if im is not None:
                        one_hot(im, b)
                    if expand:
                        picks(i + 1, b)
                    v.wait_ge(s(f"weights{b}"), i + 1)
                    w = msg[:, b, :, :, C:C + 1]
                    if kind == "conv":
                        v.tensor_tensor(msg[:, b, :, :, 0:FEAT], bcast(src[:, b, :, :], [P, K, H, FEAT], 2),
                                        w.to_broadcast([P, K, H, FEAT]), ALU.mult)
                        av = attr[:, b, :].rearrange("p (k c) -> p k c", k=K)
                        last = v.tensor_tensor(msg[:, b, :, :, FEAT:C], bcast(av, [P, K, H, C - FEAT], 2),
                                               w.to_broadcast([P, K, H, C - FEAT]), ALU.mult)
                    else:
                        at = H * C if kind == "dot" else 0
                        val = src[:, b, :, at:at + H * C].rearrange("p k (h c) -> p k h c", h=H)
                        last = v.tensor_tensor(msg[:, b, :, :, 0:C], val, w.to_broadcast([P, KS, H, C]), ALU.mult)
                    if halve:
                        ch.link(last)
                        half = msg[:, b, 0:K // 2]
                        last = v.tensor_tensor(half, half, msg[:, b, K // 2:K], ALU.add)
                    last.then_inc(s(f"messages{b}"), 1)
                    if im is not None and b:
                        add(im, b - 1)
                if im is not None:
                    add(im, U - 1)

            def merge_only(im, j):
                for b in range(U):
                    one_hot(im, b)
                for b in range(U):
                    add(im, b, tail=True)

            def node_maxima(cm):
                pen = lambda tab: tab[:, bass.ds(cm * P, P)]
                for b in range(U):
                    v.wait_ge(s(f"tops_kept{b}"), cm * S + S)
                v.nop(nofuse=True)
                mc.begin(cm)
                v.tensor_copy(mh[:], T.m[:, bass.ds(cm * (CT * H), CT * H)].rearrange("p (t h) -> p h t", h=H)
                              ).then_inc(s("by_head"), 1)
                v.wait_ge(s("rows_T"), cm + 1)
                for h in range(H):
                    last = v.tensor_tensor_scan(fwd[:, h, :], pen(T.pen), mx_ps[0:CT, h * P:(h + 1) * P], LOW,
                                                ALU.add, ALU.max)
                mc.link(last)
                v.tensor_copy(edge[:, 0, :], fwd[:, :, P - 1]).then_inc(s("edge"), 1)
                v.wait_ge(s("edge_T"), cm * 2 + 1)
                mc.link(v.tensor_copy(edgeT[:, 0, :], mx_ps[0:H, 0:CT]))
                v.tensor_tensor_scan(runs[:, 0, 1:CT + 1], T.pen_tile[0:H, bass.ds(cm * CT, CT)], edgeT[:, 0, :],
                                     runs[:, 0, 0:1], ALU.add, ALU.max).then_inc(s("runs"), 1)
                v.wait_ge(s("into_T"), cm * 2 + 1)
                mc.link(v.tensor_copy(into[:, 0, :], mx_ps[0:CT, 64:64 + H]))
                mc.link(v.tensor_copy(runs[:, 0, 0:1], runs[:, 0, CT:CT + 1]))
                for h in range(H):
                    last = v.scalar_tensor_tensor(full[:, h, :], pen(T.pen_pre), into[:, 0, h:h + 1], fwd[:, h, :],
                                                  ALU.add, ALU.max)
                mc.link(last)
                for h in range(H):
                    last = v.tensor_tensor_scan(bwd[:, h, ::-1], pen(T.pen_b), full[:, h, ::-1], LOW,
                                                ALU.add, ALU.max)
                mc.link(last)
                v.tensor_copy(edge[:, 1, :], bwd[:, :, 0]).then_inc(s("edge"), 1)
                v.wait_ge(s("edge_T"), cm * 2 + 2)
                mc.link(v.tensor_copy(edgeT[:, 1, :], mx_ps[0:H, 32:32 + CT]))
                v.tensor_tensor_scan(runs[:, 1, 0:CT][:, ::-1], T.pen_tile_b[0:H, bass.ds(cm * CT, CT)],
                                     edgeT[:, 1, ::-1], LOW, ALU.add, ALU.max).then_inc(s("runs"), 1)
                v.wait_ge(s("into_T"), cm * 2 + 2)
                mc.link(v.tensor_copy(into[:, 1, :], mx_ps[0:CT, 72:72 + H]))
                for h in range(H):
                    last = v.scalar_tensor_tensor(whole[:, h, :], pen(T.pen_suf), into[:, 1, h:h + 1], bwd[:, h, :],
                                                  ALU.add, ALU.max)
                last.then_inc(s("whole"), 1)
                v.wait_ge(s("whole"), cm + 1)
                mc.link(v.tensor_tensor(edge[0:1, 0, :], into[0:1, 0, :], whole[0:1, :, 0], ALU.subtract))
                mc.link(v.tensor_scalar(delta[:, 0:H], edge[0:1, 0, :], 0.0, None, ALU.min))
                v.nop(nofuse=True)
                v.tensor_copy(delta[:, H:H + 1], T.rel[0:1, bass.ds(cm * CT, 1)]).then_inc(s("delta"), 1)
                v.wait_ge(s("maxima"), cm + 1)
                v.tensor_tensor(gap[:], T.m[:, bass.ds(cm * (CT * H), CT * H)].rearrange("p (t h) -> p t h", h=H),
                                mx_ps[:, 128:128 + H * CT].rearrange("p (h t) -> p t h", h=H), ALU.subtract
                                ).then_inc(s("gap"), 1)
                mc.link(v.tensor_scalar(chosen[:], T.pid[:], mx_ps[:, 256 + H:257 + H], None, ALU.is_equal))
                v.tensor_scalar(shrink_log[:], mx_ps[:, 256:256 + H], chosen[:], None, ALU.mult
                                ).then_inc(s("shrink_log"), 1)
                block_of = v.value_load(T.blk[0:1, bass.ds(cm * CT, 1)], min_val=0, max_val=NB - 1)
                v.wait_ge(s("shrink"), cm + 1)
                v.nop(nofuse=True)
                v.wait_ge(s("added"), cm * CT + U + 1)
                own = acc[:, bass.ds(block_of, 1), :].rearrange("p o (h c) -> p (o h) c", h=H)
                v.tensor_tensor(own, own, bcast(shrink[:], [P, H, C + 1], 2), ALU.mult).then_inc(s("shrunk"), 1)
                v.wait_ge(s("shrunk"), cm + 1)

            def global_maximum(cm):
                for b in range(U):
                    v.wait_ge(s(f"tops_kept{b}"), cm * S + S)
                v.nop(nofuse=True)
                mc.begin(cm)
                v.tensor_reduce(top1[:], T.m[:, bass.ds(cm * (CT * H), CT * H)], X, ALU.max).then_inc(s("by_head"), 1)
                v.wait_ge(s("rows_T"), cm + 1)
                mc.link(v.tensor_reduce(edge[0:1, 0, 0:1], mx_ps[0:1, 0:P], X, ALU.max))
                mc.link(v.tensor_tensor(largest[:, 1:2], largest[:, 0:1], edge[0:1, 0, 0:1], ALU.max))
                v.tensor_tensor(delta[:, 1:2], largest[:, 0:1], largest[:, 1:2], ALU.subtract)
                mc.link(v.tensor_scalar(delta[:, 0:1], largest[:, 1:2], -1.0, None, ALU.mult))
                mc.link(v.tensor_copy(largest[:, 0:1], largest[:, 1:2]))
                v.memset(delta[:, 2:], 0.0).then_inc(s("delta"), 1)
                v.wait_ge(s("delta_all"), cm + 1)
                mc.link(v.tensor_copy(shrink_log[:, 0:2], mx_ps[:, 256:258]))
                v.tensor_copy(chosen[:], shrink_log[:, 0:1]).then_inc(s("gap"), 1)
                v.wait_ge(s("shrink"), cm + 1)
                v.nop(nofuse=True)
                v.wait_ge(s("added"), cm * CT + U + 1)
                v.tensor_scalar(acc, acc, shrink[:, 1:2], None, ALU.mult).then_inc(s("shrunk"), 1)
                v.wait_ge(s("shrunk"), cm + 1)

            v.memset(acc, 0.0).then_inc(s("added"), U + 1)
            if expand:
                v.memset(nodes_sb[:, NB, :], 0.0).then_inc(s("nodes_pad"), 1)
                for b in range(U):
                    picks(0, b)
            v.memset(runs[:], LOW)
            v.memset(largest[:], LOW).then_inc(s("blank"), 1)
            v.wait_ge(s("blank"), 1)
            all_chunks(v, edges, global_maximum if whole_max else node_maxima, merge_only)
            assert mc.k == mc.steps
            v.wait_ge(s("added"), RT + U + 1)

        @block.tensor
        def _(pe):
            def merge(im, b, tail=False):
                t = im * U + b
                pe.wait_ge(s(f"scaled{b}"), im + 1)
                pe.wait_ge(s(f"onehot{b}"), im + 1)
                pe.wait_ge(s("added"), t + U + 2 - (1 if wide and expand and not tail else (1, 3, 2)[b]))
                for j in range(2):
                    last = pe.matmul(merge_pair(b, tail)[:, j, :], onehot[:, b, j * P:(j + 1) * P],
                                     scaled[:, b, :], start=True, stop=True)
                last.then_inc(s(f"spread{b}"), 1)

            def own_nodes(n, b):
                block_of = pe.value_load(T.blk[0:1, bass.ds(n * U + b, 1)], min_val=0, max_val=NB - 1)
                pe.wait_ge(s(f"pick{b}"), n + 1)
                if b == 2:
                    pe.wait_ge(s("nodes_kept0"), n + 1)
                else:
                    reuse(pe, s(f"nodes_kept{(2, 1)[b]}"), n)
                pe.nop(nofuse=True)
                for j in range(2):
                    last = pe.matmul(nodes_ps[:, b % 2, 0:own_w], pick[:, b, j * P:(j + 1) * P],
                                     nodes_sb[:, bass.ds(block_of + j, 1), :].rearrange("p o w -> p (o w)"),
                                     start=(j == 0), stop=(j == 1))
                last.then_inc(s(f"nodes_ps{b}"), 1)

            def edges(i, j, im):
                for b in range(U):
                    if im is not None:
                        merge(im, b)
                    pe.wait_ge(s(f"messages{b}"), i + 1)
                    reuse(pe, s(f"evacuated{b}"), i)
                    slots = [k for k in range(KS) if not halve or not K // 2 <= k < K]
                    for k in slots:
                        last = pe.matmul(sums_ps[:, b, 0:F], T.ident[:],
                                         msg[:, b, k, :, :].rearrange("p h c -> p (h c)"),
                                         start=(k == 0), stop=(k == slots[-1]))
                    last.then_inc(s(f"summed{b}"), 1)
                    if expand:
                        own_nodes(i + 1, b)

            def merge_only(im, j):
                if expand:
                    for b in range(U):
                        pe.wait_ge(s(f"nodes_kept{b}"), RT // U + 1)
                for b in range(U):
                    merge(im, b, tail=True)

            def maxima(cm):
                pe.wait_ge(s("by_head"), cm + 1)
                if whole_max:
                    pe.transpose(mx_ps[0:1, 0:P], top1[:], T.ident[:]).then_inc(s("rows_T"), 1)
                    pe.wait_ge(s("delta"), cm + 1)
                    pe.matmul(mx_ps[:, 256:257 + H], T.ones[:], delta[:], start=True, stop=True
                              ).then_inc(s("delta_all"), 1)
                    return
                for h in range(H):
                    last = pe.transpose(mx_ps[0:CT, h * P:(h + 1) * P], mh[:, h, :], T.ident[:])
                last.then_inc(s("rows_T"), 1)
                for d in range(2):
                    pe.wait_ge(s("edge"), cm * 2 + d + 1)
                    pe.nop(nofuse=True)
                    pe.transpose(mx_ps[0:H, 32 * d:32 * d + CT], edge[:, d, :], T.ident[0:CT, 0:CT]
                                 ).then_inc(s("edge_T"), 1)
                    pe.wait_ge(s("runs"), cm * 2 + d + 1)
                    pe.nop(nofuse=True)
                    pe.transpose(mx_ps[0:CT, 64 + 8 * d:64 + 8 * d + H], runs[:, d, d:d + CT], T.ident[0:H, 0:H]
                                 ).then_inc(s("into_T"), 1)
                pe.wait_ge(s("whole"), cm + 1)
                pe.nop(nofuse=True)
                for h in range(H):
                    pe.transpose(mx_ps[:, 128 + h * CT:128 + (h + 1) * CT], whole[:, h, :], T.ident[0:CT, 0:CT])
                pe.wait_ge(s("delta"), cm + 1)
                pe.matmul(mx_ps[:, 256:257 + H], T.ones[:], delta[:], start=True, stop=True).then_inc(s("maxima"), 1)

            for b in range(U):
                pe.nop(nofuse=True).then_inc(s(f"spread{b}"), 1)
            if expand:
                pe.wait_ge(s("nodes_in"), 16)
                pe.wait_ge(s("nodes_pad"), 1)
                for b in range(U):
                    own_nodes(0, b)
            all_chunks(pe, edges, maxima, merge_only)

        @block.scalar
        def _(a):
            def keep(i, b, slot):
                a.wait_ge(s(f"summed{b}"), i + 1)
                a.nop(nofuse=True)
                a.copy(ring[:, slot, :], sums_ps[:, b, 0:F]).then_inc(s(f"evacuated{b}"), 1)

            def scale(im, j, b):
                t = im * U + b
                a.wait_ge(s(f"spread{b}"), im + 1)
                a.wait_ge(s(f"evacuated{b}"), im + 1)
                a.nop(nofuse=True)
                for h in range(H):
                    own = slice(h * (C + 1), (h + 1) * (C + 1))
                    last = a.activation(scaled[:, b, own],
                                        ring[:, bass.ds(j * U + b, 1), own].rearrange("p o c -> p (o c)"), ACT.Copy,
                                        scale=T.factor[:, bass.ds(t * H + h, 1)])
                last.then_inc(s(f"scaled{b}"), 1)

            def keep_nodes(n, b):
                reuse(a, s(f"messages{b}"), n)
                a.wait_ge(s(f"nodes_ps{b}"), n + 1)
                a.nop(nofuse=True)
                a.copy(src[:, b, K, :] if kind == "gat" else node[:, b, :], nodes_ps[:, b % 2, 0:own_w]
                       ).then_inc(s(f"nodes_kept{b}"), 1)

            def edges(i, j, im):
                for b in range(U):
                    t = i * U + b
                    a.wait_ge(s(f"logits{b}"), i + 1)
                    reuse(a, s(f"summed{b}"), i)
                    a.activation(msg[:, b, :, :, C], low[:, b, :, :], ACT.Exp).then_inc(s(f"weights{b}"), 1)
                    a.copy(T.m[:, bass.ds(t * H, H)], top[:, b, :]).then_inc(s(f"tops_kept{b}"), 1)
                    if b:
                        keep(i, b - 1, bass.ds(j * U + b - 1, 1))
                    elif isinstance(j, int) and im is not None:
                        keep(i - 1, U - 1, bass.ds(CT - 1, 1))
                    elif not isinstance(j, int):
                        keep(i - 1, U - 1, bass.ds(j * U - 1, 1))
                    if im is not None:
                        scale(im, j, b)
                    if expand and b:
                        keep_nodes(i + 1, b - 1)
                if expand:
                    keep_nodes(i + 1, U - 1)

            def merge_only(im, j):
                for b in range(U):
                    scale(im, j, b)

            def maxima(cm):
                if isinstance(cm, int):
                    keep(NCH * S - 1, U - 1, bass.ds(CT - 1, 1))
                a.wait_ge(s("gap"), cm + 1)
                a.nop(nofuse=True)
                mine = T.factor[:, bass.ds(cm * (CT * H), CT * H)]
                if whole_max:
                    a.activation(mine, T.m[:, bass.ds(cm * (CT * H), CT * H)], ACT.Exp, bias=chosen[:])
                    a.activation(shrink[:, 0:2], shrink_log[:, 0:2], ACT.Exp).then_inc(s("shrink"), 1)
                    a.wait_ge(s("shrink"), cm + 1)
                    return
                a.activation(mine, gap[:].rearrange("p t h -> p (t h)"), ACT.Exp)
                a.wait_ge(s("shrink_log"), cm + 1)
                a.activation(shrink[:], shrink_log[:], ACT.Exp).then_inc(s("shrink"), 1)
                a.wait_ge(s("shrink"), cm + 1)
            if expand:
                for b in range(U):
                    keep_nodes(0, b)
            all_chunks(a, edges, maxima, merge_only)
    ph.close()


LN_EPS = 1e-5


class Dense:

    def __init__(self, c, T, name, H=0, C=0, ph=None, pt=None):
        self.c, self.T, self.nc = c, T, c.nc
        self.ph = ph or Phase(c, name)
        self.s, self.sb = self.ph.sem, self.ph.sb
        self.pt = self.ph.ps("pt", [P, 8, 512]) if pt is None else pt
        self.small = self.sb("small", [P, 3, G])
        self.cen = self.sb("cen", [P, G, P])
        self.stats = self.sb("stats", [P, G, 6])
        self.mv = self.sb("mv", [P, G, 2])
        if H:
            F = H * (C + 1)
            self.acc = T.acc[:, 0:NB * F].rearrange("p (b h c) -> p b h c", h=H, c=C + 1)

    def group(self, ap, i):
        return ap[:, bass.ds(i * G, G)]

    def hT_slot(self, j):
        return self.pt[:, 5 + j // 4, (j % 4) * P:(j % 4) * P + P]

    def norm_vector(self, v, ch, i, src, out, tag, relu=False, gain=None, shift=None):
        s, small, cen, stats, mv = self.s, self.small, self.cen, self.stats, self.mv
        for j in range(G):
            last = v.bn_stats(out=stats[:, j, :], in_=src[:, j, :])
        ch.link(last)
        v.nop(nofuse=True)
        for j in range(G):
            last = v.bn_aggr(out=mv[:, j, :], in_=stats[:, j, :])
        ch.link(last)
        v.tensor_scalar(small[:, 1, :], mv[:, :, 1], LN_EPS, None, ALU.add).then_inc(s(f"{tag}_var"), 1)
        if gain is None:
            v.tensor_tensor(cen[:], src, bcast(mv[:, :, 0], [P, G, P], 2), ALU.subtract)
        else:
            for j in range(G):
                v.scalar_tensor_tensor(cen[:, j, :], src[:, j, :], mv[:, j, 0:1], gain[:], ALU.subtract, ALU.mult)
        v.wait_ge(s(f"{tag}_std"), i + 1)
        ch.link(v.reciprocal(small[:, 2, :], small[:, 2, :]))
        for j in range(G):
            rstd = small[:, 2, j:j + 1]
            if gain is None:
                last = v.tensor_scalar(out[:, j, :], cen[:, j, :], rstd, 0.0, ALU.mult, ALU.max)
            else:
                last = v.scalar_tensor_tensor(out[:, j, :], cen[:, j, :], rstd, shift[:], ALU.mult, ALU.add)
        return last

    def norm_scalar(self, a, i, tag):
        a.wait_ge(self.s(f"{tag}_var"), i + 1)
        a.activation(self.small[:, 2, :], self.small[:, 1, :], ACT.Sqrt).then_inc(self.s(f"{tag}_std"), 1)


def rows_of(table, i, n=G):
    return table[bass.ds(i * (G * P), n * P), :].rearrange("(b p) w -> p b w", p=P)


class NodeIn:

    def __init__(self, c, T, ph, pt, W, table, node_table):
        self.d = Dense(c, T, "in", ph=ph, pt=pt)
        self.T, self.W, self.s, self.pt, self.table, self.node_table = T, W, ph.sem, pt, table, node_table
        sb = ph.sb
        self.h, self.hT = sb("h", [P, G, P]), sb("hT", [P, G, P])
        self.wq, self.bq, self.kx = sb("wq", [P, 2 * P]), sb("bq", [P, 2]), sb("kx", [P, 2, 161])
        self.qT = sb("qT", [P, G, 2, P])
        self.td = sb("td", [P, G, 322])

    def weights(self, sp):
        for t, w in ((self.wq, "L0_WqT"), (self.bq, "L0_bq"), (self.kx, "L0_kx")):
            sp.dma_start(t[:], self.W[w]).then_inc(self.s("weights_in"), 16)

    def vector(self, v, ch, i):
        s, d = self.s, self.d
        reuse(v, s("h_out"), i, 16)
        reuse(v, s("hs"), i)
        reuse(v, s("hT_ps"), i)
        d.norm_vector(v, ch, i, d.group(self.T.xs, i), self.h[:], "ln").then_inc(s("h"), 1)
        v.wait_ge(s("qT_ps"), i + 1)
        for m in range(2):
            last = v.tensor_scalar(self.qT[:, :, m, :], self.pt[:, 0:G, (1 + m) * P:(2 + m) * P], self.bq[:, m:m + 1],
                                   float(P) ** -0.5, ALU.add, ALU.mult)
        last.then_inc(s("qT"), 1)

    def tensor(self, pe, i):
        s, pt = self.s, self.pt
        pe.wait_ge(s("h"), i + 1)
        for j in range(G):
            last = pe.transpose(pt[:, j, 0:P], self.h[:, j, :], self.T.ident[:])
        last.then_inc(s("hT_ps"), 1)
        pe.wait_ge(s("hT"), i + 1)
        for j in range(G):
            for m in range(2):
                last = pe.matmul(pt[:, j, (1 + m) * P:(2 + m) * P], self.wq[:, m * P:(m + 1) * P], self.hT[:, j, :],
                                 start=True, stop=True)
        last.then_inc(s("qT_ps"), 1)
        pe.wait_ge(s("qT"), i + 1)
        for j in range(G):
            for m in range(2):
                last = pe.matmul(pt[:, j, m * 161:(m + 1) * 161], self.qT[:, j, m, :], self.kx[:, m, :],
                                 start=True, stop=True)
        last.then_inc(s("td_ps"), 1)
        pe.wait_ge(s("td"), i + 1)

    def scalar(self, a, i):
        s, d, pt = self.s, self.d, self.pt
        d.norm_scalar(a, i, "ln")
        a.wait_ge(s("h"), i + 1)
        a.dma_start(rows_of(self.table, i), self.h[:]).then_inc(s("h_out"), 16)
        a.copy(d.group(self.T.hs, i), self.h[:]).then_inc(s("hs"), 1)
        a.wait_ge(s("hT_ps"), i + 1)
        a.copy(self.hT[:], pt[:, 0:G, 0:P]).then_inc(s("hT"), 1)
        a.wait_ge(s("td_ps"), i + 1)
        reuse(a, s("td_out"), i, 16)
        a.copy(self.td[:], pt[:, 0:G, 0:322]).then_inc(s("td"), 1)
        a.wait_ge(s("td"), i + 1)
        a.dma_start(rows_of(self.node_table, i), self.td[:]).then_inc(s("td_out"), 16)


def project_weights(v, s, w, HC, a_src, a_dst, prod, heads=4):
    parts = w.shape[1]
    for side, vec in enumerate((a_src, a_dst)):
        v.tensor_tensor(prod[:, side], w[:, :, 0:HC], bcast(vec[:], [P, parts, HC], 1), ALU.mult
                        ).then_inc(s("w_prod"), 1)
    v.wait_ge(s("w_prod"), 2)
    for side in range(2):
        v.tensor_reduce(w[:, :, HC + side * heads:HC + (side + 1) * heads],
                        prod[:, side].rearrange("p m (h c) -> p m h c", h=heads), X, ALU.add).then_inc(s("w_full"), 1)


def node_after_conv(c, T, W, table):
    H, C, HC = 2, 160, 256
    d = Dense(c, T, "conv_out", H, C)
    s, pt = d.s, d.pt
    names = {"wv": ("L0_WvT", [P, 2 * P]), "web": ("L0_web", [33, 2, P]), "wskip": ("L0_WskipT", [P, P]),
             "bskip": ("L0_bskip", [1, P]), "w1": ("L0_W1T", [P, 2 * P]), "b1": ("L0_b1", [P, 2]),
             "w2": ("L0_W2T", [P, 2, P]), "b2": ("L0_b2", [1, P])}
    w = {k: d.sb(k, shape) for k, (_, shape) in names.items()}
    w0 = d.sb("w0_full", [P, 1, HC + 8])
    vecs = {k: d.sb(k, [P, W[n].shape[-1]]) for k, n in
            (("g1", "L0_ln1_g"), ("s1", "L0_ln1_b"), ("g2", "L0_ln2_g"), ("s2", "L0_ln2_b"),
             ("a_src", "L1_as0"), ("a_dst", "L1_ad0"))}
    vec_of = {"g1": "L0_ln1_g", "s1": "L0_ln1_b", "g2": "L0_ln2_g", "s2": "L0_ln2_b",
              "a_src": "L1_as0", "a_dst": "L1_ad0"}
    rden = d.sb("rden", [P, G, H])
    den = d.sb("den", [P, G, H])
    agg = d.sb("agg", [P, G, H, C + 1])
    aggT = d.sb("aggT", [P, G, H, P])
    attT = d.sb("attT", [33, G, H, P])
    h0 = d.sb("h0", [P, G, P])
    hT = d.sb("hT", [P, G, P])
    pre = d.sb("pre", [P, G, P])
    pre2 = d.sb("pre2", [P, G, P])
    h1 = d.sb("h1", [P, G, P])
    h1T = d.sb("h1T", [P, G, P])
    up = d.sb("up", [P, 2, G, P])
    f1 = d.sb("f1", [P, 2, G, P])
    x1 = d.sb("x1", [P, G, P])
    h = d.sb("h", [P, G, P])
    rows = d.sb("rows", [P, G, HC + 8])
    prod = d.sb("prod", [P, 2, 1, HC])
    n_loads = len(w) + 1 + len(vecs)

    with c.nc.Block() as block:
        @block.sync
        def _(sp):
            for k, (n, _) in names.items():
                sp.dma_start(w[k][:], W[n]).then_inc(s("weights_in"), 16)
            sp.dma_start(w0[:, 0, 0:HC], W["L1_W0"]).then_inc(s("weights_in"), 16)
            for k, t in vecs.items():
                sp.dma_start(t[:], W[vec_of[k]].partition_broadcast(P)).then_inc(s("weights_in"), 16)

            def body(i):
                sp.wait_ge(s("rows"), i + 1)
                sp.dma_start(rows_of(table, i), rows[:]).then_inc(s("rows_out"), 16)
            loop(sp, NG, body)
            sp.wait_ge(s("rows_out"), 16 * NG)

        @block.vector
        def _(v):
            ch = Chain(v, s("dve"))
            v.wait_ge(s("weights_in"), 16 * n_loads)
            project_weights(v, s, w0, HC, vecs["a_src"], vecs["a_dst"], prod)

            def body(i):
                ch.begin(i)
                acc = d.group(d.acc, i)
                ch.link(v.tensor_scalar(den[:], acc[:, :, :, C], 1e-16, None, ALU.add))
                ch.link(v.reciprocal(rden[:], den[:]))
                reuse(v, s("aggT_ps"), i)
                v.tensor_tensor(agg[:], acc, bcast(rden[:], [P, G, H, C + 1], 3), ALU.mult).then_inc(s("agg"), 1)
                v.wait_ge(s("mixed"), i + 1)
                ch.link(v.scalar_tensor_tensor(pre[:], pt[:, 0:G, 0:P], 0.5, h0[:], ALU.mult, ALU.add))
                ch.link(v.tensor_tensor(pre2[:], pre[:], pt[:, 0:G, P:2 * P], ALU.add))
                d.norm_vector(v, ch, i, pre2[:], h1[:], "ln1", gain=vecs["g1"], shift=vecs["s1"]
                              ).then_inc(s("h1"), 1)
                v.wait_ge(s("up"), i + 1)
                v.scalar_tensor_tensor(f1[:].rearrange("p m g n -> p (m g n)"), up[:].rearrange("p m g n -> p (m g n)"),
                                       0.01, up[:].rearrange("p m g n -> p (m g n)"), ALU.mult, ALU.max
                                       ).then_inc(s("f1"), 1)
                v.wait_ge(s("f2_ps"), i + 1)
                ch.link(v.tensor_tensor(pre[:], h1[:], pt[:, 0:G, 0:P], ALU.add))
                ch.link(d.norm_vector(v, ch, i, pre[:], pre2[:], "ln2", gain=vecs["g2"], shift=vecs["s2"]))
                ch.link(v.tensor_tensor(x1[:], d.group(T.xs, i), pre2[:], ALU.add))
                v.tensor_scalar(d.group(T.xs, i), x1[:], 1.0, None, ALU.mult)
                d.norm_vector(v, ch, i, x1[:], h[:], "ln3").then_inc(s("h"), 1)
            loop(v, NG, body)

        @block.tensor
        def _(pe):
            pe.wait_ge(s("weights_in"), 16 * n_loads)
            pe.wait_ge(s("w_full"), 2)

            def body(i):
                reuse(pe, s("rows"), i)
                pe.wait_ge(s("agg"), i + 1)
                for j in range(G):
                    for m in range(H):
                        pe.transpose(pt[:, j, m * 256:m * 256 + P], agg[:, j, m, 0:P], T.ident[:])
                        pe.transpose(pt[0:33, j, m * 256 + P:m * 256 + 2 * P], agg[:, j, m, P:161], T.ident[:])
                pe.wait_ge(s("h0"), i + 1)
                for j in range(G):
                    last = pe.transpose(d.hT_slot(j), h0[:, j, :], T.ident[:])
                last.then_inc(s("aggT_ps"), 1)
                pe.wait_ge(s("aggT"), i + 1)
                for j in range(G):
                    for m in range(H):
                        pe.matmul(pt[:, j, 0:P], aggT[:, j, m, :], w["wv"][:, m * P:(m + 1) * P],
                                  start=(m == 0), stop=False)
                        pe.matmul(pt[:, j, 0:P], attT[:, j, m, :], w["web"][:, m, :], start=False, stop=(m == H - 1))
                    pe.matmul(pt[:, j, P:2 * P], hT[:, j, :], w["wskip"][:], start=True, stop=False)
                    last = pe.matmul(pt[:, j, P:2 * P], T.ones[:], w["bskip"][:], start=False, stop=True)
                last.then_inc(s("mixed"), 1)
                pe.wait_ge(s("h1"), i + 1)
                for j in range(G):
                    last = pe.transpose(d.hT_slot(j), h1[:, j, :], T.ident[:])
                last.then_inc(s("h1T_ps"), 1)
                pe.wait_ge(s("h1T"), i + 1)
                for j in range(G):
                    for m in range(2):
                        last = pe.matmul(pt[:, j, m * P:(m + 1) * P], w["w1"][:, m * P:(m + 1) * P], h1T[:, j, :],
                                         start=True, stop=True)
                last.then_inc(s("up_ps"), 1)
                pe.wait_ge(s("f1"), i + 1)
                for j in range(G):
                    for m in range(2):
                        pe.matmul(pt[:, j, 0:P], f1[:, m, j, :], w["w2"][:, m, :], start=(m == 0), stop=False)
                    last = pe.matmul(pt[:, j, 0:P], T.ones[:], w["b2"][:], start=False, stop=True)
                last.then_inc(s("f2_ps"), 1)
                pe.wait_ge(s("h"), i + 1)
                for j in range(G):
                    last = pe.transpose(d.hT_slot(j), h[:, j, :], T.ident[:])
                last.then_inc(s("hT2_ps"), 1)
                pe.wait_ge(s("hT2"), i + 1)
                for j in range(G):
                    last = pe.matmul(pt[:, j, 0:HC + 8], hT[:, j, :], w0[:, 0, :], start=True, stop=True)
                last.then_inc(s("xp_ps"), 1)
            loop(pe, NG, body)

        @block.scalar
        def _(a):
            a.wait_ge(s("weights_in"), 16 * n_loads)

            def slots(out, tag, i):
                a.copy(out[:, 0:4, :], pt[:, 5, :].rearrange("p (g n) -> p g n", g=4))
                a.copy(out[:, 4, :], pt[:, 6, 0:P]).then_inc(s(tag), 1)

            def body(i):
                reuse(a, s("mixed"), i)
                reuse(a, s("h1"), i)
                a.copy(h0[:], d.group(T.hs, i)).then_inc(s("h0"), 1)
                a.wait_ge(s("aggT_ps"), i + 1)
                pv = pt[:, 0:G, :].rearrange("p g (m n) -> p g m n", m=2)
                a.copy(aggT[:], pv[:, :, :, 0:P])
                a.copy(attT[:], pv[0:33, :, :, P:2 * P])
                reuse(a, s("xp_ps"), i)
                slots(hT, "aggT", i)
                d.norm_scalar(a, i, "ln1")
                a.wait_ge(s("h1T_ps"), i + 1)
                slots(h1T, "h1T", i)
                a.wait_ge(s("up_ps"), i + 1)
                for m in range(2):
                    last = a.activation(up[:, m, :, :], pt[:, 0:G, m * P:(m + 1) * P], ACT.Identity,
                                        bias=w["b1"][:, m:m + 1])
                last.then_inc(s("up"), 1)
                d.norm_scalar(a, i, "ln2")
                d.norm_scalar(a, i, "ln3")
                a.wait_ge(s("hT2_ps"), i + 1)
                slots(hT, "hT2", i)
                a.wait_ge(s("xp_ps"), i + 1)
                reuse(a, s("rows_out"), i, 16)
                a.copy(rows[:], pt[:, 0:G, 0:HC + 8]).then_inc(s("rows"), 1)
            loop(a, NG, body)
    d.ph.close()


def node_between_gats(c, T, W, name, bias_n, w_n, as_n, ad_n, HC, table):
    H, C = 4, 64
    d = Dense(c, T, name, H, C)
    s, pt = d.s, d.pt
    w = d.sb("w", [P, 2, HC + 8])
    vecs = {k: d.sb(k, [P, W[n].shape[-1]]) for k, n in (("b", bias_n), ("a_src", as_n), ("a_dst", ad_n))}
    vec_of = {"b": bias_n, "a_src": as_n, "a_dst": ad_n}
    rden = d.sb("rden", [P, G, H])
    o = d.sb("o", [P, G, H * C])
    o2 = d.sb("o2", [P, G, H * C])
    h = d.sb("h", [P, G, H * C])
    hT = d.sb("hT", [P, G, 2, P])
    rows = d.sb("rows", [P, G, HC + 8])
    prod = d.sb("prod", [P, 2, 2, HC])
    with c.nc.Block() as block:
        @block.sync
        def _(sp):
            sp.dma_start(w[:, :, 0:HC], W[w_n]).then_inc(s("weights_in"), 16)
            for k, t in vecs.items():
                sp.dma_start(t[:], W[vec_of[k]].partition_broadcast(P)).then_inc(s("weights_in"), 16)

            def body(i):
                sp.wait_ge(s("rows"), i + 1)
                sp.dma_start(rows_of(table, i), rows[:]).then_inc(s("rows_out"), 16)
            loop(sp, NG, body)
            sp.wait_ge(s("rows_out"), 16 * NG)

        @block.vector
        def _(v):
            ch = Chain(v, s("dve"))
            v.wait_ge(s("weights_in"), 64)
            project_weights(v, s, w, HC, vecs["a_src"], vecs["a_dst"], prod)

            def body(i):
                ch.begin(i)
                acc = d.group(d.acc, i)
                v.nop(nofuse=True)
                ch.link(v.tensor_copy(rden[:], acc[:, :, :, C]))
                ch.link(v.reciprocal(rden[:], rden[:]))
                ch.link(v.tensor_tensor(o[:].rearrange("p g (h c) -> p g h c", h=H), acc[:, :, :, 0:C],
                                        bcast(rden[:], [P, G, H, C], 3), ALU.mult))
                ch.link(v.tensor_tensor(o2[:], o[:], bcast(vecs["b"][:], [P, G, H * C], 1), ALU.add))
                reuse(v, s("hT_ps"), i)
                v.tensor_scalar(h[:], o2[:], 0.0, None, ALU.max).then_inc(s("h"), 1)
            loop(v, NG, body)

        @block.tensor
        def _(pe):
            pe.wait_ge(s("weights_in"), 64)
            pe.wait_ge(s("w_full"), 2)

            def body(i):
                reuse(pe, s("rows"), i)
                pe.wait_ge(s("h"), i + 1)
                for j in range(G):
                    for m in range(2):
                        last = pe.transpose(pt[:, j, m * P:(m + 1) * P], h[:, j, m * P:(m + 1) * P], T.ident[:])
                last.then_inc(s("hT_ps"), 1)
                pe.wait_ge(s("hT"), i + 1)
                for j in range(G):
                    for m in range(2):
                        last = pe.matmul(pt[:, j, 0:HC + 8], hT[:, j, m, :], w[:, m, :], start=(m == 0), stop=(m == 1))
                last.then_inc(s("xp_ps"), 1)
            loop(pe, NG, body)

        @block.scalar
        def _(a):
            def body(i):
                a.wait_ge(s("hT_ps"), i + 1)
                a.copy(hT[:], pt[:, 0:G, 0:256].rearrange("p g (m n) -> p g m n", m=2)).then_inc(s("hT"), 1)
                a.wait_ge(s("xp_ps"), i + 1)
                reuse(a, s("rows_out"), i, 16)
                a.copy(rows[:], pt[:, 0:G, 0:HC + 8]).then_inc(s("rows"), 1)
            loop(a, NG, body)
    d.ph.close()


KNOT0, BASES, STEP = 4, 7, 0.25


def node_kan(c, T, W, table, node_table):
    H, C = 4, 32
    d = Dense(c, T, "kan", H, C)
    s, pt = d.s, d.pt
    w = d.sb("w", [P, 1 + BASES, 2 * P])
    b2 = d.sb("b2", [P, P])
    centres = d.sb("centres", [P, BASES])
    two = d.sb("two", [P, 1])
    one = d.sb("one", [P, 1])
    rden = d.sb("rden", [P, G, H])
    o = d.sb("o", [P, G, P])
    o2 = d.sb("o2", [P, G, P])
    x2 = d.sb("x2", [P, G, P])
    h = d.sb("h", [P, G, P])
    hT = d.sb("hT", [P, G, P])
    ex = d.sb("ex", [P, G, P])
    sig = d.sb("sig", [P, G, P])
    dist, near2, near1, square2, square1, cube2, cube1 = [
        d.sb(n, [P, 2, BASES, P]) for n in ("dist", "near2", "near1", "square2", "square1", "cube2", "cube1")]
    far = dist
    feat = d.sb("feat", [P, G, 1 + BASES, P])
    both = d.sb("both", [P, G, 2 * P])
    with c.nc.Block() as block:
        @block.sync
        def _(sp):
            sp.dma_start(w[:], W["L2_w"]).then_inc(s("weights_in"), 16)
            sp.dma_start(b2[:], W["L1_b2"].partition_broadcast(P)).then_inc(s("weights_in"), 16)

            def body(i):
                sp.wait_ge(s("both"), i + 1)
                sp.dma_start(rows_of(table, i), both[:, :, 0:P]).then_inc(s("both_out"), 16)
                sp.dma_start(rows_of(node_table, i), both[:, :, P:2 * P]).then_inc(s("both_out"), 16)
            loop(sp, NG, body)
            sp.wait_ge(s("both_out"), 32 * NG)

        @block.vector
        def _(v):
            ch = Chain(v, s("dve"))
            ch.begin(0)
            v.memset(two[:], 2.0)
            v.memset(one[:], 1.0)
            for j in range(BASES):
                last = v.memset(centres[:, j:j + 1], -1.75 + STEP * (KNOT0 + j + 2))
            last.then_inc(s("centres"), 1)
            v.wait_ge(s("centres"), 1)
            v.wait_ge(s("weights_in"), 32)

            def body(i):
                ch.begin(i)
                acc = d.group(d.acc, i)
                v.nop(nofuse=True)
                ch.link(v.tensor_copy(rden[:], acc[:, :, :, C]))
                ch.link(v.reciprocal(rden[:], rden[:]))
                ch.link(v.tensor_tensor(o[:].rearrange("p g (h c) -> p g h c", h=H), acc[:, :, :, 0:C],
                                        bcast(rden[:], [P, G, H, C], 3), ALU.mult))
                ch.link(v.tensor_tensor(o2[:], o[:], bcast(b2[:], [P, G, P], 1), ALU.add))
                ch.link(v.tensor_tensor(x2[:], d.group(T.xs, i), o2[:], ALU.add))
                v.tensor_scalar(d.group(T.xs, i), x2[:], 1.0, None, ALU.mult)
                reuse(v, s("hT_ps"), i)
                reuse(v, s("hs"), i)
                d.norm_vector(v, ch, i, x2[:], h[:], "ln").then_inc(s("h"), 1)
                v.wait_ge(s("ex"), i + 1)
                ch.link(v.tensor_scalar(sig[:], ex[:], 1.0, None, ALU.add))
                ch.link(v.reciprocal(sig[:], sig[:]))
                reuse(v, s("both_ps"), i)
                ch.link(v.tensor_tensor(feat[:, :, 0, :], sig[:], hT[:], ALU.mult))

                def distances(j):
                    v.tensor_tensor(dist[:, j % 2], bcast(hT[:, j, :], [P, BASES, P], 1),
                                    bcast(centres[:], [P, BASES, P], 2), ALU.subtract).then_inc(s("dist"), 1)

                distances(0)
                distances(1)
                for j in range(G):
                    v.wait_ge(s("squares"), i * G + j + 1)
                    v.tensor_tensor(cube2[:, j % 2], square2[:, j % 2], near2[:, j % 2], ALU.mult)
                    ch.link(v.tensor_tensor(cube1[:, j % 2], square1[:, j % 2], near1[:, j % 2], ALU.mult))
                    v.tensor_tensor(feat[:, j, 1:1 + BASES, :], cube2[:, j % 2], cube1[:, j % 2], ALU.subtract
                                    ).then_inc(s("splines"), 1)
                    if j + 2 < G:
                        distances(j + 2)
            loop(v, NG, body)

        @block.tensor
        def _(pe):
            pe.wait_ge(s("weights_in"), 32)

            def body(i):
                pe.wait_ge(s("h"), i + 1)
                reuse(pe, s("hT"), i)
                for j in range(G):
                    last = pe.transpose(d.hT_slot(j), h[:, j, :], T.ident[:])
                last.then_inc(s("hT_ps"), 1)
                reuse(pe, s("both"), i)
                for j in range(G):
                    pe.wait_ge(s("splines"), i * G + j + 1)
                    for f in range(1 + BASES):
                        last = pe.matmul(pt[:, j, 0:2 * P], feat[:, j, f, :], w[:, f, :], start=(f == 0), stop=(f == BASES))
                last.then_inc(s("both_ps"), 1)
            loop(pe, NG, body)

        @block.scalar
        def _(a):
            ch = Chain(a, s("act"))

            def body(i):
                ch.begin(i)
                d.norm_scalar(a, i, "ln")
                a.wait_ge(s("h"), i + 1)
                a.copy(d.group(T.hs, i), h[:]).then_inc(s("hs"), 1)
                a.wait_ge(s("hT_ps"), i + 1)
                reuse(a, s("dist"), i, G)
                a.copy(hT[:, 0:4, :], pt[:, 5, :].rearrange("p (g n) -> p g n", g=4))
                a.copy(hT[:, 4, :], pt[:, 6, 0:P]).then_inc(s("hT"), 1)
                a.wait_ge(s("hT"), i + 1)
                a.activation(ex[:], hT[:], ACT.Exp, scale=-1.0).then_inc(s("ex"), 1)
                for j in range(G):
                    k = j % 2
                    a.wait_ge(s("dist"), i * G + j + 1)
                    if j >= 2:
                        a.wait_ge(s("splines"), i * G + j - 1)
                    else:
                        reuse(a, s("splines"), i, G)
                    ch.link(a.activation(far[:, k], dist[:, k], ACT.Abs, scale=1.0 / STEP))
                    a.activation(near2[:, k], far[:, k], ACT.Relu, bias=two[:], scale=-1.0)
                    ch.link(a.activation(near1[:, k], far[:, k], ACT.Relu, bias=one[:], scale=-1.0))
                    a.activation(square2[:, k], near2[:, k], ACT.Square, scale=6.0 ** -0.5)
                    a.activation(square1[:, k], near1[:, k], ACT.Square, scale=(4.0 / 6.0) ** 0.5).then_inc(s("squares"), 1)
                a.wait_ge(s("both_ps"), i + 1)
                reuse(a, s("both_out"), i, 32)
                a.copy(both[:], pt[:, 0:G, 0:2 * P]).then_inc(s("both"), 1)
            loop(a, NG, body)
    d.ph.close()


def node_after_kan(c, T, W, table, node_table):
    H, C = 4, 32
    d = Dense(c, T, "kan_out", H, C)
    s, pt = d.s, d.pt
    w = d.sb("w", [P, 3 * P])
    bias = d.sb("bias", [P, P])
    slope = d.sb("slope", [P, 1])
    den = d.sb("den", [P, G, H])
    rden = d.sb("rden", [P, G, H])
    o = d.sb("o", [P, G, P])
    o2 = d.sb("o2", [P, G, P])
    o3 = d.sb("o3", [P, G, P])
    x3 = d.sb("x3", [P, G, P])
    h = d.sb("h", [P, G, P])
    hT = d.sb("hT", [P, G, P])
    qvk = d.sb("qvk", [P, G, 3 * P])
    with c.nc.Block() as block:
        @block.sync
        def _(sp):
            sp.dma_start(w[:], W["L3_w"]).then_inc(s("weights_in"), 16)
            sp.dma_start(bias[:], W["L2_bias"].partition_broadcast(P)).then_inc(s("weights_in"), 16)
            sp.dma_start(slope[:], W["L2_prelu_a"].partition_broadcast(P)).then_inc(s("weights_in"), 16)

            def body(i):
                sp.wait_ge(s("qvk"), i + 1)
                sp.dma_start(rows_of(table, i), qvk[:, :, 0:2 * P]).then_inc(s("qvk_out"), 16)
                sp.dma_start(rows_of(node_table, i), qvk[:, :, 2 * P:3 * P]).then_inc(s("qvk_out"), 16)
            loop(sp, NG, body)
            sp.wait_ge(s("qvk_out"), 32 * NG)

        @block.vector
        def _(v):
            ch = Chain(v, s("dve"))
            v.wait_ge(s("weights_in"), 48)

            def body(i):
                ch.begin(i)
                acc = d.group(d.acc, i)
                ch.link(v.tensor_scalar(den[:], acc[:, :, :, C], 1e-16, None, ALU.add))
                ch.link(v.reciprocal(rden[:], den[:]))
                ch.link(v.tensor_tensor(o[:].rearrange("p g (h c) -> p g h c", h=H), acc[:, :, :, 0:C],
                                        bcast(rden[:], [P, G, H, C], 3), ALU.mult))
                ch.link(v.tensor_tensor(o2[:], o[:], d.group(T.hs, i), ALU.add))
                ch.link(v.tensor_tensor(o3[:], o2[:], bcast(bias[:], [P, G, P], 1), ALU.add))
                v.tensor_scalar(o[:], o3[:], 0.0, slope[:], ALU.min, ALU.mult)
                ch.link(v.tensor_scalar(o2[:], o3[:], 0.0, None, ALU.max))
                ch.link(v.tensor_tensor(o3[:], o[:], o2[:], ALU.add))
                ch.link(v.tensor_tensor(x3[:], d.group(T.xs, i), o3[:], ALU.add))
                v.tensor_scalar(d.group(T.xs, i), x3[:], 1.0, None, ALU.mult)
                reuse(v, s("hT_ps"), i)
                d.norm_vector(v, ch, i, x3[:], h[:], "ln").then_inc(s("h"), 1)
            loop(v, NG, body)

        @block.tensor
        def _(pe):
            pe.wait_ge(s("weights_in"), 48)

            def body(i):
                pe.wait_ge(s("h"), i + 1)
                reuse(pe, s("qvk"), i)
                for j in range(G):
                    last = pe.transpose(pt[:, j, 3 * P:4 * P], h[:, j, :], T.ident[:])
                last.then_inc(s("hT_ps"), 1)
                pe.wait_ge(s("hT"), i + 1)
                for j in range(G):
                    last = pe.matmul(pt[:, j, 0:3 * P], hT[:, j, :], w[:], start=True, stop=True)
                last.then_inc(s("qvk_ps"), 1)
            loop(pe, NG, body)

        @block.scalar
        def _(a):
            def body(i):
                d.norm_scalar(a, i, "ln")
                a.wait_ge(s("hT_ps"), i + 1)
                a.copy(hT[:], pt[:, 0:G, 3 * P:4 * P]).then_inc(s("hT"), 1)
                a.wait_ge(s("qvk_ps"), i + 1)
                reuse(a, s("qvk_out"), i, 32)
                a.copy(qvk[:], pt[:, 0:G, 0:3 * P]).then_inc(s("qvk"), 1)
            loop(a, NG, body)
    d.ph.close()


def node_out(c, T, out):
    H, C = 4, 32
    F = H * (C + 1)
    ph = Phase(c, "out")
    s = ph.sem
    den = ph.sb("den", [P, NB, H])
    rden = ph.sb("rden", [P, NB, H])
    o = ph.sb("o", [P, NB, P])
    res = ph.sb("res", [P, NB, P])
    acc = T.acc[:, 0:NB * F].rearrange("p (b h c) -> p b h c", h=H, c=C + 1)
    with c.nc.Block() as block:
        @block.vector
        def _(v):
            ch = Chain(v, s("dve"))
            ch.begin(0)
            ch.link(v.tensor_scalar(den[:], acc[:, :, :, C], 1e-9, None, ALU.max))
            ch.link(v.reciprocal(rden[:], den[:]))
            ch.link(v.tensor_tensor(o[:].rearrange("p b (h c) -> p b h c", h=H), acc[:, :, :, 0:C],
                                    bcast(rden[:], [P, NB, H, C], 3), ALU.mult))
            v.tensor_tensor(res[:], T.xs[:], o[:], ALU.add).then_inc(s("res"), 1)

        @block.sync
        def _(sp):
            sp.wait_ge(s("res"), 1)
            sp.dma_start(out[0:(NB - 1) * P, :].rearrange("(b p) f -> p b f", p=P), res[:, 0:NB - 1, :]
                         ).then_inc(s("stored"), 16)
            sp.dma_start(out[(NB - 1) * P:N, :], res[0:N - (NB - 1) * P, NB - 1, :]).then_inc(s("stored"), 16)
            sp.wait_ge(s("stored"), 32)
    ph.close()


def load_vec(c, T, name, dst, src):
    ph = Phase(c, name)
    s = ph.sem
    with c.nc.Block() as block:
        @block.sync
        def _(sp):
            sp.dma_start(dst[:], src.partition_broadcast(P)).then_inc(s("in"), 16)
            sp.wait_ge(s("in"), 16)
    ph.close()


class Tables:
    pass


def build(nc, A, out):
    c = Ctx(nc)
    T = Tables()
    T.ident = c.sb("ident", [P, P])
    T.ones = c.sb("ones", [1, P])
    T.iota256 = c.sb("iota256", [P, 2 * P])
    T.xs = c.sb("xs", [P, NB, P])
    T.hs = c.sb("hs", [P, NB, P])
    T.ixs = c.sb("ixs", [P, RT, ROW_IX], I32)
    T.mask = c.sb("mask", [P, RT * SLOTS])
    T.rel = c.sb("rel", [P, RT])
    T.blk = c.sb("blk", [1, RT + U], I32)
    T.d_rel = c.dram("d_rel", [RT + U, 2 * P])
    T.pid = c.sb("pid", [P, 1])
    T.pen = c.sb("pen", [CT, NCH * P])
    T.pen_b = c.sb("pen_b", [CT, NCH * P])
    T.pen_pre = c.sb("pen_pre", [CT, NCH * P])
    T.pen_suf = c.sb("pen_suf", [CT, NCH * P])
    T.pen_tile = c.sb("pen_tile", [4, RT])
    T.pen_tile_b = c.sb("pen_tile_b", [4, RT])
    T.m = c.sb("m", [P, RT * 4])
    T.factor = c.sb("factor", [P, RT * 4])
    att = c.sb("att", [P, P])
    T.acc = c.sb("acc", [P, (NB + 1) * 322])

    tab = {w: c.dram(f"tab{w}", [NP_, w]) for w in (128, 136, 256, 264)}
    node = {w: c.dram(f"node{w}", [NP_, w]) for w in (128, 322)}
    def attention(name, H, C, src_w, node_w, kind, **kw):
        message_pass(c, T, name, H, C, src_w, node_w, tab[src_w], node.get(node_w), kind, **kw)

    prepare(c, T, A["x"], A["chunk_ix"], A["dst_rows"], A, tab[128], node[322])
    attention("conv", 2, 160, 128, 322, "conv", chunk_attr=A["chunk_attr"])
    node_after_conv(c, T, A, tab[264])
    attention("gat0", 4, 64, 264, 0, "gat")
    node_between_gats(c, T, A, "mid0", "L1_b0", "L1_W1", "L1_as1", "L1_ad1", 256, tab[264])
    attention("gat1", 4, 64, 264, 0, "gat")
    node_between_gats(c, T, A, "mid1", "L1_b1", "L1_W2", "L1_as2", "L1_ad2", 128, tab[136])
    attention("gat2", 4, 32, 136, 0, "gat")
    node_kan(c, T, A, tab[128], node[128])
    load_vec(c, T, "att_in", att, A["L2_double_attn"])
    attention("gatv2", 4, 32, 128, 128, "gatv2", vec=att)
    node_after_kan(c, T, A, tab[256], node[128])
    attention("dot", 4, 32, 256, 128, "dot")
    node_out(c, T, out)
    c.keep.close()


def arrange(inputs):
    a = {k: np.ascontiguousarray(v) for k, v in inputs.items()}
    src, dst = a["src"], a["dst"]
    src_c = np.zeros((CHUNKS * K,), src.dtype)
    src_c[:E] = src
    dst_c = np.full((CHUNKS * K,), NO_NODE, dst.dtype)
    dst_c[:E] = dst
    dst_r = np.full((EROWS * P,), NO_NODE, dst.dtype)
    dst_r[:E] = dst
    ea = np.zeros((CHUNKS * K, 32), a["edge_attr_32"].dtype)
    ea[:E] = a["edge_attr_32"]
    heads2 = lambda w: w.reshape(2, P, -1).transpose(1, 0, 2)
    out = {"x": a["x"],
           "chunk_ix": np.concatenate([src_c.reshape(CHUNKS, K), dst_c.reshape(CHUNKS, K)], axis=1),
           "dst_rows": dst_r.reshape(EROWS, P),
           "chunk_attr": ea.reshape(CHUNKS, K * 32),
           "L0_WqT": a["L0_gnn_Wq"].T, "L0_bq": a["L0_gnn_bq"].reshape(2, P).T,
           "L0_kx": np.concatenate([heads2(a["L0_gnn_Wk"]), heads2(a["L0_gnn_We"]),
                                    heads2(a["L0_gnn_bk"].reshape(-1, 1))], axis=2),
           "L0_WvT": a["L0_gnn_Wv"].T,
           "L0_web": np.concatenate([a["L0_gnn_We"].T.reshape(32, 2, P), a["L0_gnn_bv"].reshape(1, 2, P)], axis=0),
           "L0_WskipT": a["L0_gnn_Wskip"].T, "L0_bskip": a["L0_gnn_bskip"].reshape(1, P),
           "L0_W1T": a["L0_gnn_W1"].T, "L0_b1": a["L0_gnn_b1"].reshape(2, P).T,
           "L0_W2T": a["L0_gnn_W2"].T.reshape(2, P, P).transpose(1, 0, 2), "L0_b2": a["L0_gnn_b2"].reshape(1, P),
           "L0_ln1_g": a["L0_gnn_ln1_g"], "L0_ln1_b": a["L0_gnn_ln1_b"],
           "L0_ln2_g": a["L0_gnn_ln2_g"], "L0_ln2_b": a["L0_gnn_ln2_b"],
           "L1_W0": a["L1_gnn_W0"], "L1_as0": a["L1_gnn_as0"].reshape(-1), "L1_ad0": a["L1_gnn_ad0"].reshape(-1),
           "L1_b0": a["L1_gnn_b0"],
           "L1_W1": a["L1_gnn_W1"].reshape(2, P, 256).transpose(1, 0, 2),
           "L1_as1": a["L1_gnn_as1"].reshape(-1), "L1_ad1": a["L1_gnn_ad1"].reshape(-1), "L1_b1": a["L1_gnn_b1"],
           "L1_W2": a["L1_gnn_W2"].reshape(2, P, P).transpose(1, 0, 2),
           "L1_as2": a["L1_gnn_as2"].reshape(-1), "L1_ad2": a["L1_gnn_ad2"].reshape(-1), "L1_b2": a["L1_gnn_b2"],
           "L2_double_attn": a["L2_gnn_double_attn"].reshape(-1), "L2_bias": a["L2_gnn_bias"],
           "L2_prelu_a": a["L2_gnn_prelu_a"].reshape(1),
           "L3_w": np.concatenate([a[f"L3_gnn_{n}"].transpose(1, 0, 2).reshape(P, P) for n in ("Wq", "Wv", "Wk")], axis=1)}
    kan = []
    for side in ("src", "dst"):
        sw = a[f"L2_gnn_spline_w_{side}"].transpose(1, 2, 0)[:, KNOT0:KNOT0 + BASES, :]
        kan.append(np.concatenate([a[f"L2_gnn_base_w_{side}"].T[:, None, :], sw], axis=1))
    out["L2_w"] = np.concatenate(kan, axis=2)
    return {k: np.ascontiguousarray(v) for k, v in out.items()}


def kernel(**inputs):
    import concourse.bacc as bacc
    from concourse.bass_utils import run_bass_kernel_spmd as run

    nc = bacc.Bacc("TRN2", target_bir_lowering=False, num_devices=1)
    arrays = {f"in_{k}": v for k, v in arrange(inputs).items()}
    A = {k[3:]: nc.dram_tensor(k, v.shape, mybir.dt.from_np(v.dtype), kind="ExternalInput").ap()
         for k, v in arrays.items()}
    out = nc.dram_tensor("out_x", (N, P), F32, kind="ExternalOutput").ap()
    build(nc, A, out)
    return run(nc, [arrays], core_ids=[0]).results[0]["out_x"]
```
